# Optimizing a Trainium2 kernel written in Bass

```python
import numpy as np
import jax
import jax.numpy as jnp

def _softmax(x, axis=-1):
    return jax.nn.softmax(x, axis=axis)

def _gelu(x):
    return jax.nn.gelu(x, approximate=True)

def _silu(x):
    return jax.nn.silu(x)

def _sigmoid(x):
    return jax.nn.sigmoid(x)

def _layernorm(x, axis=-1, eps=1e-05):
    m = jnp.mean(x, axis=axis, keepdims=True)
    v = jnp.var(x, axis=axis, keepdims=True)
    return (x - m) / jnp.sqrt(v + eps)

def _scatter_add(tgt, idx, src, axis=0):
    return tgt.at[idx].add(src)

def _segment_sum(src, seg, n):
    return jax.ops.segment_sum(src, seg, n)
kernel_name = 'mk_gnn_resnorm_d1_gnn_r8_99df54'

def setup_inputs(seed: int=0):
    np.random.seed(seed)
    _w = jnp.asarray

    def _rec_inputs():
        import jax
        import jax.numpy as jnp
        _gk = jax.random.key(seed)
        x = -0.0003713 + 1 * jax.random.normal(jax.random.fold_in(_gk, 1), (6250, 256), jnp.float32)
        _s = jax.random.randint(jax.random.fold_in(_gk, 2), (50000,), 0, 6250, jnp.int32)
        _d = jax.random.randint(jax.random.fold_in(_gk, 3), (50000,), 0, 6250, jnp.int32)
        _loop = jnp.arange(6250, dtype=jnp.int32)
        src = jnp.concatenate([_s, _d, _loop])
        dst = jnp.concatenate([_d, _s, _loop])
        _o = jnp.argsort(dst, stable=True)
        src = src[_o]
        dst = dst[_o]
        node_type_24 = jax.random.randint(jax.random.fold_in(_gk, 12), (6250,), 0, 24, jnp.int32)
        return (x, src, dst, node_type_24)
    x, src, dst, node_type_24 = _rec_inputs()

    def _L0_gnn_setup():
        import jax, jax.numpy as jnp
        import numpy as np
        N = 6250
        E = 100000
        F_IN = 256
        HID = 64
        H = 4
        NC = 23
        NEG_SLOPE = 0.2

        def _gat_layer(h, W, attn_l, attn_r, bias, src, dst):
            feat = (h @ W.T).reshape(-1, H, HID)
            el = jnp.einsum('nhd,hd->nh', feat, attn_l)
            er = jnp.einsum('nhd,hd->nh', feat, attn_r)
            e = jax.nn.leaky_relu(el[src] + er[dst], NEG_SLOPE)
            m = jax.ops.segment_max(e, dst, num_segments=N)
            m = jnp.where(jnp.isfinite(m), m, 0.0)
            ex = jnp.exp(e - m[dst])
            den = jax.ops.segment_sum(ex, dst, num_segments=N)
            a = ex / jnp.maximum(den[dst], 1e-09)
            out = jax.ops.segment_sum(a[:, :, None] * feat[src], dst, num_segments=N)
            out = out + bias.reshape(1, H, HID)
            return jax.nn.relu(out).reshape(-1, H * HID)
        key = jax.random.key(seed)
        ks = jax.random.split(key, 18)
        s = 0.05
        emb = jax.random.normal(ks[4], (NC + 1, F_IN), jnp.float32) * s
        emb = emb.at[NC].set(0.0)
        return {'features': jax.random.normal(ks[0], (N, F_IN), jnp.float32), 'input_labels': jax.random.randint(ks[1], (N,), 0, NC + 1), 'src': jax.random.randint(ks[2], (E,), 0, N), 'dst': jax.random.randint(ks[3], (E,), 0, N), 'emb': emb, 'le_W1': jax.random.normal(ks[5], (4 * F_IN, 2 * F_IN), jnp.float32) * s, 'le_b1': jnp.zeros((4 * F_IN,), jnp.float32), 'ln_g': jnp.ones((4 * F_IN,), jnp.float32), 'ln_b': jnp.zeros((4 * F_IN,), jnp.float32), 'le_W2': jax.random.normal(ks[6], (F_IN, 4 * F_IN), jnp.float32) * s, 'le_b2': jnp.zeros((F_IN,), jnp.float32), 'W1': jax.random.normal(ks[7], (H * HID, F_IN), jnp.float32) * s, 'al1': jax.random.normal(ks[8], (H, HID), jnp.float32) * s, 'ar1': jax.random.normal(ks[9], (H, HID), jnp.float32) * s, 'b1': jnp.zeros((H * HID,), jnp.float32), 'W2': jax.random.normal(ks[10], (H * HID, H * HID), jnp.float32) * s, 'al2': jax.random.normal(ks[11], (H, HID), jnp.float32) * s, 'ar2': jax.random.normal(ks[12], (H, HID), jnp.float32) * s, 'b2': jnp.zeros((H * HID,), jnp.float32)}
    _L0_gnn_all = _L0_gnn_setup()
    _L0_gnn_in = {k: v for k, v in _L0_gnn_all.items() if k in ('emb', 'le_W1', 'le_b1', 'ln_g', 'ln_b', 'le_W2', 'le_b2', 'W1', 'al1', 'ar1', 'b1', 'W2', 'al2', 'ar2', 'b2')}
    del _L0_gnn_all
    return {'x': x, 'src': src, 'dst': dst, 'node_type_24': node_type_24, 'L0_gnn_emb': _L0_gnn_in['emb'], 'L0_gnn_le_W1': _L0_gnn_in['le_W1'], 'L0_gnn_le_b1': _L0_gnn_in['le_b1'], 'L0_gnn_ln_g': _L0_gnn_in['ln_g'], 'L0_gnn_ln_b': _L0_gnn_in['ln_b'], 'L0_gnn_le_W2': _L0_gnn_in['le_W2'], 'L0_gnn_le_b2': _L0_gnn_in['le_b2'], 'L0_gnn_W1': _L0_gnn_in['W1'], 'L0_gnn_al1': _L0_gnn_in['al1'], 'L0_gnn_ar1': _L0_gnn_in['ar1'], 'L0_gnn_b1': _L0_gnn_in['b1'], 'L0_gnn_W2': _L0_gnn_in['W2'], 'L0_gnn_al2': _L0_gnn_in['al2'], 'L0_gnn_ar2': _L0_gnn_in['ar2'], 'L0_gnn_b2': _L0_gnn_in['b2']}

def reference(x, src, dst, node_type_24, L0_gnn_emb, L0_gnn_le_W1, L0_gnn_le_b1, L0_gnn_ln_g, L0_gnn_ln_b, L0_gnn_le_W2, L0_gnn_le_b2, L0_gnn_W1, L0_gnn_al1, L0_gnn_ar1, L0_gnn_b1, L0_gnn_W2, L0_gnn_al2, L0_gnn_ar2, L0_gnn_b2):
    import jax
    import jax.numpy as jnp

    def _L0_gnn_ref(features, emb, le_W1, le_b1, ln_g, ln_b, le_W2, le_b2, W1, al1, ar1, b1, W2, al2, ar2, b2, input_labels, src, dst):
        import jax, jax.numpy as jnp
        import numpy as np
        N = 6250
        E = 100000
        F_IN = 256
        HID = 64
        H = 4
        NC = 23
        NEG_SLOPE = 0.2

        def _gat_layer(h, W, attn_l, attn_r, bias, src, dst):
            feat = (h @ W.T).reshape(-1, H, HID)
            el = jnp.einsum('nhd,hd->nh', feat, attn_l)
            er = jnp.einsum('nhd,hd->nh', feat, attn_r)
            e = jax.nn.leaky_relu(el[src] + er[dst], NEG_SLOPE)
            m = jax.ops.segment_max(e, dst, num_segments=N)
            m = jnp.where(jnp.isfinite(m), m, 0.0)
            ex = jnp.exp(e - m[dst])
            den = jax.ops.segment_sum(ex, dst, num_segments=N)
            a = ex / jnp.maximum(den[dst], 1e-09)
            out = jax.ops.segment_sum(a[:, :, None] * feat[src], dst, num_segments=N)
            out = out + bias.reshape(1, H, HID)
            return jax.nn.relu(out).reshape(-1, H * HID)
        lab = emb[input_labels]
        x = jnp.concatenate([features, lab], axis=-1)
        x = x @ le_W1.T + le_b1
        mu = jnp.mean(x, axis=-1, keepdims=True)
        var = jnp.var(x, axis=-1, keepdims=True)
        x = (x - mu) * jax.lax.rsqrt(var + 1e-05) * ln_g + ln_b
        x = jax.nn.relu(x)
        h = x @ le_W2.T + le_b2
        h = _gat_layer(h, W1, al1, ar1, b1, src, dst)
        h = _gat_layer(h, W2, al2, ar2, b2, src, dst)
        return h
    x = _layernorm(x + _L0_gnn_ref(x, L0_gnn_emb, L0_gnn_le_W1, L0_gnn_le_b1, L0_gnn_ln_g, L0_gnn_ln_b, L0_gnn_le_W2, L0_gnn_le_b2, L0_gnn_W1, L0_gnn_al1, L0_gnn_ar1, L0_gnn_b1, L0_gnn_W2, L0_gnn_al2, L0_gnn_ar2, L0_gnn_b2, node_type_24, src, dst), axis=-1)
    return x

_drawn_inputs = setup_inputs


def setup_inputs(seed=0):
    import zlib

    import numpy as np

    out = dict(_drawn_inputs(seed))
    spreads = {'L0_gnn_le_b1': (0.0, 0.303),
     'L0_gnn_ln_g': (1.0, 0.2),
     'L0_gnn_ln_b': (0.0, 0.325),
     'L0_gnn_le_b2': (0.0, 0.304),
     'L0_gnn_b1': (0.0, 0.1),
     'L0_gnn_b2': (0.0, 0.1)}
    factors = {'L0_gnn_emb': 8.0,
     'L0_gnn_al1': 5.248,
     'L0_gnn_ar1': 28.495,
     'L0_gnn_al2': 28.919,
     'L0_gnn_ar2': 64.0}
    for name, (base, spread) in spreads.items():
        noise = np.random.default_rng([zlib.crc32(name.encode()), seed]).standard_normal(out[name].shape)
        drawn = base * np.exp(spread * noise) if base else spread * noise
        out[name] = jnp.asarray(drawn.astype(out[name].dtype))
    for name, factor in factors.items():
        out[name] = (out[name] * factor).astype(out[name].dtype)
    return out
```

```python
from contextlib import ExitStack

import concourse.bass as bass
from concourse import mybir

F32 = mybir.dt.float32
I32 = mybir.dt.int32
BF16 = mybir.dt.bfloat16
ALU = mybir.AluOpType
ACT = mybir.ActivationFunctionType
AX = mybir.AxisListType
ET = mybir.EngineType

P = 128
N = 6250
D = 256
H = 4
HD = D // H
HW = HD + 1
ROW = H * HW
RX = ROW + H
E = 106250
HID = 4 * D
LABELS = 24
NT = -(-N // P)
LAST = N - (NT - 1) * P
CB = 21
RING = 3
CHUNKS = (E + NT * (P - 1)) // P
NB = -(-CHUNKS // (CB * RING)) * RING
NC = NB * CB
CG = -(-NC // P)
HC = H * CB
TW = 24
MG = 3
NPS = 3
ROWS_E = 125
COLS_E = E // ROWS_E
BIG = 2.0 ** 100
PAD_DST = 8191
NEG = 0.2
LN_EPS = 1e-5
DEN_MIN = 1e-9


class Counter:

    def __init__(self, sem):
        self.sem, self.n = sem, 0

    def inc(self, ins, by=1):
        ins.then_inc(self.sem, by)
        self.n += by
        return self.n

    def wait(self, eng, n=None):
        eng.wait_ge(self.sem, self.n if n is None else n)


def gnn_kernel(nc, x, xT, src, dst, labels, embT, leW1T, le_b1, ln_g, ln_b, leW2, le_b2,
               gW, gWT, gal, gar, gb, out):
    assert ROWS_E * COLS_E == E
    table = [nc.dram_tensor(f"table{l}", (NT * P, ROW), F32, kind="Internal").ap() for l in range(2)]
    src_s = nc.dram_tensor("src_sorted", (E + P, 1), I32, kind="Internal").ap()
    dst_s = nc.dram_tensor("dst_sorted", (E + P, 1), I32, kind="Internal").ap()
    key_d = nc.dram_tensor("slot_keys", (CG * P, P), F32, kind="Internal").ap()

    with ExitStack() as top:
        def sb(name, shape, dt=F32, ctx=top):
            return ctx.enter_context(nc.sbuf_tensor(name, shape, dt))

        def sem(name, ctx=top):
            return ctx.enter_context(nc.semaphore(name))

        bank = [top.enter_context(nc.psum_tensor(f"bank{i}", [P, 512], F32)) for i in range(8)]

        ident = sb("ident", [P, P])
        ones = sb("ones", [P, P])
        iota_f = sb("iota_f", [P, P])
        pidx = sb("pidx", [P, 1])
        epst = sb("epst", [P, 1])
        pick_c = sb("pick_c", [HC, CB])
        pick_h = sb("pick_h", [HC, H])
        pick_hT = sb("pick_hT", [H, HC])
        src_idx = sb("src_idx", [P, CG * P], I32)
        dst_loc = sb("dst_loc", [P, CG * P])
        flags = sb("flags", [HC, NB, P + 1], BF16)
        flags_x = sb("flags_x", [H, NB, 2 * CB + 2])
        tile_i = sb("tile_i", [1, NB, TW], I32)
        carry_row = sb("carry_row", [P, NB])
        er = sb("er", [P, NT, H])
        wx2 = sb("wx2", [P, 2, RX])
        biasb = [sb(f"bias{l}", [P, D]) for l in range(2)]
        acc = sb("acc", [P, NT, ROW])

        with ExitStack() as ph:
            w1t = sb("w1t", [P, 4, HID], ctx=ph)
            w3 = sb("w3", [LABELS + 1, HID], ctx=ph)
            wc = sb("wc", [P, HID // P, RX], ctx=ph)
            bias_c = sb("bias_c", [P, RX], ctx=ph)
            g_col = sb("g_col", [P, HID // P], ctx=ph)
            b_col = sb("b_col", [P, HID // P], ctx=ph)

            with ExitStack() as pw:
                w2n = sb("w2n", [P, 2, HID], ctx=pw)
                wx1 = sb("wx1", [P, 2, RX], ctx=pw)
                wn = [sb(f"wn{l}", [P, 2, D], ctx=pw) for l in range(2)]
                wt = [sb(f"wt{l}", [P, 2, D], ctx=pw) for l in range(2)]
                alr = [sb(f"alr{l}", [P, 2, 2 * H], ctx=pw) for l in range(2)]
                emb_t = sb("emb_t", [P, 2, LABELS], ctx=pw)
                b2col = sb("b2col", [P, 2], ctx=pw)
                iota_i = sb("iota_i", [P, P], I32, ctx=pw)
                pidx_i = sb("pidx_i", [P, 1], I32, ctx=pw)
                masks_set = sem("masks_set", pw)
                masks_cut = sem("masks_cut", pw)
                iotas_made = sem("iotas_made", pw)
                alr_zero = sem("alr_zero", pw)
                w_loaded = sem("w_loaded", pw)
                a_loaded = sem("a_loaded", pw)
                row_loaded = sem("row_loaded", pw)
                elw_made = sem("elw_made", pw)
                wx_made = sem("wx_made", pw)
                w3_made = sem("w3_made", pw)
                w3_read = sem("w3_read", pw)
                wc_made = sem("wc_made", pw)
                wc_read = sem("wc_read", pw)
                block = pw.enter_context(nc.Block())
                wx = [wx1, wx2]
                N_W = 12

                @block.sync
                def _(sp):
                    sp.dma_start(w1t[:, :, :], leW1T.rearrange("(k p) n -> p k n", p=P)).then_inc(w_loaded, 16)
                    sp.dma_start(w2n[:, :, :], leW2.rearrange("(k p) n -> p k n", p=P)).then_inc(w_loaded, 16)
                    sp.dma_start(emb_t[:, :, :], embT.rearrange("(k p) n -> p k n", p=P)).then_inc(w_loaded, 16)
                    for l in range(2):
                        sp.dma_start(wn[l][:, :, :], gW[l].rearrange("(k p) n -> p k n", p=P)).then_inc(w_loaded, 16)
                        sp.dma_start(wt[l][:, :, :], gWT[l].rearrange("(k p) n -> p k n", p=P)).then_inc(w_loaded, 16)
                        sp.dma_start(biasb[l][:, :], gb[l].rearrange("(a n) -> a n", a=1).broadcast_to([P, D])
                                     ).then_inc(w_loaded, 16)
                    with nc.allow_non_contiguous_dma(reason="vectors of a few hundred features, one to a partition"):
                        sp.dma_start(b2col[:, :], le_b2.rearrange("(k p) -> p k", p=P)).then_inc(w_loaded, 16)
                        sp.dma_start(g_col[:, :], ln_g.rearrange("(k p) -> p k", p=P)).then_inc(w_loaded, 16)
                        sp.dma_start(b_col[:, :], ln_b.rearrange("(k p) -> p k", p=P)).then_inc(w_loaded, 16)
                    sp.wait_ge(w3_read, 2)
                    sp.dma_start(w3[LABELS:LABELS + 1, :], le_b1.rearrange("(a n) -> a n", a=1)).then_inc(row_loaded, 16)
                    sp.wait_ge(row_loaded, 16)

                @block.gpsimd
                def _(pool):
                    nc.gpsimd.memset(ones[:, :], 1.0).then_inc(masks_set, 1)
                    for l in range(2):
                        nc.gpsimd.memset(alr[l][:, :, :], 0.0).then_inc(alr_zero, 1)
                    nc.gpsimd.memset(ident[:, :], 0.0).then_inc(masks_set, 1)
                    nc.gpsimd.iota(iota_i[:, :], [[1, P]], base=0, channel_multiplier=0).then_inc(iotas_made, 1)
                    nc.gpsimd.iota(pidx_i[:, :], [[0, 1]], base=0, channel_multiplier=1).then_inc(iotas_made, 1)
                    pool.wait_ge(masks_set, 2)
                    nc.gpsimd.affine_select(out=ident[:, :], in_=ident[:, :], compare_op=ALU.not_equal, fill=1.0,
                                            base=0, pattern=[[-1, P]], channel_multiplier=1).then_inc(masks_cut, 1)

                @block.scalar
                def _(act):
                    act.wait_ge(alr_zero, 2)
                    for l in range(2):
                        for h in range(H):
                            rows = slice((h % 2) * HD, (h % 2) * HD + HD)
                            act.dma_start(alr[l][rows, h // 2, h:h + 1],
                                          gal[l][h, :].rearrange("(d a) -> d a", a=1)).then_inc(a_loaded, 16)
                            act.dma_start(alr[l][rows, h // 2, H + h:H + h + 1],
                                          gar[l][h, :].rearrange("(d a) -> d a", a=1)).then_inc(a_loaded, 16)

                @block.tensor
                def _(pe):
                    pe.wait_ge(w_loaded, 16 * N_W)
                    pe.wait_ge(a_loaded, 16 * 4 * H)
                    for l in range(2):
                        for m in range(2):
                            for k in range(2):
                                mm = nc.tensor.matmul(bank[0][:, (2 * l + m) * 8:(2 * l + m) * 8 + 8],
                                                      wn[l][:, k, m * P:(m + 1) * P], alr[l][:, k, :],
                                                      start=(k == 0), stop=(k == 1))
                    mm.then_inc(elw_made, 1)
                    for half in range(2):
                        for k in range(2):
                            mm = nc.tensor.matmul(bank[1 + half][0:LABELS, :], emb_t[:, k, :],
                                                  w1t[:, 2 + k, half * 512:(half + 1) * 512],
                                                  start=(k == 0), stop=(k == 1))
                        mm.then_inc(w3_made, 1)
                    pe.wait_ge(wx_made, 3)
                    for kb in range(HID // P):
                        if kb >= 4:
                            pe.wait_ge(wc_read, kb - 3)
                        for m in range(2):
                            mm = nc.tensor.matmul(bank[3 + kb % 4][:, 0:RX], w2n[:, m, kb * P:(kb + 1) * P],
                                                  wx1[:, m, :], start=(m == 0), stop=(m == 1))
                        mm.then_inc(wc_made, 1)
                    for m in range(2):
                        mm = nc.tensor.matmul(bank[7][:, 0:RX], b2col[:, m:m + 1].to_broadcast([P, P]),
                                              wx1[:, m, :], start=(m == 0), stop=(m == 1))
                    mm.then_inc(wc_made, 1)

                @block.vector
                def _(dve):
                    dve.wait_ge(iotas_made, 2)
                    nc.vector.tensor_copy(iota_f[:, :], iota_i[:, :])
                    nc.vector.tensor_copy(pidx[:, :], pidx_i[:, :])
                    nc.vector.memset(epst[:, :], LN_EPS)
                    dve.wait_ge(masks_cut, 1)
                    rows = ident[0:HC, 0:HC]
                    nc.vector.tensor_reduce(pick_c[:, :], rows.rearrange("p (c h) -> p c h", h=H), AX.X, ALU.add)
                    nc.vector.tensor_reduce(pick_h[:, :], rows.rearrange("p (c h) -> p h c", h=H), AX.X, ALU.add)
                    nc.vector.tensor_copy(pick_hT[:, :].rearrange("p (c h) -> p c h", h=H),
                                          ident[0:H, 0:H].unsqueeze(1).to_broadcast([H, CB, H]))
                    dve.wait_ge(w_loaded, 16 * N_W)
                    dve.wait_ge(elw_made, 1)
                    for l in range(2):
                        for m in range(2):
                            heads = wx[l][:, m, 0:ROW].rearrange("p (h w) -> p h w", w=HW)
                            nc.vector.tensor_copy(heads[:, :, 0:HD], wt[l][:, m, :].rearrange("p (h d) -> p h d", d=HD))
                            c = (2 * l + m) * 8
                            nc.vector.tensor_copy(heads[:, :, HD:HW], bank[0][:, c:c + H].rearrange("p (h a) -> p h a", a=1))
                            last = nc.vector.tensor_copy(wx[l][:, m, ROW:RX], bank[0][:, c + H:c + 2 * H])
                            if m == 1:
                                last.then_inc(wx_made, 1)
                    nc.vector.memset(tile_i[:, :, :], 0).then_inc(wx_made, 1)
                    for half in range(2):
                        dve.wait_ge(w3_made, half + 1)
                        nc.vector.tensor_copy(w3[0:LABELS, half * 512:(half + 1) * 512],
                                              bank[1 + half][0:LABELS, :]).then_inc(w3_read, 1)
                    for kb in range(HID // P):
                        dve.wait_ge(wc_made, kb + 1)
                        nc.vector.tensor_copy(wc[:, kb, :], bank[3 + kb % 4][:, 0:RX]).then_inc(wc_read, 1)
                    dve.wait_ge(wc_made, HID // P + 1)
                    nc.vector.tensor_copy(bias_c[:, :], bank[7][:, 0:RX])

            with ExitStack() as pw:
                dst_i = sb("dst_i", [ROWS_E, COLS_E], I32, ctx=pw)
                dst_f = sb("dst_f", [ROWS_E, COLS_E], ctx=pw)
                below = sb("below", [ROWS_E, COLS_E], ctx=pw)
                pad = sb("pad", [1, 2 * P], I32, ctx=pw)
                thr = sb("thr", [P, NT], ctx=pw)
                cnt = sb("cnt", [ROWS_E, NT], ctx=pw)
                first = sb("first", [P, NT + 1], ctx=pw)
                n_e = sb("n_e", [P, NT], ctx=pw)
                n_ci = sb("n_ci", [P, NT], I32, ctx=pw)
                n_c = sb("n_c", [P, NT], ctx=pw)
                chunk0 = sb("chunk0", [P, NT + 1], ctx=pw)
                cid_i = sb("cid_i", [P, CG], I32, ctx=pw)
                cid = sb("cid", [P, CG], ctx=pw)
                hit = sb("hit", [P, 3, NT], ctx=pw)
                tile_c = sb("tile_c", [P, CG], ctx=pw)
                tile_ch = sb("tile_ch", [P, CG], ctx=pw)
                tile_e = sb("tile_e", [P, CG], ctx=pw)
                node0 = sb("node0", [P, CG], ctx=pw)
                base_f = sb("base_f", [P, CG], ctx=pw)
                base_i = sb("base_i", [P, CG], I32, ctx=pw)
                sl_d = sb("sl_d", [P, CG, P], I32, ctx=pw)
                sl_s = sb("sl_s", [P, CG, P], I32, ctx=pw)
                sl_df = sb("sl_df", [P, CG, P], ctx=pw)
                sl_sf = sb("sl_sf", [P, CG, P], ctx=pw)
                sl_k = sb("sl_k", [P, CG, P], ctx=pw)
                keys = sb("keys", [P, 2 * CG * P + 1], ctx=pw)
                tile_b = sb("tile_b", [P, CG * P], ctx=pw)
                key_t = sb("key_t", [HC, NB, P], ctx=pw)
                diff = sb("diff", [H, NB, 2 * CB], ctx=pw)
                ends_k = sb("ends_k", [P, NB], ctx=pw)
                e_loaded = sem("e_loaded", pw)
                e_copied = sem("e_copied", pw)
                pad_set = sem("pad_set", pw)
                thr_set = sem("thr_set", pw)
                counted = sem("counted", pw)
                summed = sem("summed", pw)
                base_set = sem("base_set", pw)
                sl_loaded = [sem("sl_loaded_d", pw), sem("sl_loaded_s", pw)]
                turned = sem("turned", pw)
                slots_read = sem("slots_read", pw)
                keys_read = sem("keys_read", pw)
                keys_out = sem("keys_out", pw)
                keys_in = sem("keys_in", pw)
                k_ready = sem("k_ready", pw)
                step_v = Counter(sem("step_v", pw))
                block = pw.enter_context(nc.Block())

                @block.sync
                def _(sp):
                    sp.dma_start(dst_i[:, :], dst.rearrange("(p n) -> p n", p=ROWS_E)).then_inc(e_loaded, 16)
                    sp.dma_start(src_s[0:E, :].rearrange("(p n) a -> p (n a)", p=ROWS_E),
                                 src.rearrange("(p n) -> p n", p=ROWS_E)).then_inc(e_copied, 16)
                    sp.dma_start(dst_s[0:E, :].rearrange("(p n) a -> p (n a)", p=ROWS_E),
                                 dst.rearrange("(p n) -> p n", p=ROWS_E)).then_inc(e_copied, 16)
                    sp.wait_ge(pad_set, 2)
                    sp.dma_start(src_s[E:E + P, :].rearrange("(p n) a -> p (n a)", p=1), pad[:, 0:P]).then_inc(e_copied, 16)
                    sp.dma_start(dst_s[E:E + P, :].rearrange("(p n) a -> p (n a)", p=1), pad[:, P:2 * P]).then_inc(e_copied, 16)
                    sp.wait_ge(k_ready, CG)
                    sp.dma_start(key_d.rearrange("(g p) e -> p g e", p=P), sl_k[:, :, :]).then_inc(keys_out, 16)
                    sp.wait_ge(keys_out, 16)
                    for h in range(H):
                        sp.dma_start(key_t[h:HC:H, :, :],
                                     key_d[0:NC, :].rearrange("(b c) e -> c b e", c=CB)).then_inc(keys_in, 16)

                @block.gpsimd
                def _(pool):
                    nc.gpsimd.memset(pad[:, 0:P], 0).then_inc(pad_set, 1)
                    nc.gpsimd.memset(pad[:, P:2 * P], PAD_DST).then_inc(pad_set, 1)
                    nc.gpsimd.iota(cid_i[:, :], [[P, CG]], base=0, channel_multiplier=1).then_inc(thr_set, 1)
                    pool.wait_ge(base_set, 1)
                    pool.wait_ge(e_copied, 64)
                    for g in range(CG):
                        pool.indirect_dma_start(sl_d[:, g, :], None, dst_s[:, :],
                                                bass.IndirectOffsetOnAxis(base_i[:, g:g + 1], 0)).then_inc(sl_loaded[0], 16)
                    for g in range(CG):
                        pool.indirect_dma_start(sl_s[:, g, :], None, src_s[:, :],
                                                bass.IndirectOffsetOnAxis(base_i[:, g:g + 1], 0)).then_inc(sl_loaded[1], 16)

                @block.tensor
                def _(pe):
                    pe.wait_ge(counted, NT)
                    nc.tensor.matmul(bank[0][:, 0:NT], ones[0:ROWS_E, :], cnt[:, :],
                                     start=True, stop=True).then_inc(summed, 1)
                    pe.wait_ge(k_ready, CG)
                    for g in range(CG):
                        if g >= 2:
                            pe.wait_ge(slots_read, g - 1)
                            pe.wait_ge(keys_read, g - 1)
                        a, b = bank[1 + g % 2], bank[3 + g % 2]
                        nc.tensor.transpose(a[:, 0:P], sl_sf[:, g, :], ident[:, :])
                        nc.tensor.transpose(a[:, P:2 * P], sl_df[:, g, :], ident[:, :])
                        nc.tensor.matmul(b[:, 0:P], sl_k[:, g, 0:1].to_broadcast([P, P]), ident[:, :], start=True, stop=True)
                        nc.tensor.matmul(b[:, P:2 * P], sl_k[:, g, P - 1:P].to_broadcast([P, P]), ident[:, :], start=True, stop=True)
                        nc.tensor.matmul(b[:, 2 * P:3 * P], tile_c[:, g:g + 1].to_broadcast([P, P]), ident[:, :],
                                         start=True, stop=True).then_inc(turned, 1)

                @block.scalar
                def _(act):
                    for g in range(CG):
                        act.wait_ge(turned, g + 1)
                        nc.scalar.copy(src_idx[:, g * P:(g + 1) * P], bank[1 + g % 2][:, 0:P])
                        nc.scalar.copy(dst_loc[:, g * P:(g + 1) * P], bank[1 + g % 2][:, P:2 * P]).then_inc(slots_read, 1)

                @block.vector
                def _(dve):
                    s = step_v
                    s.inc(nc.vector.tensor_scalar(thr[:, :], iota_f[:, 0:NT], float(P), float(P), ALU.mult, ALU.add))
                    dve.wait_ge(e_loaded, 16)
                    s.inc(nc.vector.tensor_copy(dst_f[:, :], dst_i[:, :]))
                    s.wait(dve)
                    with dve.Fori(0, NT) as t:
                        nc.vector.tensor_scalar(below[:, :], dst_f[:, :], thr[0:ROWS_E, bass.ds(t, 1)], 0.0,
                                                ALU.is_lt, ALU.add, accum_out=cnt[:, bass.ds(t, 1)]).then_inc(counted, 1)
                        dve.wait_ge(counted, t + 1)
                    s.inc(nc.vector.memset(first[:, 0:1], 0.0))
                    s.inc(nc.vector.memset(chunk0[:, 0:1], 0.0))
                    s.inc(nc.vector.memset(keys[:, 0:1], -BIG))
                    s.inc(nc.vector.memset(flags[:, :, :], 0.0))
                    s.inc(nc.vector.memset(flags_x[:, :, :], 0.0))
                    dve.wait_ge(thr_set, 1)
                    s.inc(nc.vector.tensor_copy(cid[:, :], cid_i[:, :]))
                    dve.wait_ge(summed, 1)
                    s.inc(nc.vector.tensor_copy(first[:, 1:NT + 1], bank[0][:, 0:NT]))
                    s.wait(dve)
                    s.inc(nc.vector.tensor_tensor(n_e[:, :], first[:, 1:NT + 1], first[:, 0:NT], ALU.subtract))
                    s.wait(dve)
                    s.inc(nc.vector.tensor_scalar(n_ci[:, :], n_e[:, :], float(P - 1), None, ALU.add))
                    s.wait(dve)
                    s.inc(nc.vector.tensor_scalar(n_ci[:, :], n_ci[:, :], 7, None, ALU.arith_shift_right))
                    s.wait(dve)
                    s.inc(nc.vector.tensor_copy(n_c[:, :], n_ci[:, :]))
                    s.wait(dve)
                    s.inc(nc.vector.tensor_tensor_scan(chunk0[:, 1:NT + 1], ones[:, 0:NT], n_c[:, :], 0.0, ALU.mult, ALU.add))
                    s.wait(dve)
                    starts = chunk0[:, 1:NT]
                    for g in range(CG):
                        c = cid[:, g:g + 1]
                        s.inc(nc.vector.tensor_scalar(hit[:, 0, 0:NT - 1], starts, c, 0.0, ALU.is_le, ALU.add,
                                                      accum_out=tile_c[:, g:g + 1]))
                        s.inc(nc.vector.scalar_tensor_tensor(hit[:, 1, 0:NT - 1], starts, c, n_c[:, 0:NT - 1], ALU.is_le,
                                                             ALU.mult, accum_out=tile_ch[:, g:g + 1]))
                        s.inc(nc.vector.scalar_tensor_tensor(hit[:, 2, 0:NT - 1], starts, c, n_e[:, 0:NT - 1], ALU.is_le,
                                                             ALU.mult, accum_out=tile_e[:, g:g + 1]))
                        s.wait(dve)
                    s.inc(nc.vector.tensor_scalar(node0[:, :], tile_c[:, :], float(P), None, ALU.mult))
                    s.inc(nc.vector.tensor_tensor(base_f[:, :], cid[:, :], tile_ch[:, :], ALU.subtract))
                    s.wait(dve)
                    s.inc(nc.vector.scalar_tensor_tensor(base_f[:, :], base_f[:, :], float(P), tile_e[:, :], ALU.mult, ALU.add))
                    s.wait(dve)
                    nc.vector.tensor_scalar(base_i[:, :], base_f[:, :], float(E), None, ALU.min).then_inc(base_set, 1)
                    dve.wait_ge(sl_loaded[0], 16 * CG)
                    dve.wait_ge(sl_loaded[1], 16 * CG)
                    for g in range(CG):
                        nc.vector.tensor_copy(sl_sf[:, g, :], sl_s[:, g, :])
                        nc.vector.tensor_scalar(sl_df[:, g, :], sl_d[:, g, :], node0[:, g:g + 1], None, ALU.subtract)
                        nc.vector.tensor_scalar(sl_k[:, g, :], sl_d[:, g, :], BIG, None, ALU.mult).then_inc(k_ready, 1)
                    for g in range(CG):
                        dve.wait_ge(turned, g + 1)
                        b = bank[3 + g % 2]
                        ends = keys[:, 1 + 2 * g * P:1 + 2 * (g + 1) * P].rearrange("p (c two) -> p two c", two=2)
                        s.inc(nc.vector.tensor_copy(ends, b[:, 0:2 * P].rearrange("p (two c) -> p two c", two=2)))
                        nc.vector.tensor_copy(tile_b[:, g * P:(g + 1) * P], b[:, 2 * P:3 * P]).then_inc(keys_read, 1)
                    s.wait(dve)
                    dve.wait_ge(keys_read, CG)
                    s.inc(nc.vector.tensor_copy(tile_i[:, :, 0:CB], tile_b[0:1, 0:NC].rearrange("p (b c) -> p b c", c=CB)))
                    k0 = keys[0:H, 0:2 * NC].rearrange("p (b c) -> p b c", c=2 * CB)
                    k1 = keys[0:H, 1:2 * NC + 1].rearrange("p (b c) -> p b c", c=2 * CB)
                    s.inc(nc.vector.tensor_tensor(diff[:, :, :], k0, k1, ALU.subtract))
                    k_end = keys[:, 0:2 * NC].rearrange("p (b c) -> p b c", c=2 * CB)[:, :, 0]
                    t_first = tile_b[:, 0:NC].rearrange("p (b c) -> p b c", c=CB)[:, :, 0]
                    s.inc(nc.vector.tensor_scalar(ends_k[:, :], k_end, 1.0 / BIG, None, ALU.mult))
                    s.wait(dve)
                    s.inc(nc.vector.scalar_tensor_tensor(flags_x[:, :, 1:2 * CB + 1], diff[:, :, :], -1.0, diff[:, :, :],
                                                         ALU.mult, ALU.min))
                    s.inc(nc.vector.scalar_tensor_tensor(ends_k[:, :], t_first, -float(P), ends_k[:, :], ALU.mult, ALU.add))
                    s.wait(dve)
                    s.inc(nc.vector.tensor_scalar(carry_row[:, :], ends_k[:, :], pidx[:, 0:1], None, ALU.is_equal))
                    dve.wait_ge(keys_in, 16 * H)
                    s.inc(nc.vector.tensor_tensor(flags[:, :, 1:P], key_t[:, :, 0:P - 1], key_t[:, :, 1:P], ALU.subtract))
                    s.wait(dve)

            with ExitStack() as pw:
                xt = sb("xt", [P, 2, 2, P], ctx=pw)
                lab = sb("lab", [LABELS + 1, 2, P], I32, ctx=pw)
                onehot = sb("onehot", [LABELS + 1, 2, P], ctx=pw)
                stats = sb("stats", [P, 2, 12], ctx=pw)
                mv = sb("mv", [P, 2, 2], ctx=pw)
                sd = sb("sd", [P, 2, 1], ctx=pw)
                rs = sb("rs", [P, 2, 2], ctx=pw)
                nrm = sb("nrm", [P, 2, HID], ctx=pw)
                xn = sb("xn", [P, 2, HID // P, P], ctx=pw)
                feat = sb("feat", [P, 2, RX], ctx=pw)
                lab_set = sem("lab_set", pw)
                x_loaded = [sem(f"x_loaded{p}", pw) for p in range(2)]
                oh_made = sem("oh_made", pw)
                h1_made = sem("h1_made", pw)
                stat_st = sem("stat_st", pw)
                stats_seen = sem("stats_seen", pw)
                mv_made = sem("mv_made", pw)
                sd_made = sem("sd_made", pw)
                rs_step = sem("rs_step", pw)
                rs_made = sem("rs_made", pw)
                nrm_made = sem("nrm_made", pw)
                tp_made = sem("tp_made", pw)
                xn_made = sem("xn_made", pw)
                feat_mm = sem("feat_mm", pw)
                feat_made = sem("feat_made", pw)
                feat_out = [sem(f"feat_out{p}", pw) for p in range(2)]
                block = pw.enter_context(nc.Block())
                h1 = [[bank[0], bank[1]], [bank[2], bank[3]]]
                tp = [bank[4], bank[5]]
                fp = [bank[6], bank[7]]
                x_t = xT.rearrange("(k p) n -> p k n", p=P)
                KB = HID // P

                @block.sync
                def _(sp):
                    def load(i, p, n, n_before):
                        if n_before is not None:
                            sp.wait_ge(h1_made, n_before)
                            sp.wait_ge(oh_made, n_before)
                        sp.dma_start(xt[:, p, :, 0:n], x_t[:, :, bass.ds(i * P, n)]).then_inc(x_loaded[p], 16)
                        sp.dma_start(lab[0:LABELS, p, 0:n],
                                     labels.rearrange("(a n) -> a n", a=1)[:, bass.ds(i * P, n)].broadcast_to([LABELS, n])
                                     ).then_inc(x_loaded[p], 16)

                    def store(i, p, done):
                        sp.wait_ge(feat_made, done)
                        sp.dma_start(table[0][bass.ds(i * P, P), :], feat[:, p, 0:ROW]).then_inc(feat_out[p], 16)

                    sp.wait_ge(lab_set, 1)
                    load(0, 0, P, None)
                    load(1, 1, P, None)
                    with sp.Fori(0, (NT - 3) // 2) as j:
                        load(2 * j + 2, 0, P, 2 * j + 1)
                        load(2 * j + 3, 1, P, 2 * j + 2)
                        store(2 * j, 0, 2 * j + 1)
                        store(2 * j + 1, 1, 2 * j + 2)
                    load(NT - 1, 0, LAST, NT - 2)
                    for i in range(NT - 3, NT):
                        store(i, i % 2, i + 1)
                    sp.wait_ge(feat_out[0], 16 * ((NT + 1) // 2))
                    sp.wait_ge(feat_out[1], 16 * (NT // 2))

                @block.tensor
                def _(pe):
                    def first(i, p, rounds, free):
                        pe.wait_ge(x_loaded[p], rounds)
                        pe.wait_ge(oh_made, i + 1)
                        if free is not None:
                            pe.wait_ge(nrm_made, free)
                        for half in range(2):
                            cols = slice(half * 512, (half + 1) * 512)
                            for k in range(2):
                                nc.tensor.matmul(h1[p][half][:, :], xt[:, p, k, :], w1t[:, k, cols], start=(k == 0), stop=False)
                            mm = nc.tensor.matmul(h1[p][half][:, :], onehot[:, p, :], w3[:, cols], start=False, stop=True)
                        mm.then_inc(h1_made, 1)

                    def turn(i, p):
                        pe.wait_ge(nrm_made, i + 1)
                        for b in range(2):
                            pe.wait_ge(xn_made, 2 * i + 0)
                            for k in range(4):
                                tr = nc.tensor.transpose(tp[b][:, k * P:(k + 1) * P],
                                                         nrm[:, p, (4 * b + k) * P:(4 * b + k + 1) * P], ident[:, :])
                            tr.then_inc(tp_made, 1)

                    def second(i, p, free):
                        pe.wait_ge(xn_made, 2 * i + 2)
                        if free is not None:
                            pe.wait_ge(feat_made, free)
                        for k in range(KB):
                            mm = nc.tensor.matmul(fp[p][:, 0:RX], xn[:, p, k, :], wc[:, k, :], start=(k == 0), stop=(k == KB - 1))
                        mm.then_inc(feat_mm, 1)

                    first(0, 0, 32, None)
                    turn(0, 0)
                    first(1, 1, 32, None)
                    second(0, 0, None)
                    turn(1, 1)
                    first(2, 0, 64, 1)
                    second(1, 1, None)
                    with pe.Fori(1, (NT - 1) // 2) as j:
                        turn(2 * j, 0)
                        first(2 * j + 1, 1, 32 * j + 32, 2 * j)
                        second(2 * j, 0, 2 * j - 1)
                        turn(2 * j + 1, 1)
                        first(2 * j + 2, 0, 32 * j + 64, 2 * j + 1)
                        second(2 * j + 1, 1, 2 * j)
                    turn(NT - 1, 0)
                    second(NT - 1, 0, NT - 2)

                @block.scalar
                def _(act):
                    def tile(i, p, started):
                        act.wait_ge(mv_made, i + 1)
                        nc.scalar.activation(sd[:, p, :], mv[:, p, 1:2], ACT.Sqrt, bias=epst[:, 0:1]).then_inc(sd_made, 1)
                        act.wait_ge(rs_made, i + 1)
                        if started:
                            act.wait_ge(tp_made, 2 * i - 2)
                        for half in range(2):
                            a = nc.scalar.activation(nrm[:, p, half * 512:(half + 1) * 512], h1[p][half][:, :], ACT.Identity,
                                                     bias=rs[:, p, 1:2], scale=rs[:, p, 0:1])
                        a.then_inc(nrm_made, 1)
                        if started:
                            act.wait_ge(feat_mm, i - 1)
                        for b in range(2):
                            act.wait_ge(tp_made, 2 * i + b + 1)
                            for k in range(4):
                                kk = 4 * b + k
                                a = nc.scalar.activation(xn[:, p, kk, :], tp[b][:, k * P:(k + 1) * P], ACT.Relu,
                                                         bias=b_col[:, kk:kk + 1], scale=g_col[:, kk:kk + 1])
                            a.then_inc(xn_made, 1)

                    tile(0, 0, False)
                    tile(1, 1, False)
                    with act.Fori(1, (NT - 1) // 2) as j:
                        tile(2 * j, 0, True)
                        tile(2 * j + 1, 1, True)
                    tile(NT - 1, 0, True)

                @block.vector
                def _(dve):
                    def one_hot(i, p, rounds):
                        dve.wait_ge(x_loaded[p], rounds)
                        nc.vector.tensor_scalar(onehot[:, p, :], lab[:, p, :], pidx[0:LABELS + 1, 0:1], None,
                                                ALU.is_equal).then_inc(oh_made, 1)

                    def stat(i, p):
                        dve.wait_ge(h1_made, i + 1)
                        for half in range(2):
                            nc.vector.bn_stats(stats[:, p, half * 6:half * 6 + 6], h1[p][half][:, :]).then_inc(stat_st, 1)
                        dve.wait_ge(stat_st, 2 * i + 2)
                        dve.sem_inc(stats_seen, 1)
                        nc.vector.bn_aggr(mv[:, p, :], stats[:, p, :]).then_inc(mv_made, 1)
                        dve.wait_ge(sd_made, i + 1)
                        nc.vector.reciprocal(rs[:, p, 0:1], sd[:, p, :]).then_inc(rs_step, 1)
                        dve.wait_ge(rs_step, i + 1)
                        nc.vector.scalar_tensor_tensor(rs[:, p, 1:2], mv[:, p, 0:1], -1.0, rs[:, p, 0:1], ALU.mult,
                                                       ALU.mult).then_inc(rs_made, 1)

                    def features(i, p, rounds):
                        dve.wait_ge(feat_mm, i + 1)
                        if rounds is not None:
                            dve.wait_ge(feat_out[p], rounds)
                        nc.vector.tensor_tensor(er[:, bass.ds(i, 1), :].rearrange("p a h -> p (a h)"), fp[p][:, ROW:RX],
                                                bias_c[:, ROW:RX], ALU.add)
                        nc.vector.tensor_tensor(feat[:, p, :], fp[p][:, 0:RX], bias_c[:, :], ALU.add).then_inc(feat_made, 1)

                    nc.vector.memset(lab[:, :, :], LABELS).then_inc(lab_set, 1)
                    one_hot(0, 0, 32)
                    one_hot(1, 1, 32)
                    stat(0, 0)
                    one_hot(2, 0, 64)
                    stat(1, 1)
                    features(0, 0, None)
                    one_hot(3, 1, 64)
                    stat(2, 0)
                    features(1, 1, None)
                    one_hot(4, 0, 96)
                    with dve.Fori(1, (NT - 3) // 2) as j:
                        stat(2 * j + 1, 1)
                        features(2 * j, 0, 16 * j)
                        one_hot(2 * j + 3, 1, 32 * j + 64)
                        stat(2 * j + 2, 0)
                        features(2 * j + 1, 1, 16 * j)
                        one_hot(2 * j + 4, 0, 32 * j + 96)
                    j = (NT - 3) // 2
                    stat(NT - 2, 1)
                    features(NT - 3, 0, 16 * j)
                    stat(NT - 1, 0)
                    features(NT - 2, 1, 16 * j)
                    features(NT - 1, 0, 16 * j + 16)

        for layer in range(2):
            attention(nc, layer, table[layer], bank, ident, ones, iota_f, pick_c, pick_h, pick_hT, src_idx, dst_loc,
                      flags, flags_x, tile_i, carry_row, er, acc)
            if layer == 0:
                next_features(nc, bank, ident, biasb[0], acc, er, wx2, table[1])
        finish(nc, x, biasb[1], acc, epst, out)


def attention(nc, layer, table, bank, ident, ones, iota_f, pick_c, pick_h, pick_hT, src_idx, dst_loc, flags, flags_x,
              tile_i, carry_row, er, acc):
    with ExitStack() as ctx:
        def sb(name, shape, dt=F32):
            return ctx.enter_context(nc.sbuf_tensor(f"{name}_{layer}", shape, dt))

        def sem(name):
            return ctx.enter_context(nc.semaphore(f"{name}_{layer}"))

        G = sb("gathered", [P, RING, CB, ROW])
        O = sb("onehots", [P, RING, CB, P])
        idx = sb("idx", [P, RING, CB], I32)
        fl = sb("flags_b", [HC, RING, P + 1], BF16)
        fx = sb("flags_xb", [H, RING, 2 * CB + 2])
        OT = sb("onehots_T", [P, 2, 4, P])
        fw = sb("fw", [HC, P])
        seg = sb("seg", [HC, P])
        fw2 = sb("fw2", [HC, P])
        seg2 = sb("seg2", [HC, P])
        spread = sb("spread", [HC, CB, 2])
        ends = sb("ends", [H, 2 * CB + 1])
        ends_f = sb("ends_f", [H, 2 * CB + 1])
        ends_m = sb("ends_m", [H, 2 * CB + 1])
        moved = sb("moved", [H, 2, H])
        back = sb("back", [HC, 2, CB])
        ends_c = sb("ends_c", [HC, 2])
        ref = sb("ref", [P, 2, H])
        ref_l = sb("ref_l", [P, 2, H])
        ref_d = sb("ref_d", [P, H])
        alpha = sb("alpha", [P, H])
        er_e = sb("er_e", [P, HC])
        z = sb("z", [P, 2, HC])
        zl = sb("zl", [P, 2, HC])
        zd = sb("zd", [P, HC])

        el_T = bank[0]
        small = bank[1]
        ends_ps = small[0:H, 0:2 * CB]
        back_ps = small[0:HC, 64:64 + 2 * CB]
        moved_ps = small[:, 128:128 + 2 * H]
        m_ps = small[:, 256:256 + HC]
        er_ps = bank[2][:, 0:HC]
        ot_ps = [bank[3], bank[4]]
        part = [bank[5], bank[6], bank[7]]

        gathered = [sem(f"gathered{u}") for u in range(RING)]
        idx_set = sem("idx_set")
        granted = sem("granted")
        flags_set = sem("flags_set")
        acc_zero = sem("acc_zero")
        el_turned = sem("el_turned")
        scan_step = sem("scan_step")
        spread_made = sem("spread_made")
        ends_made = sem("ends_made")
        ends_step = sem("ends_step")
        moved_made = sem("moved_made")
        back_made = sem("back_made")
        back_step = sem("back_step")
        seg_made = sem("seg_made")
        m_turned = sem("m_turned")
        ref_step = sem("ref_step")
        ref_made = sem("ref_made")
        alpha_made = sem("alpha_made")
        o_made = sem("o_made")
        o_turned = sem("o_turned")
        ot_made = sem("ot_made")
        er_mm = sem("er_mm")
        er_made = sem("er_made")
        z_step = sem("z_step")
        zd_made = sem("zd_made")
        ex_made = sem("ex_made")
        weighted = sem("weighted")
        part_made = sem("part_made")
        summed = sem("summed")
        scaled = sem("scaled")
        block = ctx.enter_context(nc.Block())
        CREDIT = RING * CB
        TG = 4
        NTG = -(-CB // TG)
        LOOPS = NB // RING - 1

        def el(u):
            return G[:, u, :, :].rearrange("p c (h w) -> p (c h) w", w=HW)[:, :, HD]

        def tiles(engine, b):
            return nc.values_load_multi_w_load_instructions(
                tile_i[0:1, bass.ds(b, 1), :].rearrange("p a c -> p (a c)"), engines=(engine,), min_val=0, max_val=NT - 1,
                skip_runtime_bounds_check_because="a count of at most NT - 1 tiles that start before the chunk")[1]

        def steps(eng, step, before, after):
            before()
            with eng.Fori(0, LOOPS) as i:
                for u in range(RING):
                    step(i * RING + u, u, i, True)
            for u in range(RING):
                step(LOOPS * RING + u, u, LOOPS, u < RING - 1)
            after()

        @block.gpsimd
        def _(pool):
            pool.sem_inc(summed, CREDIT)

            def gather(b, u):
                pool.wait_ge(idx_set, b + 1)
                for c in range(CB):
                    if c % MG == 0:
                        pool.wait_ge(summed, CB * b + c + MG)
                        pool.sem_inc(granted, 1)
                    pool.indirect_dma_start(G[:, u, c, :], None, table[:, :],
                                            bass.IndirectOffsetOnAxis(idx[:, u, c:c + 1], 0)).then_inc(gathered[u], 16)

            with pool.Fori(0, NB // RING) as i:
                for u in range(RING):
                    gather(i * RING + u, u)

        @block.tensor
        def _(pe):
            def segments(b, u, i):
                pe.wait_ge(gathered[u], 16 * CB * (i + 1))
                nc.tensor.transpose(el_T[0:HC, 0:P], el(u), ident[:, :]).then_inc(el_turned, 1)

            def ends_across(b):
                pe.wait_ge(spread_made, b + 1)
                nc.tensor.matmul(ends_ps, pick_h[:, :], spread[:, :, :].rearrange("p c two -> p (c two)"),
                                 start=True, stop=True).then_inc(ends_made, 1)

            def ends_back(b):
                pe.wait_ge(moved_made, b + 1)
                nc.tensor.matmul(back_ps, pick_hT[:, :], ends_m[:, 1:2 * CB + 1], start=True, stop=True)
                nc.tensor.matmul(moved_ps, ones[0:H, :], moved[:, :, :].rearrange("p a h -> p (a h)"),
                                 start=True, stop=True).then_inc(back_made, 1)

            def maxima(b):
                pe.wait_ge(seg_made, b + 1)
                nc.tensor.transpose(m_ps, seg2[:, :], ident[0:HC, 0:HC]).then_inc(m_turned, 1)

            def turn(b, u, g):
                pe.wait_ge(ot_made, NTG * b + max(g - 1, 0))
                for c in range(g * TG, min(g * TG + TG, CB)):
                    tr = nc.tensor.transpose(ot_ps[g % 2][:, (c % TG) * P:(c % TG + 1) * P], O[:, u, c, :], ident[:, :])
                tr.then_inc(o_turned, 1)

            def er_of_slots(b, t, g):
                pe.wait_ge(ot_made, NTG * b + g + 1)
                for c in range(g * TG, min(g * TG + TG, CB)):
                    mm = nc.tensor.matmul(er_ps[:, c * H:(c + 1) * H], OT[:, g % 2, c % TG, :],
                                          er[:, bass.ds(t[c], 1), :].rearrange("p a h -> p (a h)"), start=True, stop=True)
                mm.then_inc(er_mm, 1)

            def sums(b, u, c0, c1):
                for c in range(c0, c1):
                    pe.wait_ge(weighted, CB * b + c + 1)
                    pe.wait_ge(summed, CREDIT + CB * b + c - NPS + 1)
                    nc.tensor.matmul(part[c % NPS][:, 0:ROW], O[:, u, c, :], G[:, u, c, :],
                                     start=True, stop=True).then_inc(part_made, 1)

            def step(b, u, i, has_next):
                un, i_n = (u + 1) % RING, i + (u + 1) // RING
                if not has_next:
                    sums(b, u, 0, CB)
                    return
                t = tiles(ET.PE, b + 1)
                sums(b, u, 0, 4)
                for g in range(NTG + 1):
                    if g < NTG:
                        pe.wait_ge(o_made, 3 * (b + 1) + min(TG * g + TG - 1, CB - 1) // (CB // 3) + 1)
                        turn(b + 1, un, g)
                    if g:
                        er_of_slots(b + 1, t, g - 1)
                    sums(b, u, 4 + g, 5 + g)
                sums(b, u, 11, 12)
                segments(b + 1, un, i_n)
                sums(b, u, 12, 14)
                ends_across(b + 1)
                sums(b, u, 14, 17)
                ends_back(b + 1)
                sums(b, u, 17, 19)
                maxima(b + 1)
                sums(b, u, 19, CB)

            def before():
                t = tiles(ET.PE, 0)
                pe.wait_ge(o_made, 3)
                for g in range(NTG + 1):
                    if g < NTG:
                        turn(0, 0, g)
                    if g >= 1:
                        er_of_slots(0, t, g - 1)
                segments(0, 0, 0)
                ends_across(0)
                ends_back(0)
                maxima(0)

            pe.wait_ge(summed, CREDIT)
            steps(pe, step, before, lambda: None)

        @block.scalar
        def _(act):
            def indices(b, u, i):
                act.wait_ge(gathered[u], 16 * CB * i)
                nc.scalar.copy(fl[:, u, :], flags[:, bass.ds(b, 1), :].rearrange("p a e -> p (a e)"))
                nc.scalar.copy(fx[:, u, :], flags_x[:, bass.ds(b, 1), :].rearrange("p a c -> p (a c)")).then_inc(flags_set, 1)
                nc.scalar.copy(idx[:, u, :], src_idx[:, bass.ds(b * CB, CB)]).then_inc(idx_set, 1)

            def turned(b):
                for g in range(NTG):
                    act.wait_ge(o_turned, NTG * b + g + 1)
                    act.wait_ge(er_mm, NTG * b + max(g - 1, 0))
                    n = min(TG, CB - g * TG)
                    nc.scalar.copy(OT[:, g % 2, 0:n, :], ot_ps[g % 2][:, 0:n * P].rearrange("p (c e) -> p c e", e=P)).then_inc(ot_made, 1)
                act.wait_ge(er_mm, NTG * (b + 1))
                nc.scalar.copy(er_e[:, :], er_ps).then_inc(er_made, 1)

            def exps(b, u):
                act.wait_ge(ref_made, b + 1)
                nc.scalar.activation(alpha[:, :], ref_d[:, :], ACT.Exp, scale=carry_row[:, bass.ds(b, 1)]).then_inc(alpha_made, 1)
                act.wait_ge(zd_made, b + 1)
                nc.scalar.activation(el(u), zd[:, :], ACT.Exp).then_inc(ex_made, 1)

            def step(b, u, i, has_next):
                un, i_n = (u + 1) % RING, i + (u + 1) // RING
                if has_next:
                    turned(b + 1)
                    exps(b + 1, un)

            for u in range(RING):
                indices(u, u, 0)
            turned(0)
            exps(0, 0)
            with act.Fori(0, LOOPS) as i:
                for u in range(RING):
                    step(i * RING + u, u, i, True)
                    indices(i * RING + u + RING, u, i + 1)
            for u in range(RING):
                step(LOOPS * RING + u, u, LOOPS, u < RING - 1)

        @block.vector
        def _(dve):
            def one_hots(b, u, g):
                n = CB // 3
                nc.vector.tensor_tensor(O[:, u, g * n:(g + 1) * n, :], iota_f[:, :].unsqueeze(1).to_broadcast([P, n, P]),
                                        dst_loc[:, bass.ds(b * CB + g * n, n)].unsqueeze(2).to_broadcast([P, n, P]),
                                        ALU.is_equal).then_inc(o_made, 1)

            def chunk_forward(b, u):
                dve.wait_ge(flags_set, b + 1)
                dve.wait_ge(el_turned, b + 1)
                nc.vector.tensor_tensor_scan(fw[:, :], fl[:, u, 0:P], el_T[0:HC, 0:P], -BIG, ALU.add, ALU.max).then_inc(scan_step, 1)

            def chunk_backward(b, u):
                dve.wait_ge(scan_step, 2 * b + 1)
                nc.vector.tensor_tensor_scan(seg[:, :][:, ::-1], fl[:, u, 1:P + 1][:, ::-1], fw[:, :][:, ::-1], -BIG,
                                             ALU.add, ALU.max).then_inc(scan_step, 1)

            def spread_ends(b):
                dve.wait_ge(scan_step, 2 * b + 2)
                nc.vector.tensor_tensor(spread[:, :, :], pick_c[:, :].unsqueeze(2).to_broadcast([HC, CB, 2]),
                                        seg[:, 0:P:P - 1].unsqueeze(1).to_broadcast([HC, CB, 2]), ALU.mult).then_inc(spread_made, 1)

            def ends_in(b):
                nc.vector.tensor_copy(ends[:, 0:1], ends_m[:, 2 * CB:2 * CB + 1])
                dve.wait_ge(ends_made, b + 1)
                nc.vector.tensor_copy(ends[:, 1:2 * CB + 1], ends_ps).then_inc(ends_step, 1)

            def ends_forward(b, u):
                dve.wait_ge(ends_step, 3 * b + 1)
                nc.vector.tensor_tensor_scan(ends_f[:, :], fx[:, u, 0:2 * CB + 1], ends[:, :], -BIG, ALU.add, ALU.max).then_inc(ends_step, 1)

            def ends_backward(b, u):
                dve.wait_ge(ends_step, 3 * b + 2)
                nc.vector.tensor_tensor_scan(ends_m[:, :][:, ::-1], fx[:, u, 1:2 * CB + 2][:, ::-1], ends_f[:, :][:, ::-1], -BIG,
                                             ALU.add, ALU.max).then_inc(ends_step, 1)

            def moved_maxima(b):
                dve.wait_ge(ends_step, 3 * b + 3)
                nc.vector.tensor_scalar(moved[:, 0, :], ident[0:H, 0:H], ends[:, 0:1], None, ALU.mult)
                nc.vector.tensor_scalar(moved[:, 1, :], ident[0:H, 0:H], ends_m[:, 0:1], None, ALU.mult).then_inc(moved_made, 1)

            def own_ends(b, t0):
                dve.wait_ge(back_made, b + 1)
                nc.vector.tensor_tensor(back[:, :, :], back_ps.rearrange("p (c two) -> p two c", two=2),
                                        pick_c[:, :].unsqueeze(1).to_broadcast([HC, 2, CB]), ALU.mult).then_inc(back_step, 1)
                nc.vector.tensor_tensor(ref[:, :, :], moved_ps.rearrange("p (a h) -> p a h", a=2),
                                        er[:, bass.ds(t0, 1), :].to_broadcast([P, 2, H]), ALU.add).then_inc(ref_step, 1)

            def own_ends_sum(b):
                dve.wait_ge(back_step, 3 * b + 1)
                nc.vector.tensor_reduce(ends_c[:, :], back[:, :, :], AX.X, ALU.add).then_inc(back_step, 1)
                dve.wait_ge(ref_step, 2 * b + 1)
                nc.vector.scalar_tensor_tensor(ref_l[:, :, :], ref[:, :, :], NEG, ref[:, :, :], ALU.mult, ALU.max).then_inc(ref_step, 1)

            def join_forward(b, u):
                dve.wait_ge(back_step, 3 * b + 2)
                nc.vector.tensor_tensor_scan(fw2[:, :], fl[:, u, 0:P], seg[:, :], ends_c[:, 0:1], ALU.add, ALU.max).then_inc(back_step, 1)
                dve.wait_ge(ref_step, 2 * b + 2)
                nc.vector.tensor_tensor(ref_d[:, :], ref_l[:, 0, :], ref_l[:, 1, :], ALU.subtract).then_inc(ref_made, 1)

            def join_backward(b, u):
                dve.wait_ge(back_step, 3 * b + 3)
                nc.vector.tensor_tensor_scan(seg2[:, :][:, ::-1], fl[:, u, 1:P + 1][:, ::-1], fw2[:, :][:, ::-1], ends_c[:, 1:2],
                                             ALU.add, ALU.max).then_inc(seg_made, 1)

            def scores(b, u):
                dve.wait_ge(er_made, b + 1)
                nc.vector.tensor_tensor(z[:, 0, :], el(u), er_e[:, :], ALU.add).then_inc(z_step, 1)
                dve.wait_ge(m_turned, b + 1)
                nc.vector.tensor_tensor(z[:, 1, :], m_ps, er_e[:, :], ALU.add).then_inc(z_step, 1)

            def leaky(b):
                dve.wait_ge(z_step, 3 * b + 2)
                nc.vector.scalar_tensor_tensor(zl[:, :, :], z[:, :, :], NEG, z[:, :, :], ALU.mult, ALU.max).then_inc(z_step, 1)

            def below_maximum(b):
                dve.wait_ge(z_step, 3 * b + 3)
                nc.vector.tensor_tensor(zd[:, :], zl[:, 0, :], zl[:, 1, :], ALU.subtract).then_inc(zd_made, 1)

            def rescale(b, t0):
                dve.wait_ge(alpha_made, b + 1)
                dve.wait_ge(summed, CREDIT + CB * b)
                a = acc[:, bass.ds(t0, 1), :].rearrange("p a (h w) -> p (a h) w", w=HW)
                nc.vector.tensor_tensor(a, a, alpha[:, :].unsqueeze(2).to_broadcast([P, H, HW]), ALU.mult).then_inc(scaled, 1)

            def weight(b, u, c0, c1):
                for c in range(c0, c1):
                    rows = G[:, u, c, :].rearrange("p (h w) -> p h w", w=HW)
                    nc.vector.tensor_tensor(rows[:, :, 0:HD], rows[:, :, 0:HD], rows[:, :, HD:HW].to_broadcast([P, H, HD]),
                                            ALU.mult).then_inc(weighted, 1)

            def add(b, t, c):
                dve.wait_ge(part_made, CB * b + c + 1)
                if c:
                    dve.wait_ge(summed, CREDIT + CB * b + c)
                else:
                    dve.wait_ge(scaled, b + 1)
                a = acc[:, bass.ds(t[c], 1), :].rearrange("p a w -> p (a w)")
                nc.vector.tensor_tensor(a, a, part[c % NPS][:, 0:ROW], ALU.add).then_inc(summed, 1)

            def step(b, u, i, has_next):
                un = (u + 1) % RING
                t = tiles(ET.DVE, b)
                dve.wait_ge(ex_made, b + 1)
                weight(b, u, 0, 4)
                rescale(b, t[0])
                done = 4
                for c in range(9):
                    if has_next and c < 3:
                        one_hots(b + 1, un, c)
                    add(b, t, c)
                    more = 1 if c < 2 else 2 if c < 7 else 3
                    weight(b, u, done, min(done + more, CB))
                    done = min(done + more, CB)
                if not has_next:
                    for c in range(9, CB):
                        add(b, t, c)
                    return
                t_next = nc.values_load_multi_w_load_instructions(
                    tile_i[0:1, bass.ds(b + 1, 1), 0:1].rearrange("p a c -> p (a c)"), engines=(ET.DVE,), min_val=0,
                    max_val=NT - 1, skip_runtime_bounds_check_because="as in tiles")[1]
                chunk_forward(b + 1, un)
                add(b, t, 9)
                chunk_backward(b + 1, un)
                add(b, t, 10)
                spread_ends(b + 1)
                add(b, t, 11)
                ends_in(b + 1)
                add(b, t, 12)
                ends_forward(b + 1, un)
                add(b, t, 13)
                ends_backward(b + 1, un)
                add(b, t, 14)
                moved_maxima(b + 1)
                add(b, t, 15)
                own_ends(b + 1, t_next[0])
                add(b, t, 16)
                own_ends_sum(b + 1)
                add(b, t, 17)
                join_forward(b + 1, un)
                join_backward(b + 1, un)
                add(b, t, 18)
                scores(b + 1, un)
                add(b, t, 19)
                leaky(b + 1)
                below_maximum(b + 1)
                add(b, t, 20)

            def before():
                nc.vector.memset(acc[:, :, :], 0.0).then_inc(acc_zero, 1)
                nc.vector.memset(ends_m[:, :], -BIG).then_inc(acc_zero, 1)
                for g in range(3):
                    one_hots(0, 0, g)
                dve.wait_ge(acc_zero, 2)
                t0 = nc.values_load_multi_w_load_instructions(
                    tile_i[0:1, 0, 0:1], engines=(ET.DVE,), min_val=0, max_val=NT - 1,
                    skip_runtime_bounds_check_because="as in tiles")[1]
                chunk_forward(0, 0)
                chunk_backward(0, 0)
                spread_ends(0)
                ends_in(0)
                ends_forward(0, 0)
                ends_backward(0, 0)
                moved_maxima(0)
                own_ends(0, t0[0])
                own_ends_sum(0)
                join_forward(0, 0)
                join_backward(0, 0)
                scores(0, 0)
                leaky(0)
                below_maximum(0)
                dve.wait_ge(summed, CREDIT)

            steps(dve, step, before, lambda: None)


def next_features(nc, bank, ident, bias, acc, er, wx2, table):
    with ExitStack() as ctx:
        def sb(name, shape, dt=F32):
            return ctx.enter_context(nc.sbuf_tensor(name, shape, dt))

        def sem(name):
            return ctx.enter_context(nc.semaphore(name))

        den = sb("nf_den", [P, 2, H])
        rden = sb("nf_rden", [P, 2, H])
        hid = sb("nf_hid", [P, 2, D])
        hid_T = sb("nf_hid_T", [P, 2, 2, P])
        feat = sb("nf_feat", [P, 2, RX])
        d_step = sem("nf_d_step")
        h_step = sem("nf_h_step")
        h_made = sem("nf_h_made")
        turned = sem("nf_turned")
        hT_made = sem("nf_hT_made")
        mm_made = sem("nf_mm_made")
        f_made = sem("nf_f_made")
        f_out = [sem(f"nf_f_out{p}") for p in range(2)]
        block = ctx.enter_context(nc.Block())

        def pairs(eng, tile):
            tile(0, 0, False, 0)
            tile(1, 1, False, 0)
            with eng.Fori(1, NT // 2) as j:
                tile(2 * j, 0, True, j)
                tile(2 * j + 1, 1, True, j)
            tile(NT - 1, 0, True, NT // 2)

        @block.vector
        def _(dve):
            def tile(i, p, again, j):
                a = acc[:, bass.ds(i, 1), :].rearrange("p a (h w) -> p (a h) w", w=HW)
                nc.vector.tensor_scalar(den[:, p, :].unsqueeze(2), a[:, :, HD:HW], DEN_MIN, None, ALU.max).then_inc(d_step, 1)
                dve.wait_ge(d_step, 2 * i + 1)
                nc.vector.reciprocal(rden[:, p, :], den[:, p, :]).then_inc(d_step, 1)
                dve.wait_ge(d_step, 2 * i + 2)
                if again:
                    dve.wait_ge(turned, i - 1)
                nc.vector.tensor_tensor(hid[:, p, :].rearrange("p (h d) -> p h d", d=HD), a[:, :, 0:HD],
                                        rden[:, p, :].unsqueeze(2).to_broadcast([P, H, HD]), ALU.mult).then_inc(h_step, 1)
                dve.wait_ge(h_step, i + 1)
                nc.vector.tensor_tensor(hid[:, p, :], hid[:, p, :], bias[:, :], ALU.add).then_inc(h_made, 1)

            pairs(dve, tile)

        @block.tensor
        def _(pe):
            def tile(i, p, again, j):
                pe.wait_ge(h_made, i + 1)
                if again:
                    pe.wait_ge(hT_made, i - 1)
                for k in range(2):
                    tr = nc.tensor.transpose(bank[p][:, k * P:(k + 1) * P], hid[:, p, k * P:(k + 1) * P], ident[:, :])
                tr.then_inc(turned, 1)
                pe.wait_ge(hT_made, i + 1)
                if again:
                    pe.wait_ge(f_made, i - 1)
                for k in range(2):
                    mm = nc.tensor.matmul(bank[2 + p][:, 0:RX], hid_T[:, p, k, :], wx2[:, k, :], start=(k == 0), stop=(k == 1))
                mm.then_inc(mm_made, 1)

            pairs(pe, tile)

        @block.scalar
        def _(act):
            def tile(i, p, again, j):
                act.wait_ge(turned, i + 1)
                if again:
                    act.wait_ge(mm_made, i - 1)
                nc.scalar.activation(hid_T[:, p, :, :], bank[p][:, 0:2 * P].rearrange("p (k n) -> p k n", k=2),
                                     ACT.Relu).then_inc(hT_made, 1)
                act.wait_ge(mm_made, i + 1)
                if again:
                    act.wait_ge(f_out[p], 16 * j)
                nc.scalar.copy(er[:, bass.ds(i, 1), :].rearrange("p a h -> p (a h)"), bank[2 + p][:, ROW:RX])
                nc.scalar.copy(feat[:, p, :], bank[2 + p][:, 0:RX]).then_inc(f_made, 1)

            pairs(act, tile)

        @block.sync
        def _(sp):
            def tile(i, p, again, j):
                sp.wait_ge(f_made, i + 1)
                sp.dma_start(table[bass.ds(i * P, P), :], feat[:, p, 0:ROW]).then_inc(f_out[p], 16)

            pairs(sp, tile)
            sp.wait_ge(f_out[0], 16 * ((NT + 1) // 2))
            sp.wait_ge(f_out[1], 16 * (NT // 2))


def finish(nc, x, bias, acc, epst, out):
    with ExitStack() as ctx:
        def sb(name, shape, dt=F32):
            return ctx.enter_context(nc.sbuf_tensor(name, shape, dt))

        def sem(name):
            return ctx.enter_context(nc.semaphore(name))

        xs = sb("fi_x", [P, 2, D])
        den = sb("fi_den", [P, 2, H])
        rden = sb("fi_rden", [P, 2, H])
        y = sb("fi_y", [P, 2, D])
        stats = sb("fi_stats", [P, 2, 6])
        mv = sb("fi_mv", [P, 2, 2])
        sd = sb("fi_sd", [P, 2, 1])
        rs = sb("fi_rs", [P, 2, 2])
        res = sb("fi_res", [P, 2, D])
        x_in = [sem(f"fi_x_in{p}") for p in range(2)]
        step = sem("fi_step")
        x_used = sem("fi_x_used")
        stats_seen = sem("fi_stats_seen")
        mv_made = sem("fi_mv_made")
        sd_made = sem("fi_sd_made")
        rs_made = sem("fi_rs_made")
        r_made = sem("fi_r_made")
        r_out = [sem(f"fi_r_out{p}") for p in range(2)]
        block = ctx.enter_context(nc.Block())
        PAIRS = NT // 2

        @block.sync
        def _(sp):
            def load(i, p, n):
                sp.dma_start(xs[0:n, p, :], x[bass.ds(i * P, n), :]).then_inc(x_in[p], 16)

            def store(i, p, n):
                sp.wait_ge(r_made, i + 1)
                sp.dma_start(out[bass.ds(i * P, n), :], res[0:n, p, :]).then_inc(r_out[p], 16)

            load(0, 0, P)
            load(1, 1, P)
            with sp.Fori(0, PAIRS - 1) as j:
                for p in range(2):
                    sp.wait_ge(x_used, 2 * j + p + 1)
                    load(2 * j + p + 2, p, P)
                    store(2 * j + p, p, P)
            sp.wait_ge(x_used, NT - 2)
            load(NT - 1, 0, LAST)
            store(NT - 3, 0, P)
            store(NT - 2, 1, P)
            store(NT - 1, 0, LAST)
            sp.wait_ge(r_out[0], 16 * (PAIRS + 1))
            sp.wait_ge(r_out[1], 16 * PAIRS)

        @block.vector
        def _(dve):
            S = 7

            def tile(i, p, j, j_out):
                a = acc[:, bass.ds(i, 1), :].rearrange("p a (h w) -> p (a h) w", w=HW)
                nc.vector.tensor_scalar(den[:, p, :].unsqueeze(2), a[:, :, HD:HW], DEN_MIN, None, ALU.max).then_inc(step, 1)
                dve.wait_ge(step, S * i + 1)
                nc.vector.reciprocal(rden[:, p, :], den[:, p, :]).then_inc(step, 1)
                dve.wait_ge(step, S * i + 2)
                nc.vector.tensor_tensor(y[:, p, :].rearrange("p (h d) -> p h d", d=HD), a[:, :, 0:HD],
                                        rden[:, p, :].unsqueeze(2).to_broadcast([P, H, HD]), ALU.mult).then_inc(step, 1)
                dve.wait_ge(step, S * i + 3)
                nc.vector.tensor_tensor(y[:, p, :], y[:, p, :], bias[:, :], ALU.add).then_inc(step, 1)
                dve.wait_ge(step, S * i + 4)
                dve.wait_ge(x_in[p], 16 * j + 16)
                nc.vector.scalar_tensor_tensor(y[:, p, :], y[:, p, :], 0.0, xs[:, p, :], ALU.max, ALU.add).then_inc(x_used, 1)
                dve.wait_ge(x_used, i + 1)
                nc.vector.bn_stats(stats[:, p, :], y[:, p, :]).then_inc(step, 1)
                dve.wait_ge(step, S * i + 5)
                dve.sem_inc(stats_seen, 1)
                nc.vector.bn_aggr(mv[:, p, :], stats[:, p, :]).then_inc(mv_made, 1)
                dve.wait_ge(sd_made, i + 1)
                nc.vector.reciprocal(rs[:, p, 0:1], sd[:, p, :]).then_inc(step, 1)
                dve.wait_ge(step, S * i + 6)
                nc.vector.scalar_tensor_tensor(rs[:, p, 1:2], mv[:, p, 0:1], -1.0, rs[:, p, 0:1], ALU.mult, ALU.mult).then_inc(step, 1)
                dve.wait_ge(step, S * i + 7)
                if j_out is not None:
                    dve.wait_ge(r_out[p], j_out)
                nc.vector.tensor_scalar(res[:, p, :], y[:, p, :], rs[:, p, 0:1], rs[:, p, 1:2], ALU.mult, ALU.add).then_inc(r_made, 1)

            tile(0, 0, 0, None)
            tile(1, 1, 0, None)
            with dve.Fori(1, PAIRS) as j:
                tile(2 * j, 0, j, 16 * j)
                tile(2 * j + 1, 1, j, 16 * j)
            tile(NT - 1, 0, PAIRS, 16 * PAIRS)

        @block.scalar
        def _(act):
            def tile(i, p):
                act.wait_ge(mv_made, i + 1)
                nc.scalar.activation(sd[:, p, :], mv[:, p, 1:2], ACT.Sqrt, bias=epst[:, 0:1]).then_inc(sd_made, 1)

            with act.Fori(0, PAIRS) as j:
                tile(2 * j, 0)
                tile(2 * j + 1, 1)
            tile(NT - 1, 0)


def kernel(x, src, dst, node_type_24, L0_gnn_emb, L0_gnn_le_W1, L0_gnn_le_b1, L0_gnn_ln_g, L0_gnn_ln_b, L0_gnn_le_W2,
           L0_gnn_le_b2, L0_gnn_W1, L0_gnn_al1, L0_gnn_ar1, L0_gnn_b1, L0_gnn_W2, L0_gnn_al2, L0_gnn_ar2, L0_gnn_b2):
    import numpy as np
    import concourse.bacc as bacc
    from concourse.bass_utils import run_bass_kernel_spmd

    nc = bacc.Bacc("TRN2", target_bir_lowering=False, num_devices=1)
    arrays = {}

    def given(name, a):
        arrays[name] = np.ascontiguousarray(a)
        return nc.dram_tensor(name, arrays[name].shape, mybir.dt.from_np(arrays[name].dtype), kind="ExternalInput").ap()

    t = np.transpose
    out = nc.dram_tensor("out", (N, D), F32, kind="ExternalOutput").ap()
    gnn_kernel(
        nc, given("x", x), given("xT", t(np.asarray(x))), given("src", src), given("dst", dst), given("labels", node_type_24),
        given("embT", t(np.asarray(L0_gnn_emb))), given("leW1T", t(np.asarray(L0_gnn_le_W1))), given("le_b1", L0_gnn_le_b1),
        given("ln_g", L0_gnn_ln_g), given("ln_b", L0_gnn_ln_b), given("leW2", L0_gnn_le_W2), given("le_b2", L0_gnn_le_b2),
        [given("W1", L0_gnn_W1), given("W2", L0_gnn_W2)],
        [given("W1T", t(np.asarray(L0_gnn_W1))), given("W2T", t(np.asarray(L0_gnn_W2)))],
        [given("al1", L0_gnn_al1), given("al2", L0_gnn_al2)], [given("ar1", L0_gnn_ar1), given("ar2", L0_gnn_ar2)],
        [given("b1", L0_gnn_b1), given("b2", L0_gnn_b2)], out)
    r = run_bass_kernel_spmd(nc, [arrays], core_ids=[0])
    return r.results[0]["out"]
```

```python
from contextlib import ExitStack

import concourse.bass as bass
from concourse import mybir

F32 = mybir.dt.float32
I32 = mybir.dt.int32
BF16 = mybir.dt.bfloat16
ALU = mybir.AluOpType
ACT = mybir.ActivationFunctionType
AX = mybir.AxisListType
ET = mybir.EngineType

P = 128
N = 6250
D = 256
H = 4
HD = D // H
HW = HD + 1
ROW = H * HW
RX = ROW + H
E = 106250
HID = 4 * D
LABELS = 24
NT = -(-N // P)
LAST = N - (NT - 1) * P
CB = 21
RING = 3
CHUNKS = (E + NT * (P - 1)) // P
NB = -(-CHUNKS // (CB * RING)) * RING
NC = NB * CB
CG = -(-NC // P)
HC = H * CB
PARTS = 3
PR = 32
K3 = PARTS * PR
TW = 24
MG = 3
NPS = 3
ROWS_E = 125
COLS_E = E // ROWS_E
BIG = 2.0 ** 100
PAD_DST = 8191
NEG = 0.2
LN_EPS = 1e-5
DEN_MIN = 1e-9


class Counter:

    def __init__(self, sem):
        self.sem, self.n = sem, 0

    def inc(self, ins, by=1):
        ins.then_inc(self.sem, by)
        self.n += by
        return self.n

    def wait(self, eng, n=None):
        eng.wait_ge(self.sem, self.n if n is None else n)


def beyond(i, n):
    return not isinstance(i, int) or i >= n


def gnn_kernel(nc, x, xT, src, dst, labels, embT, leW1T, le_b1, ln_g, ln_b, leW2, le_b2,
               gW, gWT, gal, gar, gb, out):
    assert ROWS_E * COLS_E == E
    table = [nc.dram_tensor(f"table{l}", (NT * P, ROW), F32, kind="Internal").ap() for l in range(2)]
    src_s = nc.dram_tensor("src_sorted", (E + P, 1), I32, kind="Internal").ap()
    dst_s = nc.dram_tensor("dst_sorted", (E + P, 1), I32, kind="Internal").ap()
    key_d = nc.dram_tensor("slot_keys", (CG * P, P), F32, kind="Internal").ap()

    with ExitStack() as top:
        def sb(name, shape, dt=F32, ctx=top):
            return ctx.enter_context(nc.sbuf_tensor(name, shape, dt))

        def sem(name, ctx=top):
            return ctx.enter_context(nc.semaphore(name))

        bank = [top.enter_context(nc.psum_tensor(f"bank{i}", [P, 512], F32)) for i in range(8)]

        ident = sb("ident", [P, P])
        ones = sb("ones", [P, P])
        iota_f = sb("iota_f", [P, P])
        pidx = sb("pidx", [P, 1])
        epst = sb("epst", [P, 1])
        pick_c = sb("pick_c", [HC, CB])
        pick_h = sb("pick_h", [HC, H])
        pick_hT = sb("pick_hT", [H, HC])
        src_idx = sb("src_idx", [P, CG * P], I32)
        dst_loc = sb("dst_loc", [P, CG * P])
        flags = sb("flags", [HC, NB, P + 1], BF16)
        flags_x = sb("flags_x", [H, NB, 2 * CB + 2])
        tile_i = sb("tile_i", [1, NB, TW], I32)
        carry_row = sb("carry_row", [P, NB])
        er = sb("er", [P, NT, H])
        wx2 = sb("wx2", [P, 2, RX])
        biasb = [sb(f"bias{l}", [P, D]) for l in range(2)]
        acc = sb("acc", [P, NT, ROW])

        with ExitStack() as ph:
            w1t = sb("w1t", [P, 4, HID], ctx=ph)
            w3 = sb("w3", [K3, HID], BF16, ctx=ph)
            hot = sb("hot", [K3, N], BF16, ctx=ph)
            wc = sb("wc", [P, HID // P, RX], ctx=ph)
            bias_c = sb("bias_c", [P, RX], ctx=ph)
            g_col = sb("g_col", [P, HID // P], ctx=ph)
            b_col = sb("b_col", [P, HID // P], ctx=ph)

            with ExitStack() as pw:
                w2n = sb("w2n", [P, 2, HID], ctx=pw)
                wx1 = sb("wx1", [P, 2, RX], ctx=pw)
                wn = [sb(f"wn{l}", [P, 2, D], ctx=pw) for l in range(2)]
                wt = [sb(f"wt{l}", [P, 2, D], ctx=pw) for l in range(2)]
                alr = [sb(f"alr{l}", [P, 2, 2 * H], ctx=pw) for l in range(2)]
                emb_t = sb("emb_t", [P, 2, LABELS], ctx=pw)
                emb_r = sb("emb_r", [P, 2, PARTS, PR], ctx=pw)
                lab = sb("lab", [K3, N], I32, ctx=pw)
                row_i = sb("row_i", [P, 1], I32, ctx=pw)
                row_f = sb("row_f", [P, 1], ctx=pw)
                w_sum = sb("w_sum", [P, 2], ctx=pw)
                w_mean = sb("w_mean", [P, 2], ctx=pw)
                w3_f = sb("w3_f", [K3, HID], ctx=pw)
                w3_sum = sb("w3_sum", [K3, 1], ctx=pw)
                w3_mean = sb("w3_mean", [K3, 1], ctx=pw)
                w3_p = sb("w3_p", [K3, PARTS, HID], BF16, ctx=pw)
                lab_set = sem("lab_set", pw)
                lab_loaded = sem("lab_loaded", pw)
                emb_made = sem("emb_made", pw)
                hot_made = sem("hot_made", pw)
                centre = Counter(sem("centre", pw))
                b2col = sb("b2col", [P, 2], ctx=pw)
                iota_i = sb("iota_i", [P, P], I32, ctx=pw)
                pidx_i = sb("pidx_i", [P, 1], I32, ctx=pw)
                masks_set = sem("masks_set", pw)
                masks_cut = sem("masks_cut", pw)
                iotas_made = sem("iotas_made", pw)
                alr_zero = sem("alr_zero", pw)
                w_loaded = sem("w_loaded", pw)
                a_loaded = sem("a_loaded", pw)
                row_loaded = sem("row_loaded", pw)
                elw_made = sem("elw_made", pw)
                wx_made = sem("wx_made", pw)
                w3_made = sem("w3_made", pw)
                w3_read = sem("w3_read", pw)
                wc_made = sem("wc_made", pw)
                wc_read = sem("wc_read", pw)
                block = pw.enter_context(nc.Block())
                wx = [wx1, wx2]
                N_W = 12

                @block.sync
                def _(sp):
                    sp.dma_start(w1t[:, :, :], leW1T.rearrange("(k p) n -> p k n", p=P)).then_inc(w_loaded, 16)
                    sp.dma_start(w2n[:, :, :], leW2.rearrange("(k p) n -> p k n", p=P)).then_inc(w_loaded, 16)
                    sp.dma_start(emb_t[:, :, :], embT.rearrange("(k p) n -> p k n", p=P)).then_inc(w_loaded, 16)
                    for l in range(2):
                        sp.dma_start(wn[l][:, :, :], gW[l].rearrange("(k p) n -> p k n", p=P)).then_inc(w_loaded, 16)
                        sp.dma_start(wt[l][:, :, :], gWT[l].rearrange("(k p) n -> p k n", p=P)).then_inc(w_loaded, 16)
                        sp.dma_start(biasb[l][:, :], gb[l].rearrange("(a n) -> a n", a=1).broadcast_to([P, D])
                                     ).then_inc(w_loaded, 16)
                    with nc.allow_non_contiguous_dma(reason="vectors of a few hundred features, one to a partition"):
                        sp.dma_start(b2col[:, :], le_b2.rearrange("(k p) -> p k", p=P)).then_inc(w_loaded, 16)
                        sp.dma_start(g_col[:, :], ln_g.rearrange("(k p) -> p k", p=P)).then_inc(w_loaded, 16)
                        sp.dma_start(b_col[:, :], ln_b.rearrange("(k p) -> p k", p=P)).then_inc(w_loaded, 16)
                    sp.wait_ge(lab_set, 1)
                    for k in range(PARTS):
                        sp.dma_start(lab[k * PR:k * PR + LABELS, :],
                                     labels.rearrange("(a n) -> a n", a=1).broadcast_to([LABELS, N])).then_inc(lab_loaded, 16)
                    sp.wait_ge(w3_read, 2)
                    for k in range(PARTS):
                        r = k * PR + LABELS
                        sp.dma_start(w3_f[r:r + 1, :], le_b1.rearrange("(a n) -> a n", a=1)).then_inc(row_loaded, 16)

                @block.gpsimd
                def _(pool):
                    nc.gpsimd.memset(ones[:, :], 1.0).then_inc(masks_set, 1)
                    for l in range(2):
                        nc.gpsimd.memset(alr[l][:, :, :], 0.0).then_inc(alr_zero, 1)
                    nc.gpsimd.memset(ident[:, :], 0.0).then_inc(masks_set, 1)
                    nc.gpsimd.iota(iota_i[:, :], [[1, P]], base=0, channel_multiplier=0).then_inc(iotas_made, 1)
                    nc.gpsimd.iota(pidx_i[:, :], [[0, 1]], base=0, channel_multiplier=1).then_inc(iotas_made, 1)
                    pool.wait_ge(masks_set, 2)
                    nc.gpsimd.affine_select(out=ident[:, :], in_=ident[:, :], compare_op=ALU.not_equal, fill=1.0,
                                            base=0, pattern=[[-1, P]], channel_multiplier=1).then_inc(masks_cut, 1)

                @block.scalar
                def _(act):
                    act.wait_ge(alr_zero, 2)
                    for l in range(2):
                        for h in range(H):
                            rows = slice((h % 2) * HD, (h % 2) * HD + HD)
                            act.dma_start(alr[l][rows, h // 2, h:h + 1],
                                          gal[l][h, :].rearrange("(d a) -> d a", a=1)).then_inc(a_loaded, 16)
                            act.dma_start(alr[l][rows, h // 2, H + h:H + h + 1],
                                          gar[l][h, :].rearrange("(d a) -> d a", a=1)).then_inc(a_loaded, 16)

                @block.tensor
                def _(pe):
                    pe.wait_ge(w_loaded, 16 * N_W)
                    pe.wait_ge(a_loaded, 16 * 4 * H)
                    for l in range(2):
                        for m in range(2):
                            for k in range(2):
                                mm = nc.tensor.matmul(bank[0][:, (2 * l + m) * 8:(2 * l + m) * 8 + 8],
                                                      wn[l][:, k, m * P:(m + 1) * P], alr[l][:, k, :],
                                                      start=(k == 0), stop=(k == 1))
                    mm.then_inc(elw_made, 1)
                    pe.wait_ge(emb_made, 1)
                    for half in range(2):
                        for k in range(2):
                            mm = nc.tensor.matmul(bank[1 + half][0:K3, :], emb_r[:, k, :, :].rearrange("p a r -> p (a r)"),
                                                  w1t[:, 2 + k, half * 512:(half + 1) * 512],
                                                  start=(k == 0), stop=(k == 1))
                        mm.then_inc(w3_made, 1)
                    pe.wait_ge(wx_made, 3)
                    for kb in range(HID // P):
                        if kb >= 4:
                            pe.wait_ge(wc_read, kb - 3)
                        for m in range(2):
                            mm = nc.tensor.matmul(bank[3 + kb % 4][:, 0:RX], w2n[:, m, kb * P:(kb + 1) * P],
                                                  wx1[:, m, :], start=(m == 0), stop=(m == 1))
                        mm.then_inc(wc_made, 1)
                    for m in range(2):
                        mm = nc.tensor.matmul(bank[7][:, 0:RX], b2col[:, m:m + 1].to_broadcast([P, P]),
                                              wx1[:, m, :], start=(m == 0), stop=(m == 1))
                    mm.then_inc(wc_made, 1)

                @block.vector
                def _(dve):
                    nc.vector.memset(lab[:, :], LABELS).then_inc(lab_set, 1)
                    centre.inc(nc.vector.memset(emb_r[:, :, :, :], 0.0))
                    dve.wait_ge(iotas_made, 2)
                    nc.vector.tensor_copy(iota_f[:, :], iota_i[:, :])
                    nc.vector.tensor_copy(pidx[:, :], pidx_i[:, :])
                    centre.inc(nc.vector.tensor_scalar(row_i[:, :], pidx_i[:, :], PR - 1, None, ALU.bitwise_and))
                    centre.wait(dve)
                    centre.inc(nc.vector.tensor_copy(row_f[:, :], row_i[:, :]))
                    nc.vector.memset(epst[:, :], LN_EPS)
                    dve.wait_ge(masks_cut, 1)
                    rows = ident[0:HC, 0:HC]
                    nc.vector.tensor_reduce(pick_c[:, :], rows.rearrange("p (c h) -> p c h", h=H), AX.X, ALU.add)
                    nc.vector.tensor_reduce(pick_h[:, :], rows.rearrange("p (c h) -> p h c", h=H), AX.X, ALU.add)
                    nc.vector.tensor_copy(pick_hT[:, :].rearrange("p (c h) -> p c h", h=H),
                                          ident[0:H, 0:H].unsqueeze(1).to_broadcast([H, CB, H]))
                    dve.wait_ge(w_loaded, 16 * N_W)
                    nc.vector.tensor_copy(emb_r[:, :, :, 0:LABELS], emb_t[:, :, :].unsqueeze(2).to_broadcast([P, 2, PARTS, LABELS])
                                          ).then_inc(emb_made, 1)
                    centre.inc(nc.vector.tensor_reduce(w_sum[:, :], w1t[:, 0:2, :], AX.X, ALU.add))
                    centre.wait(dve)
                    centre.inc(nc.vector.tensor_scalar(w_mean[:, :], w_sum[:, :], 1.0 / HID, None, ALU.mult))
                    centre.wait(dve)
                    for k in range(2):
                        nc.vector.tensor_scalar(w1t[:, k, :], w1t[:, k, :], w_mean[:, k:k + 1], None, ALU.subtract)
                    dve.wait_ge(elw_made, 1)
                    for l in range(2):
                        for m in range(2):
                            heads = wx[l][:, m, 0:ROW].rearrange("p (h w) -> p h w", w=HW)
                            nc.vector.tensor_copy(heads[:, :, 0:HD], wt[l][:, m, :].rearrange("p (h d) -> p h d", d=HD))
                            c = (2 * l + m) * 8
                            nc.vector.tensor_copy(heads[:, :, HD:HW], bank[0][:, c:c + H].rearrange("p (h a) -> p h a", a=1))
                            last = nc.vector.tensor_copy(wx[l][:, m, ROW:RX], bank[0][:, c + H:c + 2 * H])
                            if m == 1:
                                last.then_inc(wx_made, 1)
                    nc.vector.memset(tile_i[:, :, :], 0).then_inc(wx_made, 1)
                    for half in range(2):
                        dve.wait_ge(w3_made, half + 1)
                        nc.vector.tensor_copy(w3_f[:, half * 512:(half + 1) * 512], bank[1 + half][0:K3, :]).then_inc(w3_read, 1)
                    for kb in range(HID // P):
                        dve.wait_ge(wc_made, kb + 1)
                        nc.vector.tensor_copy(wc[:, kb, :], bank[3 + kb % 4][:, 0:RX]).then_inc(wc_read, 1)
                    dve.wait_ge(wc_made, HID // P + 1)
                    nc.vector.tensor_copy(bias_c[:, :], bank[7][:, 0:RX])
                    dve.wait_ge(row_loaded, 16 * PARTS)
                    centre.inc(nc.vector.tensor_reduce(w3_sum[:, :], w3_f[:, :], AX.X, ALU.add))
                    centre.wait(dve)
                    centre.inc(nc.vector.tensor_scalar(w3_mean[:, :], w3_sum[:, :], 1.0 / HID, None, ALU.mult))
                    centre.wait(dve)
                    centre.inc(nc.vector.tensor_scalar(w3_f[:, :], w3_f[:, :], w3_mean[:, 0:1], None, ALU.subtract))
                    for k in range(PARTS):
                        centre.wait(dve)
                        centre.inc(nc.vector.tensor_copy(w3_p[:, k, :], w3_f[:, :]))
                        centre.wait(dve)
                        rows = slice(k * PR, (k + 1) * PR)
                        nc.vector.tensor_copy(w3[rows, :], w3_p[rows, k, :])
                        if k < PARTS - 1:
                            centre.inc(nc.vector.tensor_tensor(w3_f[:, :], w3_f[:, :], w3_p[:, k, :], ALU.subtract))
                    dve.wait_ge(lab_loaded, 16 * PARTS)
                    nc.vector.tensor_scalar(hot[:, :], lab[:, :], row_f[0:K3, 0:1], None, ALU.is_equal).then_inc(hot_made, 1)

            with ExitStack() as pw:
                dst_i = sb("dst_i", [ROWS_E, COLS_E], I32, ctx=pw)
                dst_f = sb("dst_f", [ROWS_E, COLS_E], ctx=pw)
                below = sb("below", [ROWS_E, COLS_E], ctx=pw)
                pad = sb("pad", [1, 2 * P], I32, ctx=pw)
                thr = sb("thr", [P, NT], ctx=pw)
                cnt = sb("cnt", [ROWS_E, NT], ctx=pw)
                first = sb("first", [P, NT + 1], ctx=pw)
                n_e = sb("n_e", [P, NT], ctx=pw)
                n_ci = sb("n_ci", [P, NT], I32, ctx=pw)
                n_c = sb("n_c", [P, NT], ctx=pw)
                chunk0 = sb("chunk0", [P, NT + 1], ctx=pw)
                cid_i = sb("cid_i", [P, CG], I32, ctx=pw)
                cid = sb("cid", [P, CG], ctx=pw)
                hit = sb("hit", [P, 3, NT], ctx=pw)
                tile_c = sb("tile_c", [P, CG], ctx=pw)
                tile_ch = sb("tile_ch", [P, CG], ctx=pw)
                tile_e = sb("tile_e", [P, CG], ctx=pw)
                node0 = sb("node0", [P, CG], ctx=pw)
                base_f = sb("base_f", [P, CG], ctx=pw)
                base_i = sb("base_i", [P, CG], I32, ctx=pw)
                sl_d = sb("sl_d", [P, CG, P], I32, ctx=pw)
                sl_s = sb("sl_s", [P, CG, P], I32, ctx=pw)
                sl_df = sb("sl_df", [P, CG, P], ctx=pw)
                sl_sf = sb("sl_sf", [P, CG, P], ctx=pw)
                sl_k = sb("sl_k", [P, CG, P], ctx=pw)
                keys = sb("keys", [P, 2 * CG * P + 1], ctx=pw)
                tile_b = sb("tile_b", [P, CG * P], ctx=pw)
                key_t = sb("key_t", [HC, NB, P], ctx=pw)
                diff = sb("diff", [H, NB, 2 * CB], ctx=pw)
                ends_k = sb("ends_k", [P, NB], ctx=pw)
                e_loaded = sem("e_loaded", pw)
                e_copied = sem("e_copied", pw)
                pad_set = sem("pad_set", pw)
                thr_set = sem("thr_set", pw)
                counted = sem("counted", pw)
                summed = sem("summed", pw)
                base_set = sem("base_set", pw)
                sl_loaded = [sem("sl_loaded_d", pw), sem("sl_loaded_s", pw)]
                turned = sem("turned", pw)
                slots_read = sem("slots_read", pw)
                keys_read = sem("keys_read", pw)
                keys_out = sem("keys_out", pw)
                keys_in = sem("keys_in", pw)
                k_ready = sem("k_ready", pw)
                step_v = Counter(sem("step_v", pw))
                block = pw.enter_context(nc.Block())

                @block.sync
                def _(sp):
                    sp.dma_start(dst_i[:, :], dst.rearrange("(p n) -> p n", p=ROWS_E)).then_inc(e_loaded, 16)
                    sp.dma_start(src_s[0:E, :].rearrange("(p n) a -> p (n a)", p=ROWS_E),
                                 src.rearrange("(p n) -> p n", p=ROWS_E)).then_inc(e_copied, 16)
                    sp.dma_start(dst_s[0:E, :].rearrange("(p n) a -> p (n a)", p=ROWS_E),
                                 dst.rearrange("(p n) -> p n", p=ROWS_E)).then_inc(e_copied, 16)
                    sp.wait_ge(pad_set, 2)
                    sp.dma_start(src_s[E:E + P, :].rearrange("(p n) a -> p (n a)", p=1), pad[:, 0:P]).then_inc(e_copied, 16)
                    sp.dma_start(dst_s[E:E + P, :].rearrange("(p n) a -> p (n a)", p=1), pad[:, P:2 * P]).then_inc(e_copied, 16)
                    sp.wait_ge(k_ready, CG)
                    sp.dma_start(key_d.rearrange("(g p) e -> p g e", p=P), sl_k[:, :, :]).then_inc(keys_out, 16)
                    sp.wait_ge(keys_out, 16)
                    for h in range(H):
                        sp.dma_start(key_t[h:HC:H, :, :],
                                     key_d[0:NC, :].rearrange("(b c) e -> c b e", c=CB)).then_inc(keys_in, 16)

                @block.gpsimd
                def _(pool):
                    nc.gpsimd.memset(pad[:, 0:P], 0).then_inc(pad_set, 1)
                    nc.gpsimd.memset(pad[:, P:2 * P], PAD_DST).then_inc(pad_set, 1)
                    nc.gpsimd.iota(cid_i[:, :], [[P, CG]], base=0, channel_multiplier=1).then_inc(thr_set, 1)
                    pool.wait_ge(base_set, 1)
                    pool.wait_ge(e_copied, 64)
                    for g in range(CG):
                        pool.indirect_dma_start(sl_d[:, g, :], None, dst_s[:, :],
                                                bass.IndirectOffsetOnAxis(base_i[:, g:g + 1], 0)).then_inc(sl_loaded[0], 16)
                    for g in range(CG):
                        pool.indirect_dma_start(sl_s[:, g, :], None, src_s[:, :],
                                                bass.IndirectOffsetOnAxis(base_i[:, g:g + 1], 0)).then_inc(sl_loaded[1], 16)

                @block.tensor
                def _(pe):
                    pe.wait_ge(counted, NT)
                    nc.tensor.matmul(bank[0][:, 0:NT], ones[0:ROWS_E, :], cnt[:, :],
                                     start=True, stop=True).then_inc(summed, 1)
                    pe.wait_ge(k_ready, CG)
                    for g in range(CG):
                        if g >= 2:
                            pe.wait_ge(slots_read, g - 1)
                            pe.wait_ge(keys_read, g - 1)
                        a, b = bank[1 + g % 2], bank[3 + g % 2]
                        nc.tensor.transpose(a[:, 0:P], sl_sf[:, g, :], ident[:, :])
                        nc.tensor.transpose(a[:, P:2 * P], sl_df[:, g, :], ident[:, :])
                        nc.tensor.matmul(b[:, 0:P], sl_k[:, g, 0:1].to_broadcast([P, P]), ident[:, :], start=True, stop=True)
                        nc.tensor.matmul(b[:, P:2 * P], sl_k[:, g, P - 1:P].to_broadcast([P, P]), ident[:, :], start=True, stop=True)
                        nc.tensor.matmul(b[:, 2 * P:3 * P], tile_c[:, g:g + 1].to_broadcast([P, P]), ident[:, :],
                                         start=True, stop=True).then_inc(turned, 1)

                @block.scalar
                def _(act):
                    for g in range(CG):
                        act.wait_ge(turned, g + 1)
                        nc.scalar.copy(src_idx[:, g * P:(g + 1) * P], bank[1 + g % 2][:, 0:P])
                        nc.scalar.copy(dst_loc[:, g * P:(g + 1) * P], bank[1 + g % 2][:, P:2 * P]).then_inc(slots_read, 1)

                @block.vector
                def _(dve):
                    s = step_v
                    s.inc(nc.vector.tensor_scalar(thr[:, :], iota_f[:, 0:NT], float(P), float(P), ALU.mult, ALU.add))
                    dve.wait_ge(e_loaded, 16)
                    s.inc(nc.vector.tensor_copy(dst_f[:, :], dst_i[:, :]))
                    s.wait(dve)
                    with dve.Fori(0, NT) as t:
                        nc.vector.tensor_scalar(below[:, :], dst_f[:, :], thr[0:ROWS_E, bass.ds(t, 1)], 0.0,
                                                ALU.is_lt, ALU.add, accum_out=cnt[:, bass.ds(t, 1)]).then_inc(counted, 1)
                        dve.wait_ge(counted, t + 1)
                    s.inc(nc.vector.memset(first[:, 0:1], 0.0))
                    s.inc(nc.vector.memset(chunk0[:, 0:1], 0.0))
                    s.inc(nc.vector.memset(keys[:, 0:1], -BIG))
                    s.inc(nc.vector.memset(flags[:, :, :], 0.0))
                    s.inc(nc.vector.memset(flags_x[:, :, :], 0.0))
                    dve.wait_ge(thr_set, 1)
                    s.inc(nc.vector.tensor_copy(cid[:, :], cid_i[:, :]))
                    dve.wait_ge(summed, 1)
                    s.inc(nc.vector.tensor_copy(first[:, 1:NT + 1], bank[0][:, 0:NT]))
                    s.wait(dve)
                    s.inc(nc.vector.tensor_tensor(n_e[:, :], first[:, 1:NT + 1], first[:, 0:NT], ALU.subtract))
                    s.wait(dve)
                    s.inc(nc.vector.tensor_scalar(n_ci[:, :], n_e[:, :], float(P - 1), None, ALU.add))
                    s.wait(dve)
                    s.inc(nc.vector.tensor_scalar(n_ci[:, :], n_ci[:, :], 7, None, ALU.arith_shift_right))
                    s.wait(dve)
                    s.inc(nc.vector.tensor_copy(n_c[:, :], n_ci[:, :]))
                    s.wait(dve)
                    s.inc(nc.vector.tensor_tensor_scan(chunk0[:, 1:NT + 1], ones[:, 0:NT], n_c[:, :], 0.0, ALU.mult, ALU.add))
                    s.wait(dve)
                    starts = chunk0[:, 1:NT]
                    for g in range(CG):
                        c = cid[:, g:g + 1]
                        s.inc(nc.vector.tensor_scalar(hit[:, 0, 0:NT - 1], starts, c, 0.0, ALU.is_le, ALU.add,
                                                      accum_out=tile_c[:, g:g + 1]))
                        s.inc(nc.vector.scalar_tensor_tensor(hit[:, 1, 0:NT - 1], starts, c, n_c[:, 0:NT - 1], ALU.is_le,
                                                             ALU.mult, accum_out=tile_ch[:, g:g + 1]))
                        s.inc(nc.vector.scalar_tensor_tensor(hit[:, 2, 0:NT - 1], starts, c, n_e[:, 0:NT - 1], ALU.is_le,
                                                             ALU.mult, accum_out=tile_e[:, g:g + 1]))
                        s.wait(dve)
                    s.inc(nc.vector.tensor_scalar(node0[:, :], tile_c[:, :], float(P), None, ALU.mult))
                    s.inc(nc.vector.tensor_tensor(base_f[:, :], cid[:, :], tile_ch[:, :], ALU.subtract))
                    s.wait(dve)
                    s.inc(nc.vector.scalar_tensor_tensor(base_f[:, :], base_f[:, :], float(P), tile_e[:, :], ALU.mult, ALU.add))
                    s.wait(dve)
                    nc.vector.tensor_scalar(base_i[:, :], base_f[:, :], float(E), None, ALU.min).then_inc(base_set, 1)
                    dve.wait_ge(sl_loaded[0], 16 * CG)
                    dve.wait_ge(sl_loaded[1], 16 * CG)
                    for g in range(CG):
                        nc.vector.tensor_copy(sl_sf[:, g, :], sl_s[:, g, :])
                        nc.vector.tensor_scalar(sl_df[:, g, :], sl_d[:, g, :], node0[:, g:g + 1], None, ALU.subtract)
                        nc.vector.tensor_scalar(sl_k[:, g, :], sl_d[:, g, :], BIG, None, ALU.mult).then_inc(k_ready, 1)
                    for g in range(CG):
                        dve.wait_ge(turned, g + 1)
                        b = bank[3 + g % 2]
                        ends = keys[:, 1 + 2 * g * P:1 + 2 * (g + 1) * P].rearrange("p (c two) -> p two c", two=2)
                        s.inc(nc.vector.tensor_copy(ends, b[:, 0:2 * P].rearrange("p (two c) -> p two c", two=2)))
                        nc.vector.tensor_copy(tile_b[:, g * P:(g + 1) * P], b[:, 2 * P:3 * P]).then_inc(keys_read, 1)
                    s.wait(dve)
                    dve.wait_ge(keys_read, CG)
                    s.inc(nc.vector.tensor_copy(tile_i[:, :, 0:CB], tile_b[0:1, 0:NC].rearrange("p (b c) -> p b c", c=CB)))
                    k0 = keys[0:H, 0:2 * NC].rearrange("p (b c) -> p b c", c=2 * CB)
                    k1 = keys[0:H, 1:2 * NC + 1].rearrange("p (b c) -> p b c", c=2 * CB)
                    s.inc(nc.vector.tensor_tensor(diff[:, :, :], k0, k1, ALU.subtract))
                    k_end = keys[:, 0:2 * NC].rearrange("p (b c) -> p b c", c=2 * CB)[:, :, 0]
                    t_first = tile_b[:, 0:NC].rearrange("p (b c) -> p b c", c=CB)[:, :, 0]
                    s.inc(nc.vector.tensor_scalar(ends_k[:, :], k_end, 1.0 / BIG, None, ALU.mult))
                    s.wait(dve)
                    s.inc(nc.vector.scalar_tensor_tensor(flags_x[:, :, 1:2 * CB + 1], diff[:, :, :], -1.0, diff[:, :, :],
                                                         ALU.mult, ALU.min))
                    s.inc(nc.vector.scalar_tensor_tensor(ends_k[:, :], t_first, -float(P), ends_k[:, :], ALU.mult, ALU.add))
                    s.wait(dve)
                    s.inc(nc.vector.tensor_scalar(carry_row[:, :], ends_k[:, :], pidx[:, 0:1], None, ALU.is_equal))
                    dve.wait_ge(keys_in, 16 * H)
                    s.inc(nc.vector.tensor_tensor(flags[:, :, 1:P], key_t[:, :, 0:P - 1], key_t[:, :, 1:P], ALU.subtract))
                    s.wait(dve)

            with ExitStack() as pw:
                W = 2 * P
                STRIPS = -(-NT // 2)
                KB = HID // P
                xt = sb("xt", [P, 2, 2, W], ctx=pw)
                sq = sb("sq", [P, KB // 2, 2 * W], ctx=pw)
                sq_sum = sb("sq_sum", [P, W], ctx=pw)
                sd = sb("sd", [P, W], ctx=pw)
                rs = sb("rs", [P, W], ctx=pw)
                nrm = sb("nrm", [P, KB, W], ctx=pw)
                xn = sb("xn", [P, 2, KB, W], ctx=pw)
                feat = sb("feat", [P, 2, 2, RX], ctx=pw)
                x_loaded = [sem(f"x_loaded{p}", pw) for p in range(2)]
                h1_made = sem("h1_made", pw)
                sq_made = sem("sq_made", pw)
                sum_made = sem("sum_made", pw)
                var_made = sem("var_made", pw)
                sd_made = sem("sd_made", pw)
                rs_made = sem("rs_made", pw)
                nrm_made = sem("nrm_made", pw)
                xn_made = sem("xn_made", pw)
                feat_mm = sem("feat_mm", pw)
                feat_made = sem("feat_made", pw)
                feat_out = [sem(f"feat_out{p}", pw) for p in range(2)]
                block = pw.enter_context(nc.Block())
                h1 = bank[0:4]
                fp = bank[4:6]
                var = bank[6]
                B = KB // 2
                x_t = xT.rearrange("(k p) n -> p k n", p=P)

                def blocks(ap, w):
                    return ap.rearrange("p (two n) -> p two n", two=2)[:, :, 0:w]

                @block.sync
                def _(sp):
                    def load(s, p, w):
                        sp.dma_start(xt[:, p, :, 0:w], x_t[:, :, bass.ds(s * W, w)]).then_inc(x_loaded[p], 16)

                    def store(s, p, tiles):
                        sp.wait_ge(feat_made, 2 * s + tiles)
                        sp.dma_start(table[0][bass.ds(s * W, tiles * P), :].rearrange("(t p) w -> p t w", p=P),
                                     feat[:, p, 0:tiles, 0:ROW]).then_inc(feat_out[p], 16)

                    load(0, 0, W)
                    load(1, 1, W)
                    with sp.Fori(0, (STRIPS - 3) // 2) as j:
                        for p in range(2):
                            sp.wait_ge(h1_made, B * (2 * j + p + 1))
                            load(2 * j + p + 2, p, W)
                            store(2 * j + p, p, 2)
                    s = STRIPS - 3
                    sp.wait_ge(h1_made, B * (s + 1))
                    load(s + 2, 0, LAST)
                    store(s, 0, 2)
                    store(s + 1, 1, 2)
                    store(s + 2, 0, 1)
                    sp.wait_ge(feat_out[0], 16 * ((STRIPS + 1) // 2))
                    sp.wait_ge(feat_out[1], 16 * (STRIPS // 2))

                @block.tensor
                def _(pe):
                    def first(s, p, w, x_rounds):
                        pe.wait_ge(x_loaded[p], x_rounds)
                        for b in range(B):
                            if beyond(s, 1):
                                pe.wait_ge(nrm_made, B * (s - 1) + b + 1)
                            for half in range(2):
                                cols = slice((2 * b + half) * P, (2 * b + half + 1) * P)
                                o = h1[b][:, half * W:half * W + w]
                                for k in range(2):
                                    nc.tensor.matmul(o, w1t[:, k, cols], xt[:, p, k, 0:w], start=(k == 0), stop=False)
                                mm = nc.tensor.matmul(o, w3[:, cols], hot[:, bass.ds(s * W, w)], start=False, stop=True)
                            mm.then_inc(h1_made, 1)

                    def variance(s, w):
                        pe.wait_ge(sum_made, s + 1)
                        nc.tensor.matmul(var[:, 0:w], ones[:, :], sq_sum[:, 0:w], start=True, stop=True).then_inc(var_made, 1)

                    def second(s, p, t):
                        pe.wait_ge(xn_made, s + 1)
                        if beyond(s, 1):
                            pe.wait_ge(feat_made, 2 * (s - 1) + t + 1)
                        for k in range(KB):
                            mm = nc.tensor.matmul(fp[t][:, 0:RX], xn[:, p, k, t * P:(t + 1) * P], wc[:, k, :],
                                                  start=(k == 0), stop=(k == KB - 1))
                        mm.then_inc(feat_mm, 1)

                    def strip(s, p, w, x_rounds):
                        first(s, p, w, x_rounds)
                        if beyond(s, 1):
                            second(s - 1, 1 - p, 0)
                        variance(s, w)
                        if beyond(s, 1):
                            second(s - 1, 1 - p, 1)

                    strip(0, 0, W, 16)
                    strip(1, 1, W, 16)
                    with pe.Fori(1, (STRIPS - 1) // 2) as j:
                        strip(2 * j, 0, W, 16 * j + 16)
                        strip(2 * j + 1, 1, W, 16 * j + 16)
                    strip(STRIPS - 1, 0, LAST, 16 * (STRIPS // 2) + 16)
                    second(STRIPS - 1, 0, 0)

                @block.scalar
                def _(act):
                    def strip(s, p, w):
                        if beyond(s, 1):
                            act.wait_ge(sum_made, s)
                        for b in range(B):
                            act.wait_ge(h1_made, B * s + b + 1)
                            nc.scalar.activation(blocks(sq[:, b, :], w), blocks(h1[b][:, :], w), ACT.Square).then_inc(sq_made, 1)
                        act.wait_ge(var_made, s + 1)
                        nc.scalar.activation(sd[:, 0:w], var[:, 0:w], ACT.Sqrt, bias=epst[:, 0:1], scale=1.0 / HID
                                             ).then_inc(sd_made, 1)
                        if beyond(s, 2):
                            act.wait_ge(feat_mm, 2 * (s - 1))
                        for k in range(KB):
                            if k % 2 == 0:
                                act.wait_ge(nrm_made, B * s + k // 2 + 1)
                            a = nc.scalar.activation(xn[:, p, k, 0:w], nrm[:, k, 0:w], ACT.Relu, bias=b_col[:, k:k + 1],
                                                     scale=g_col[:, k:k + 1])
                        a.then_inc(xn_made, 1)

                    strip(0, 0, W)
                    strip(1, 1, W)
                    with act.Fori(1, (STRIPS - 1) // 2) as j:
                        strip(2 * j, 0, W)
                        strip(2 * j + 1, 1, W)
                    strip(STRIPS - 1, 0, LAST)

                @block.vector
                def _(dve):
                    def norm(s, w):
                        dve.wait_ge(sq_made, B * (s + 1))
                        if beyond(s, 1):
                            dve.wait_ge(var_made, s)
                        nc.vector.tensor_reduce(sq_sum[:, 0:w], sq[:, :, :].rearrange("p b (two n) -> p n (b two)", two=2)[:, 0:w, :],
                                                AX.X, ALU.add).then_inc(sum_made, 1)
                        dve.wait_ge(sd_made, s + 1)
                        nc.vector.reciprocal(rs[:, 0:w], sd[:, 0:w]).then_inc(rs_made, 1)
                        dve.wait_ge(rs_made, s + 1)
                        if beyond(s, 1):
                            dve.wait_ge(xn_made, s)
                        for b in range(B):
                            nc.vector.tensor_tensor(nrm[:, 2 * b:2 * b + 2, 0:w], blocks(h1[b][:, :], w),
                                                    rs[:, 0:w].unsqueeze(1).to_broadcast([P, 2, w]), ALU.mult).then_inc(nrm_made, 1)

                    def features(s, p, t, out_rounds):
                        dve.wait_ge(feat_mm, 2 * s + t + 1)
                        if out_rounds is not None:
                            dve.wait_ge(feat_out[p], out_rounds)
                        nc.vector.tensor_tensor(er[:, bass.ds(2 * s + t, 1), :].rearrange("p a h -> p (a h)"), fp[t][:, ROW:RX],
                                                bias_c[:, ROW:RX], ALU.add)
                        nc.vector.tensor_tensor(feat[:, p, t, :], fp[t][:, 0:RX], bias_c[:, :], ALU.add).then_inc(feat_made, 1)

                    def strip(s, p, w, out_rounds):
                        norm(s, w)
                        for t in range(2):
                            features(s - 1, 1 - p, t, out_rounds)

                    norm(0, W)
                    strip(1, 1, W, None)
                    strip(2, 0, W, None)
                    with dve.Fori(1, (STRIPS - 3) // 2) as j:
                        strip(2 * j + 1, 1, W, 16 * j)
                        strip(2 * j + 2, 0, W, 16 * j)
                    rounds = (STRIPS - 1) // 2
                    strip(STRIPS - 2, 1, W, 16 * (rounds - 1))
                    strip(STRIPS - 1, 0, LAST, 16 * (rounds - 1))
                    features(STRIPS - 1, 0, 0, 16 * rounds)

        for layer in range(2):
            attention(nc, layer, table[layer], bank, ident, ones, iota_f, pick_c, pick_h, pick_hT, src_idx, dst_loc,
                      flags, flags_x, tile_i, carry_row, er, acc)
            if layer == 0:
                next_features(nc, bank, ident, biasb[0], acc, er, wx2, table[1])
        finish(nc, x, biasb[1], acc, epst, out)


def attention(nc, layer, table, bank, ident, ones, iota_f, pick_c, pick_h, pick_hT, src_idx, dst_loc, flags, flags_x,
              tile_i, carry_row, er, acc):
    with ExitStack() as ctx:
        def sb(name, shape, dt=F32):
            return ctx.enter_context(nc.sbuf_tensor(f"{name}_{layer}", shape, dt))

        def sem(name):
            return ctx.enter_context(nc.semaphore(f"{name}_{layer}"))

        G = sb("gathered", [P, RING, CB, ROW])
        O = sb("onehots", [P, RING, CB, P])
        idx = sb("idx", [P, RING, CB], I32)
        fl = sb("flags_b", [HC, RING, P + 1], BF16)
        fx = sb("flags_xb", [H, RING, 2 * CB + 2])
        OT = sb("onehots_T", [P, 2, 4, P])
        fw = sb("fw", [HC, P])
        seg = sb("seg", [HC, P])
        fw2 = sb("fw2", [HC, P])
        seg2 = sb("seg2", [HC, P])
        spread = sb("spread", [HC, CB, 2])
        ends = sb("ends", [H, 2 * CB + 1])
        ends_f = sb("ends_f", [H, 2 * CB + 1])
        ends_m = sb("ends_m", [H, 2 * CB + 1])
        moved = sb("moved", [H, 2, H])
        back = sb("back", [HC, 2, CB])
        ends_c = sb("ends_c", [HC, 2])
        ref = sb("ref", [P, 2, H])
        ref_l = sb("ref_l", [P, 2, H])
        ref_d = sb("ref_d", [P, H])
        alpha = sb("alpha", [P, H])
        er_e = sb("er_e", [P, HC])
        z = sb("z", [P, 2, HC])
        zl = sb("zl", [P, 2, HC])
        zd = sb("zd", [P, HC])

        el_T = bank[0]
        small = bank[1]
        ends_ps = small[0:H, 0:2 * CB]
        back_ps = small[0:HC, 64:64 + 2 * CB]
        moved_ps = small[:, 128:128 + 2 * H]
        m_ps = small[:, 256:256 + HC]
        er_ps = bank[2][:, 0:HC]
        ot_ps = [bank[3], bank[4]]
        part = [bank[5], bank[6], bank[7]]

        gathered = [sem(f"gathered{u}") for u in range(RING)]
        idx_set = sem("idx_set")
        granted = sem("granted")
        flags_set = sem("flags_set")
        acc_zero = sem("acc_zero")
        el_turned = sem("el_turned")
        scan_step = sem("scan_step")
        spread_made = sem("spread_made")
        ends_made = sem("ends_made")
        ends_step = sem("ends_step")
        moved_made = sem("moved_made")
        back_made = sem("back_made")
        back_step = sem("back_step")
        seg_made = sem("seg_made")
        m_turned = sem("m_turned")
        ref_step = sem("ref_step")
        ref_made = sem("ref_made")
        alpha_made = sem("alpha_made")
        o_made = sem("o_made")
        o_turned = sem("o_turned")
        ot_made = sem("ot_made")
        er_mm = sem("er_mm")
        er_made = sem("er_made")
        z_step = sem("z_step")
        zd_made = sem("zd_made")
        ex_made = sem("ex_made")
        weighted = sem("weighted")
        part_made = sem("part_made")
        summed = sem("summed")
        scaled = sem("scaled")
        block = ctx.enter_context(nc.Block())
        CREDIT = RING * CB
        TG = 4
        NTG = -(-CB // TG)
        LOOPS = NB // RING - 1

        def el(u):
            return G[:, u, :, :].rearrange("p c (h w) -> p (c h) w", w=HW)[:, :, HD]

        def tiles(engine, b):
            return nc.values_load_multi_w_load_instructions(
                tile_i[0:1, bass.ds(b, 1), :].rearrange("p a c -> p (a c)"), engines=(engine,), min_val=0, max_val=NT - 1,
                skip_runtime_bounds_check_because="a count of at most NT - 1 tiles that start before the chunk")[1]

        def steps(eng, step, before, after):
            before()
            with eng.Fori(0, LOOPS) as i:
                for u in range(RING):
                    step(i * RING + u, u, i, True)
            for u in range(RING):
                step(LOOPS * RING + u, u, LOOPS, u < RING - 1)
            after()

        @block.gpsimd
        def _(pool):
            pool.sem_inc(summed, CREDIT)

            def gather(b, u):
                pool.wait_ge(idx_set, b + 1)
                for c in range(CB):
                    if c % MG == 0:
                        pool.wait_ge(summed, CB * b + c + MG)
                        pool.sem_inc(granted, 1)
                    pool.indirect_dma_start(G[:, u, c, :], None, table[:, :],
                                            bass.IndirectOffsetOnAxis(idx[:, u, c:c + 1], 0)).then_inc(gathered[u], 16)

            with pool.Fori(0, NB // RING) as i:
                for u in range(RING):
                    gather(i * RING + u, u)

        @block.tensor
        def _(pe):
            def segments(b, u, i):
                pe.wait_ge(gathered[u], 16 * CB * (i + 1))
                nc.tensor.transpose(el_T[0:HC, 0:P], el(u), ident[:, :]).then_inc(el_turned, 1)

            def ends_across(b):
                pe.wait_ge(spread_made, b + 1)
                nc.tensor.matmul(ends_ps, pick_h[:, :], spread[:, :, :].rearrange("p c two -> p (c two)"),
                                 start=True, stop=True).then_inc(ends_made, 1)

            def ends_back(b):
                pe.wait_ge(moved_made, b + 1)
                nc.tensor.matmul(back_ps, pick_hT[:, :], ends_m[:, 1:2 * CB + 1], start=True, stop=True)
                nc.tensor.matmul(moved_ps, ones[0:H, :], moved[:, :, :].rearrange("p a h -> p (a h)"),
                                 start=True, stop=True).then_inc(back_made, 1)

            def maxima(b):
                pe.wait_ge(seg_made, b + 1)
                nc.tensor.transpose(m_ps, seg2[:, :], ident[0:HC, 0:HC]).then_inc(m_turned, 1)

            def turn(b, u, g):
                pe.wait_ge(ot_made, NTG * b + max(g - 1, 0))
                for c in range(g * TG, min(g * TG + TG, CB)):
                    tr = nc.tensor.transpose(ot_ps[g % 2][:, (c % TG) * P:(c % TG + 1) * P], O[:, u, c, :], ident[:, :])
                tr.then_inc(o_turned, 1)

            def er_of_slots(b, t, g):
                pe.wait_ge(ot_made, NTG * b + g + 1)
                for c in range(g * TG, min(g * TG + TG, CB)):
                    mm = nc.tensor.matmul(er_ps[:, c * H:(c + 1) * H], OT[:, g % 2, c % TG, :],
                                          er[:, bass.ds(t[c], 1), :].rearrange("p a h -> p (a h)"), start=True, stop=True)
                mm.then_inc(er_mm, 1)

            def sums(b, u, c0, c1):
                for c in range(c0, c1):
                    pe.wait_ge(weighted, CB * b + c + 1)
                    pe.wait_ge(summed, CREDIT + CB * b + c - NPS + 1)
                    nc.tensor.matmul(part[c % NPS][:, 0:ROW], O[:, u, c, :], G[:, u, c, :],
                                     start=True, stop=True).then_inc(part_made, 1)

            def step(b, u, i, has_next):
                un, i_n = (u + 1) % RING, i + (u + 1) // RING
                if not has_next:
                    sums(b, u, 0, CB)
                    return
                t = tiles(ET.PE, b + 1)
                sums(b, u, 0, 4)
                for g in range(NTG + 1):
                    if g < NTG:
                        pe.wait_ge(o_made, 3 * (b + 1) + min(TG * g + TG - 1, CB - 1) // (CB // 3) + 1)
                        turn(b + 1, un, g)
                    if g:
                        er_of_slots(b + 1, t, g - 1)
                    sums(b, u, 4 + g, 5 + g)
                sums(b, u, 11, 12)
                segments(b + 1, un, i_n)
                sums(b, u, 12, 14)
                ends_across(b + 1)
                sums(b, u, 14, 17)
                ends_back(b + 1)
                sums(b, u, 17, 19)
                maxima(b + 1)
                sums(b, u, 19, CB)

            def before():
                t = tiles(ET.PE, 0)
                pe.wait_ge(o_made, 3)
                for g in range(NTG + 1):
                    if g < NTG:
                        turn(0, 0, g)
                    if g >= 1:
                        er_of_slots(0, t, g - 1)
                segments(0, 0, 0)
                ends_across(0)
                ends_back(0)
                maxima(0)

            pe.wait_ge(summed, CREDIT)
            steps(pe, step, before, lambda: None)

        @block.scalar
        def _(act):
            def indices(b, u, i):
                act.wait_ge(gathered[u], 16 * CB * i)
                nc.scalar.copy(fl[:, u, :], flags[:, bass.ds(b, 1), :].rearrange("p a e -> p (a e)"))
                nc.scalar.copy(fx[:, u, :], flags_x[:, bass.ds(b, 1), :].rearrange("p a c -> p (a c)")).then_inc(flags_set, 1)
                nc.scalar.copy(idx[:, u, :], src_idx[:, bass.ds(b * CB, CB)]).then_inc(idx_set, 1)

            def turned(b):
                for g in range(NTG):
                    act.wait_ge(o_turned, NTG * b + g + 1)
                    act.wait_ge(er_mm, NTG * b + max(g - 1, 0))
                    n = min(TG, CB - g * TG)
                    nc.scalar.copy(OT[:, g % 2, 0:n, :], ot_ps[g % 2][:, 0:n * P].rearrange("p (c e) -> p c e", e=P)).then_inc(ot_made, 1)
                act.wait_ge(er_mm, NTG * (b + 1))
                nc.scalar.copy(er_e[:, :], er_ps).then_inc(er_made, 1)

            def exps(b, u):
                act.wait_ge(ref_made, b + 1)
                nc.scalar.activation(alpha[:, :], ref_d[:, :], ACT.Exp, scale=carry_row[:, bass.ds(b, 1)]).then_inc(alpha_made, 1)
                act.wait_ge(zd_made, b + 1)
                nc.scalar.activation(el(u), zd[:, :], ACT.Exp).then_inc(ex_made, 1)

            def step(b, u, i, has_next):
                un, i_n = (u + 1) % RING, i + (u + 1) // RING
                if has_next:
                    turned(b + 1)
                    exps(b + 1, un)

            for u in range(RING):
                indices(u, u, 0)
            turned(0)
            exps(0, 0)
            with act.Fori(0, LOOPS) as i:
                for u in range(RING):
                    step(i * RING + u, u, i, True)
                    indices(i * RING + u + RING, u, i + 1)
            for u in range(RING):
                step(LOOPS * RING + u, u, LOOPS, u < RING - 1)

        @block.vector
        def _(dve):
            def one_hots(b, u, g):
                n = CB // 3
                nc.vector.tensor_tensor(O[:, u, g * n:(g + 1) * n, :], iota_f[:, :].unsqueeze(1).to_broadcast([P, n, P]),
                                        dst_loc[:, bass.ds(b * CB + g * n, n)].unsqueeze(2).to_broadcast([P, n, P]),
                                        ALU.is_equal).then_inc(o_made, 1)

            def chunk_forward(b, u):
                dve.wait_ge(flags_set, b + 1)
                dve.wait_ge(el_turned, b + 1)
                nc.vector.tensor_tensor_scan(fw[:, :], fl[:, u, 0:P], el_T[0:HC, 0:P], -BIG, ALU.add, ALU.max).then_inc(scan_step, 1)

            def chunk_backward(b, u):
                dve.wait_ge(scan_step, 2 * b + 1)
                nc.vector.tensor_tensor_scan(seg[:, :][:, ::-1], fl[:, u, 1:P + 1][:, ::-1], fw[:, :][:, ::-1], -BIG,
                                             ALU.add, ALU.max).then_inc(scan_step, 1)

            def spread_ends(b):
                dve.wait_ge(scan_step, 2 * b + 2)
                nc.vector.tensor_tensor(spread[:, :, :], pick_c[:, :].unsqueeze(2).to_broadcast([HC, CB, 2]),
                                        seg[:, 0:P:P - 1].unsqueeze(1).to_broadcast([HC, CB, 2]), ALU.mult).then_inc(spread_made, 1)

            def ends_in(b):
                nc.vector.tensor_copy(ends[:, 0:1], ends_m[:, 2 * CB:2 * CB + 1])
                dve.wait_ge(ends_made, b + 1)
                nc.vector.tensor_copy(ends[:, 1:2 * CB + 1], ends_ps).then_inc(ends_step, 1)

            def ends_forward(b, u):
                dve.wait_ge(ends_step, 3 * b + 1)
                nc.vector.tensor_tensor_scan(ends_f[:, :], fx[:, u, 0:2 * CB + 1], ends[:, :], -BIG, ALU.add, ALU.max).then_inc(ends_step, 1)

            def ends_backward(b, u):
                dve.wait_ge(ends_step, 3 * b + 2)
                nc.vector.tensor_tensor_scan(ends_m[:, :][:, ::-1], fx[:, u, 1:2 * CB + 2][:, ::-1], ends_f[:, :][:, ::-1], -BIG,
                                             ALU.add, ALU.max).then_inc(ends_step, 1)

            def moved_maxima(b):
                dve.wait_ge(ends_step, 3 * b + 3)
                nc.vector.tensor_scalar(moved[:, 0, :], ident[0:H, 0:H], ends[:, 0:1], None, ALU.mult)
                nc.vector.tensor_scalar(moved[:, 1, :], ident[0:H, 0:H], ends_m[:, 0:1], None, ALU.mult).then_inc(moved_made, 1)

            def own_ends(b, t0):
                dve.wait_ge(back_made, b + 1)
                nc.vector.tensor_tensor(back[:, :, :], back_ps.rearrange("p (c two) -> p two c", two=2),
                                        pick_c[:, :].unsqueeze(1).to_broadcast([HC, 2, CB]), ALU.mult).then_inc(back_step, 1)
                nc.vector.tensor_tensor(ref[:, :, :], moved_ps.rearrange("p (a h) -> p a h", a=2),
                                        er[:, bass.ds(t0, 1), :].to_broadcast([P, 2, H]), ALU.add).then_inc(ref_step, 1)

            def own_ends_sum(b):
                dve.wait_ge(back_step, 3 * b + 1)
                nc.vector.tensor_reduce(ends_c[:, :], back[:, :, :], AX.X, ALU.add).then_inc(back_step, 1)
                dve.wait_ge(ref_step, 2 * b + 1)
                nc.vector.scalar_tensor_tensor(ref_l[:, :, :], ref[:, :, :], NEG, ref[:, :, :], ALU.mult, ALU.max).then_inc(ref_step, 1)

            def join_forward(b, u):
                dve.wait_ge(back_step, 3 * b + 2)
                nc.vector.tensor_tensor_scan(fw2[:, :], fl[:, u, 0:P], seg[:, :], ends_c[:, 0:1], ALU.add, ALU.max).then_inc(back_step, 1)
                dve.wait_ge(ref_step, 2 * b + 2)
                nc.vector.tensor_tensor(ref_d[:, :], ref_l[:, 0, :], ref_l[:, 1, :], ALU.subtract).then_inc(ref_made, 1)

            def join_backward(b, u):
                dve.wait_ge(back_step, 3 * b + 3)
                nc.vector.tensor_tensor_scan(seg2[:, :][:, ::-1], fl[:, u, 1:P + 1][:, ::-1], fw2[:, :][:, ::-1], ends_c[:, 1:2],
                                             ALU.add, ALU.max).then_inc(seg_made, 1)

            def scores(b, u):
                dve.wait_ge(er_made, b + 1)
                nc.vector.tensor_tensor(z[:, 0, :], el(u), er_e[:, :], ALU.add).then_inc(z_step, 1)
                dve.wait_ge(m_turned, b + 1)
                nc.vector.tensor_tensor(z[:, 1, :], m_ps, er_e[:, :], ALU.add).then_inc(z_step, 1)

            def leaky(b):
                dve.wait_ge(z_step, 3 * b + 2)
                nc.vector.scalar_tensor_tensor(zl[:, :, :], z[:, :, :], NEG, z[:, :, :], ALU.mult, ALU.max).then_inc(z_step, 1)

            def below_maximum(b):
                dve.wait_ge(z_step, 3 * b + 3)
                nc.vector.tensor_tensor(zd[:, :], zl[:, 0, :], zl[:, 1, :], ALU.subtract).then_inc(zd_made, 1)

            def rescale(b, t0):
                dve.wait_ge(alpha_made, b + 1)
                dve.wait_ge(summed, CREDIT + CB * b)
                a = acc[:, bass.ds(t0, 1), :].rearrange("p a (h w) -> p (a h) w", w=HW)
                nc.vector.tensor_tensor(a, a, alpha[:, :].unsqueeze(2).to_broadcast([P, H, HW]), ALU.mult).then_inc(scaled, 1)

            def weight(b, u, c0, c1):
                for c in range(c0, c1):
                    rows = G[:, u, c, :].rearrange("p (h w) -> p h w", w=HW)
                    nc.vector.tensor_tensor(rows[:, :, 0:HD], rows[:, :, 0:HD], rows[:, :, HD:HW].to_broadcast([P, H, HD]),
                                            ALU.mult).then_inc(weighted, 1)

            def add(b, t, c):
                dve.wait_ge(part_made, CB * b + c + 1)
                if c:
                    dve.wait_ge(summed, CREDIT + CB * b + c)
                else:
                    dve.wait_ge(scaled, b + 1)
                a = acc[:, bass.ds(t[c], 1), :].rearrange("p a w -> p (a w)")
                nc.vector.tensor_tensor(a, a, part[c % NPS][:, 0:ROW], ALU.add).then_inc(summed, 1)

            def step(b, u, i, has_next):
                un = (u + 1) % RING
                t = tiles(ET.DVE, b)
                dve.wait_ge(ex_made, b + 1)
                weight(b, u, 0, 4)
                rescale(b, t[0])
                done = 4
                for c in range(9):
                    if has_next and c < 3:
                        one_hots(b + 1, un, c)
                    add(b, t, c)
                    more = 1 if c < 2 else 2 if c < 7 else 3
                    weight(b, u, done, min(done + more, CB))
                    done = min(done + more, CB)
                if not has_next:
                    for c in range(9, CB):
                        add(b, t, c)
                    return
                t_next = nc.values_load_multi_w_load_instructions(
                    tile_i[0:1, bass.ds(b + 1, 1), 0:1].rearrange("p a c -> p (a c)"), engines=(ET.DVE,), min_val=0,
                    max_val=NT - 1, skip_runtime_bounds_check_because="as in tiles")[1]
                chunk_forward(b + 1, un)
                add(b, t, 9)
                chunk_backward(b + 1, un)
                add(b, t, 10)
                spread_ends(b + 1)
                add(b, t, 11)
                ends_in(b + 1)
                add(b, t, 12)
                ends_forward(b + 1, un)
                add(b, t, 13)
                ends_backward(b + 1, un)
                add(b, t, 14)
                moved_maxima(b + 1)
                add(b, t, 15)
                own_ends(b + 1, t_next[0])
                add(b, t, 16)
                own_ends_sum(b + 1)
                add(b, t, 17)
                join_forward(b + 1, un)
                join_backward(b + 1, un)
                add(b, t, 18)
                scores(b + 1, un)
                add(b, t, 19)
                leaky(b + 1)
                below_maximum(b + 1)
                add(b, t, 20)

            def before():
                nc.vector.memset(acc[:, :, :], 0.0).then_inc(acc_zero, 1)
                nc.vector.memset(ends_m[:, :], -BIG).then_inc(acc_zero, 1)
                for g in range(3):
                    one_hots(0, 0, g)
                dve.wait_ge(acc_zero, 2)
                t0 = nc.values_load_multi_w_load_instructions(
                    tile_i[0:1, 0, 0:1], engines=(ET.DVE,), min_val=0, max_val=NT - 1,
                    skip_runtime_bounds_check_because="as in tiles")[1]
                chunk_forward(0, 0)
                chunk_backward(0, 0)
                spread_ends(0)
                ends_in(0)
                ends_forward(0, 0)
                ends_backward(0, 0)
                moved_maxima(0)
                own_ends(0, t0[0])
                own_ends_sum(0)
                join_forward(0, 0)
                join_backward(0, 0)
                scores(0, 0)
                leaky(0)
                below_maximum(0)
                dve.wait_ge(summed, CREDIT)

            steps(dve, step, before, lambda: None)


def node_reciprocals(acc, rden, step, dve):
    den = acc[:, :, :].rearrange("p t (h w) -> p (t h) w", w=HW)[:, :, HD]
    flat = rden[:, :, :].rearrange("p t h -> p (t h)")
    nc_op = dve.tensor_scalar(flat, den, DEN_MIN, None, ALU.max)
    nc_op.then_inc(step, 1)
    dve.wait_ge(step, 1)
    dve.reciprocal(flat, flat).then_inc(step, 1)
    dve.wait_ge(step, 2)


def next_features(nc, bank, ident, bias, acc, er, wx2, table):
    RN = 4
    ROUNDS = NT // RN
    with ExitStack() as ctx:
        def sb(name, shape, dt=F32):
            return ctx.enter_context(nc.sbuf_tensor(name, shape, dt))

        def sem(name):
            return ctx.enter_context(nc.semaphore(name))

        rden = sb("nf_rden", [P, NT, H])
        hid = sb("nf_hid", [P, RN, D])
        hid_T = sb("nf_hid_T", [P, RN, 2, P])
        feat = sb("nf_feat", [P, RN, RX])
        d_step = sem("nf_d_step")
        h_scaled = sem("nf_h_scaled")
        h_made = sem("nf_h_made")
        turned = sem("nf_turned")
        hT_made = sem("nf_hT_made")
        mm_made = sem("nf_mm_made")
        f_made = sem("nf_f_made")
        f_out = [sem(f"nf_f_out{u}") for u in range(RN)]
        block = ctx.enter_context(nc.Block())

        def rounds(eng, ahead, behind):
            ahead(0, 0, 0)
            for u in range(RN):
                ahead(u + 1, (u + 1) % RN, (u + 1) // RN)
                behind(u, u, 0)
            with eng.Fori(1, ROUNDS) as j:
                for u in range(RN):
                    ahead(RN * j + u + 1, (u + 1) % RN, j + (u + 1) // RN)
                    behind(RN * j + u, u, j)
            behind(NT - 1, 0, ROUNDS)

        assert NT == RN * ROUNDS + 1

        @block.vector
        def _(dve):
            node_reciprocals(acc, rden, d_step, nc.vector)

            def scale(i, u, j):
                if beyond(j, 1):
                    dve.wait_ge(turned, i - RN + 1)
                a = acc[:, bass.ds(i, 1), :].rearrange("p a (h w) -> p (a h) w", w=HW)
                nc.vector.tensor_tensor(hid[:, u, :].rearrange("p (h d) -> p h d", d=HD), a[:, :, 0:HD],
                                        rden[:, bass.ds(i, 1), :].rearrange("p a h -> p (a h)").unsqueeze(2)
                                        .to_broadcast([P, H, HD]), ALU.mult).then_inc(h_scaled, 1)

            def add_bias(i, u, j):
                dve.wait_ge(h_scaled, i + 1)
                nc.vector.tensor_tensor(hid[:, u, :], hid[:, u, :], bias[:, :], ALU.add).then_inc(h_made, 1)

            rounds(dve, scale, add_bias)

        @block.tensor
        def _(pe):
            def turn(i, u, j):
                pe.wait_ge(h_made, i + 1)
                if beyond(i, 2):
                    pe.wait_ge(hT_made, i - 1)
                for k in range(2):
                    tr = nc.tensor.transpose(bank[u % 2][:, k * P:(k + 1) * P], hid[:, u, k * P:(k + 1) * P], ident[:, :])
                tr.then_inc(turned, 1)

            def product(i, u, j):
                pe.wait_ge(hT_made, i + 1)
                if beyond(i, 2):
                    pe.wait_ge(f_made, i - 1)
                for k in range(2):
                    mm = nc.tensor.matmul(bank[2 + u % 2][:, 0:RX], hid_T[:, u, k, :], wx2[:, k, :], start=(k == 0), stop=(k == 1))
                mm.then_inc(mm_made, 1)

            rounds(pe, turn, product)

        @block.scalar
        def _(act):
            def rectify(i, u, j):
                act.wait_ge(turned, i + 1)
                if beyond(j, 1):
                    act.wait_ge(mm_made, i - RN + 1)
                nc.scalar.activation(hid_T[:, u, :, :], bank[u % 2][:, 0:2 * P].rearrange("p (k n) -> p k n", k=2),
                                     ACT.Relu).then_inc(hT_made, 1)

            def copy_out(i, u, j):
                act.wait_ge(mm_made, i + 1)
                if beyond(j, 1):
                    act.wait_ge(f_out[u], 16 * j)
                nc.scalar.copy(er[:, bass.ds(i, 1), :].rearrange("p a h -> p (a h)"), bank[2 + u % 2][:, ROW:RX])
                nc.scalar.copy(feat[:, u, :], bank[2 + u % 2][:, 0:RX]).then_inc(f_made, 1)

            rounds(act, rectify, copy_out)

        @block.sync
        def _(sp):
            def store(i, u):
                sp.wait_ge(f_made, i + 1)
                sp.dma_start(table[bass.ds(i * P, P), :], feat[:, u, 0:ROW]).then_inc(f_out[u], 16)

            with sp.Fori(0, ROUNDS) as j:
                for u in range(RN):
                    store(RN * j + u, u)
            store(NT - 1, 0)
            for u in range(RN):
                sp.wait_ge(f_out[u], 16 * (ROUNDS + (u == 0)))


def finish(nc, x, bias, acc, epst, out):
    GT = 7
    GROUPS = NT // GT
    ROUNDS = GROUPS // 2
    assert NT == GT * GROUPS and GROUPS == 2 * ROUNDS + 1
    with ExitStack() as ctx:
        def sb(name, shape, dt=F32):
            return ctx.enter_context(nc.sbuf_tensor(name, shape, dt))

        def sem(name):
            return ctx.enter_context(nc.semaphore(name))

        xs = sb("fi_x", [P, 2, GT, D])
        rden = sb("fi_rden", [P, NT, H])
        y = sb("fi_y", [P, 2, GT, D])
        res = sb("fi_res", [P, 2, GT, D])
        stats = sb("fi_stats", [P, 2, GT, 6])
        mv = sb("fi_mv", [P, 2, GT, 2])
        sd = sb("fi_sd", [P, 2, GT])
        rs = sb("fi_rs", [P, 2, 2, GT])
        x_in = [sem(f"fi_x_in{p}") for p in range(2)]
        d_step = sem("fi_d_step")
        y_step = sem("fi_y_step")
        x_used = sem("fi_x_used")
        stats_made = sem("fi_stats_made")
        stats_seen = sem("fi_stats_seen")
        mv_made = sem("fi_mv_made")
        sd_made = sem("fi_sd_made")
        rs_step = sem("fi_rs_step")
        rs_made = sem("fi_rs_made")
        r_made = sem("fi_r_made")
        r_out = [sem(f"fi_r_out{p}") for p in range(2)]
        block = ctx.enter_context(nc.Block())
        GP = GT * P

        @block.sync
        def _(sp):
            def load(g, p):
                sp.dma_start(xs[:, p, :, :], x[bass.ds(g * GP, GP), :].rearrange("(t p) d -> p t d", p=P)).then_inc(x_in[p], 16)

            def store(g, p):
                for t in range(GT):
                    sp.wait_ge(r_made, g * GT + t + 1)
                    sp.dma_start(out[bass.ds(g * GP + t * P, P), :], res[:, p, t, :]).then_inc(r_out[p], 16)

            load(0, 0)
            load(1, 1)
            with sp.Fori(0, ROUNDS - 1) as j:
                for p in range(2):
                    sp.wait_ge(x_used, 2 * j + p + 1)
                    load(2 * j + p + 2, p)
                    store(2 * j + p, p)
            sp.wait_ge(x_used, GROUPS - 2)
            sp.dma_start(xs[:, 0, 0:GT - 1, :], x[(GROUPS - 1) * GP:(NT - 1) * P, :].rearrange("(t p) d -> p t d", p=P)
                         ).then_inc(x_in[0], 16)
            sp.dma_start(xs[0:LAST, 0, GT - 1, :], x[(NT - 1) * P:N, :]).then_inc(x_in[0], 16)
            store(GROUPS - 3, 0)
            store(GROUPS - 2, 1)
            for t in range(GT):
                sp.wait_ge(r_made, NT - GT + t + 1)
                n = P if t < GT - 1 else LAST
                r = (NT - GT + t) * P
                sp.dma_start(out[r:r + n, :], res[0:n, 0, t, :]).then_inc(r_out[0], 16)
            sp.wait_ge(r_out[0], 16 * GT * (ROUNDS + 1))
            sp.wait_ge(r_out[1], 16 * GT * ROUNDS)

        @block.vector
        def _(dve):
            node_reciprocals(acc, rden, d_step, nc.vector)

            def scale(g, p, again):
                if again:
                    dve.wait_ge(r_made, GT * (g - 1))
                a = acc[:, bass.ds(g * GT, GT), :].rearrange("p t (h w) -> p (t h) w", w=HW)
                r = rden[:, bass.ds(g * GT, GT), :].rearrange("p t h -> p (t h)")
                nc.vector.tensor_tensor(y[:, p, :, :].rearrange("p t (h d) -> p (t h) d", d=HD), a[:, :, 0:HD],
                                        r.unsqueeze(2).to_broadcast([P, GT * H, HD]), ALU.mult).then_inc(y_step, 1)

            def inverse_deviation(g, p):
                dve.wait_ge(sd_made, g + 1)
                nc.vector.reciprocal(rs[:, p, 0, :], sd[:, p, :]).then_inc(rs_step, 1)

            def mean_shift(g, p):
                dve.wait_ge(rs_step, g + 1)
                nc.vector.scalar_tensor_tensor(rs[:, p, 1, :], mv[:, p, :, 0], -1.0, rs[:, p, 0, :], ALU.mult,
                                               ALU.mult).then_inc(rs_made, 1)

            def residual(g, p, x_rounds, before):
                dve.wait_ge(y_step, 2 * g + 1)
                nc.vector.tensor_tensor(y[:, p, :, :], y[:, p, :, :], bias[:, :].unsqueeze(1).to_broadcast([P, GT, D]),
                                        ALU.add).then_inc(y_step, 1)
                if before:
                    mean_shift(g - 1, 1 - p)
                dve.wait_ge(y_step, 2 * g + 2)
                dve.wait_ge(x_in[p], x_rounds)
                nc.vector.scalar_tensor_tensor(y[:, p, :, :], y[:, p, :, :], 0.0, xs[:, p, :, :], ALU.max,
                                               ALU.add).then_inc(x_used, 1)
                dve.wait_ge(x_used, g + 1)
                for t in range(GT):
                    nc.vector.bn_stats(stats[:, p, t, :], y[:, p, t, :]).then_inc(stats_made, 1)
                for t in range(GT):
                    dve.wait_ge(stats_made, GT * g + t + 1)
                    dve.sem_inc(stats_seen, 1)
                    nc.vector.bn_aggr(mv[:, p, t, :], stats[:, p, t, :]).then_inc(mv_made, 1)

            def group(g, p, j, x_rounds, before, again):
                scale(g, p, again)
                if before:
                    inverse_deviation(g - 1, 1 - p)
                residual(g, p, x_rounds, before)

            group(0, 0, 0, 16, False, False)
            group(1, 1, 0, 16, True, False)
            with dve.Fori(1, ROUNDS) as j:
                group(2 * j, 0, j, 16 * j + 16, True, True)
                group(2 * j + 1, 1, j, 16 * j + 16, True, True)
            group(GROUPS - 1, 0, ROUNDS, 16 * ROUNDS + 32, True, True)
            inverse_deviation(GROUPS - 1, 0)
            mean_shift(GROUPS - 1, 0)

        @block.scalar
        def _(act):
            def deviation(g, p):
                act.wait_ge(mv_made, GT * (g + 1))
                nc.scalar.activation(sd[:, p, :], mv[:, p, :, 1], ACT.Sqrt, bias=epst[:, 0:1]).then_inc(sd_made, 1)

            def norm(g, p, j_out):
                act.wait_ge(rs_made, g + 1)
                if j_out is not None:
                    act.wait_ge(r_out[p], j_out)
                for t in range(GT):
                    nc.scalar.activation(res[:, p, t, :], y[:, p, t, :], ACT.Identity, bias=rs[:, p, 1, t:t + 1],
                                         scale=rs[:, p, 0, t:t + 1]).then_inc(r_made, 1)

            deviation(0, 0)
            norm(0, 0, None)
            deviation(1, 1)
            norm(1, 1, None)
            with act.Fori(1, ROUNDS) as j:
                for p in range(2):
                    deviation(2 * j + p, p)
                    norm(2 * j + p, p, 16 * GT * j)
            deviation(GROUPS - 1, 0)
            norm(GROUPS - 1, 0, 16 * GT * ROUNDS)


def kernel(x, src, dst, node_type_24, L0_gnn_emb, L0_gnn_le_W1, L0_gnn_le_b1, L0_gnn_ln_g, L0_gnn_ln_b, L0_gnn_le_W2,
           L0_gnn_le_b2, L0_gnn_W1, L0_gnn_al1, L0_gnn_ar1, L0_gnn_b1, L0_gnn_W2, L0_gnn_al2, L0_gnn_ar2, L0_gnn_b2):
    import numpy as np
    import concourse.bacc as bacc
    from concourse.bass_utils import run_bass_kernel_spmd

    nc = bacc.Bacc("TRN2", target_bir_lowering=False, num_devices=1)
    arrays = {}

    def given(name, a):
        arrays[name] = np.ascontiguousarray(a)
        return nc.dram_tensor(name, arrays[name].shape, mybir.dt.from_np(arrays[name].dtype), kind="ExternalInput").ap()

    t = np.transpose
    out = nc.dram_tensor("out", (N, D), F32, kind="ExternalOutput").ap()
    gnn_kernel(
        nc, given("x", x), given("xT", t(np.asarray(x))), given("src", src), given("dst", dst), given("labels", node_type_24),
        given("embT", t(np.asarray(L0_gnn_emb))), given("leW1T", t(np.asarray(L0_gnn_le_W1))), given("le_b1", L0_gnn_le_b1),
        given("ln_g", L0_gnn_ln_g), given("ln_b", L0_gnn_ln_b), given("leW2", L0_gnn_le_W2), given("le_b2", L0_gnn_le_b2),
        [given("W1", L0_gnn_W1), given("W2", L0_gnn_W2)],
        [given("W1T", t(np.asarray(L0_gnn_W1))), given("W2T", t(np.asarray(L0_gnn_W2)))],
        [given("al1", L0_gnn_al1), given("al2", L0_gnn_al2)], [given("ar1", L0_gnn_ar1), given("ar2", L0_gnn_ar2)],
        [given("b1", L0_gnn_b1), given("b2", L0_gnn_b2)], out)
    r = run_bass_kernel_spmd(nc, [arrays], core_ids=[0])
    return r.results[0]["out"]
```

```python
from contextlib import ExitStack

import concourse.bass as bass
from concourse import mybir

F32 = mybir.dt.float32
I32 = mybir.dt.int32
BF16 = mybir.dt.bfloat16
ALU = mybir.AluOpType
ACT = mybir.ActivationFunctionType
AX = mybir.AxisListType
ET = mybir.EngineType

P = 128
N = 6250
D = 256
H = 4
HD = D // H
HW = HD + 1
ROW = H * HW
RX = ROW + H
E = 106250
HID = 4 * D
LABELS = 24
NT = -(-N // P)
LAST = N - (NT - 1) * P
CB = 21
RING = 3
CHUNKS = (E + NT * (P - 1)) // P
NB = -(-CHUNKS // (CB * RING)) * RING
NC = NB * CB
CB_LAST = CHUNKS - (NB - 1) * CB
CG = -(-NC // P)
HC = H * CB
PARTS = 3
PR = 32
K3 = PARTS * PR
TW = 24
MG = 3
NPS = 3
NT_A = 37
ROWS_E = 125
COLS_E = E // ROWS_E
BIG = 2.0 ** 100
PAD_DST = 8191
NEG = 0.2
LN_EPS = 1e-5
DEN_MIN = 1e-9


class Counter:

    def __init__(self, sem):
        self.sem, self.n = sem, 0

    def inc(self, ins, by=1):
        ins.then_inc(self.sem, by)
        self.n += by
        return self.n

    def wait(self, eng, n=None):
        eng.wait_ge(self.sem, self.n if n is None else n)


def beyond(i, n):
    return not isinstance(i, int) or i >= n


def gnn_kernel(nc, x, xT, src, dst, labels, embT, leW1T, le_b1, ln_g, ln_b, leW2, le_b2,
               gW, gWT, gal, gar, gb, out):
    assert ROWS_E * COLS_E == E
    table = [nc.dram_tensor(f"table{l}", (NT * P, ROW), F32, kind="Internal").ap() for l in range(2)]
    src_s = nc.dram_tensor("src_sorted", (E + P, 1), I32, kind="Internal").ap()
    dst_s = nc.dram_tensor("dst_sorted", (E + P, 1), I32, kind="Internal").ap()
    loc_d = nc.dram_tensor("slot_locs", (CG * P, P), BF16, kind="Internal").ap()
    key_d = nc.dram_tensor("slot_keys", (CG * P, P), F32, kind="Internal").ap()

    with ExitStack() as top:
        def sb(name, shape, dt=F32, ctx=top):
            return ctx.enter_context(nc.sbuf_tensor(name, shape, dt))

        def sem(name, ctx=top):
            return ctx.enter_context(nc.semaphore(name))

        bank = [top.enter_context(nc.psum_tensor(f"bank{i}", [P, 512], F32)) for i in range(8)]

        ident = sb("ident", [P, P])
        ones = sb("ones", [P, P])
        iota_f = sb("iota_f", [P, P])
        pidx = sb("pidx", [P, 1])
        epst = sb("epst", [P, 1])
        pick_c = sb("pick_c", [HC, CB])
        pick_h = sb("pick_h", [HC, H])
        pick_hT = sb("pick_hT", [H, HC])
        src_idx = sb("src_idx", [P, CG * P], I32)
        dst_loc = sb("dst_loc", [P, CG * P])
        loc_t = sb("loc_t", [P, NB, P], BF16)
        ident_b = sb("ident_b", [P, P], BF16)
        flags = sb("flags", [HC, NB, P + 1], BF16)
        flags_x = sb("flags_x", [H, NB, 2 * CB + 2])
        tile_i = sb("tile_i", [1, NB, TW], I32)
        n_chunks = sb("n_chunks", [1, 1], I32)
        carry_row = sb("carry_row", [P, NB])
        er = sb("er", [P, NT, H])
        wx2 = sb("wx2", [P, 2, RX])
        biasb = [sb(f"bias{l}", [P, D]) for l in range(2)]

        with ExitStack() as ph:
            w1t = sb("w1t", [P, 4, HID], ctx=ph)
            w3 = sb("w3", [K3, HID], BF16, ctx=ph)
            hot = sb("hot", [K3, N], BF16, ctx=ph)
            wc = sb("wc", [P, HID // P, RX], ctx=ph)
            bias_c = sb("bias_c", [P, RX], ctx=ph)
            dst_i = sb("dst_i", [ROWS_E, COLS_E], I32, ctx=ph)
            src_i = sb("src_i", [ROWS_E, COLS_E], I32, ctx=ph)
            dst_f = sb("dst_f", [ROWS_E, COLS_E], ctx=ph)
            cnt = sb("cnt", [ROWS_E, NT + 2], ctx=ph)
            g_col = sb("g_col", [P, HID // P], ctx=ph)
            b_col = sb("b_col", [P, HID // P], ctx=ph)

            with ExitStack() as pw:
                w2n = sb("w2n", [P, 2, HID], ctx=pw)
                wx1 = sb("wx1", [P, 2, RX], ctx=pw)
                wn = [sb(f"wn{l}", [P, 2, D], ctx=pw) for l in range(2)]
                wt = [sb(f"wt{l}", [P, 2, D], ctx=pw) for l in range(2)]
                alr = [sb(f"alr{l}", [P, 2, 2 * H], ctx=pw) for l in range(2)]
                emb_t = sb("emb_t", [P, 2, LABELS], ctx=pw)
                emb_r = sb("emb_r", [P, 2, PARTS, PR], ctx=pw)
                lab = sb("lab", [K3, N], I32, ctx=pw)
                row_i = sb("row_i", [P, 1], I32, ctx=pw)
                row_f = sb("row_f", [P, 1], ctx=pw)
                w_sum = sb("w_sum", [P, 2], ctx=pw)
                w_mean = sb("w_mean", [P, 2], ctx=pw)
                w3_f = sb("w3_f", [K3, HID], ctx=pw)
                b1_rows = sb("b1_rows", [K3, HID], ctx=pw)
                w3_sum = sb("w3_sum", [K3, 1], ctx=pw)
                w3_mean = sb("w3_mean", [K3, 1], ctx=pw)
                w3_p = sb("w3_p", [K3, PARTS, HID], BF16, ctx=pw)
                counted = sem("counted", pw)
                side = sb("side", [ROWS_E, 2, COLS_E], BF16, ctx=pw)
                fall = sb("fall", [ROWS_E, 2, COLS_E], BF16, ctx=pw)
                fall_made = sem("fall_made", pw)
                row_next = sb("row_next", [ROWS_E, 1], I32, ctx=pw)
                thr = sb("thr", [P, NT], ctx=pw)
                pad = sb("pad", [1, 2 * P], I32, ctx=pw)
                e_loaded = sem("e_loaded", pw)
                e_copied = sem("e_copied", pw)
                thr_set = sem("thr_set", pw)
                dst_cast = sem("dst_cast", pw)
                lab_loaded = sem("lab_loaded", pw)
                emb_made = sem("emb_made", pw)
                centre = Counter(sem("centre", pw))
                b2col = sb("b2col", [P, 2], ctx=pw)
                iota_i = sb("iota_i", [P, P], I32, ctx=pw)
                pidx_i = sb("pidx_i", [P, 1], I32, ctx=pw)
                masks_set = sem("masks_set", pw)
                iotas_made = sem("iotas_made", pw)
                alr_zero = sem("alr_zero", pw)
                w_loaded = sem("w_loaded", pw)
                a_loaded = sem("a_loaded", pw)
                elw_made = sem("elw_made", pw)
                wx_made = sem("wx_made", pw)
                w3_made = sem("w3_made", pw)
                w3_read = sem("w3_read", pw)
                wc_made = sem("wc_made", pw)
                wc_read = sem("wc_read", pw)
                block = pw.enter_context(nc.Block())
                wx = [wx1, wx2]
                N_W = 13

                @block.sync
                def _(sp):
                    sp.dma_start(dst_i[:, :], dst.rearrange("(p n) -> p n", p=ROWS_E)).then_inc(e_loaded, 16)
                    with nc.allow_non_contiguous_dma(reason="the first destination of each row"):
                        sp.dma_start(row_next[0:ROWS_E - 1, :], dst.rearrange("(p n) -> p n", p=ROWS_E)[1:ROWS_E, 0:1]
                                     ).then_inc(e_loaded, 16)
                    sp.dma_start(w1t[:, :, :], leW1T.rearrange("(k p) n -> p k n", p=P)).then_inc(w_loaded, 16)
                    sp.dma_start(w2n[:, :, :], leW2.rearrange("(k p) n -> p k n", p=P)).then_inc(w_loaded, 16)
                    sp.dma_start(emb_t[:, :, :], embT.rearrange("(k p) n -> p k n", p=P)).then_inc(w_loaded, 16)
                    for l in range(2):
                        sp.dma_start(wn[l][:, :, :], gW[l].rearrange("(k p) n -> p k n", p=P)).then_inc(w_loaded, 16)
                        sp.dma_start(wt[l][:, :, :], gWT[l].rearrange("(k p) n -> p k n", p=P)).then_inc(w_loaded, 16)
                        sp.dma_start(biasb[l][:, :], gb[l].rearrange("(a n) -> a n", a=1).broadcast_to([P, D])
                                     ).then_inc(w_loaded, 16)
                    with nc.allow_non_contiguous_dma(reason="vectors of a few hundred features, one to a partition"):
                        sp.dma_start(b2col[:, :], le_b2.rearrange("(k p) -> p k", p=P)).then_inc(w_loaded, 16)
                        sp.dma_start(g_col[:, :], ln_g.rearrange("(k p) -> p k", p=P)).then_inc(w_loaded, 16)
                        sp.dma_start(b_col[:, :], ln_b.rearrange("(k p) -> p k", p=P)).then_inc(w_loaded, 16)
                    sp.dma_start(b1_rows[:, :], le_b1.rearrange("(a n) -> a n", a=1).broadcast_to([K3, HID])).then_inc(w_loaded, 16)
                    sp.dma_start(lab[:, :], labels.rearrange("(a n) -> a n", a=1).broadcast_to([K3, N])).then_inc(lab_loaded, 16)
                    sp.dma_start(src_i[:, :], src.rearrange("(p n) -> p n", p=ROWS_E)).then_inc(e_copied, 16)
                    sp.dma_start(src_s[0:E, :].rearrange("(p n) a -> p (n a)", p=ROWS_E),
                                 src.rearrange("(p n) -> p n", p=ROWS_E)).then_inc(e_copied, 16)
                    sp.dma_start(dst_s[0:E, :].rearrange("(p n) a -> p (n a)", p=ROWS_E),
                                 dst.rearrange("(p n) -> p n", p=ROWS_E)).then_inc(e_copied, 16)
                    sp.wait_ge(masks_set, 5)
                    sp.dma_start(src_s[E:E + P, :].rearrange("(p n) a -> p (n a)", p=1), pad[:, 0:P]).then_inc(e_copied, 16)
                    sp.dma_start(dst_s[E:E + P, :].rearrange("(p n) a -> p (n a)", p=1), pad[:, P:2 * P]).then_inc(e_copied, 16)
                    sp.wait_ge(e_copied, 16 * 5)

                @block.gpsimd
                def _(pool):
                    nc.gpsimd.memset(ones[:, :], 1.0).then_inc(masks_set, 1)
                    for l in range(2):
                        nc.gpsimd.memset(alr[l][:, :, :], 0.0).then_inc(alr_zero, 1)
                    nc.gpsimd.memset(ident[:, :], 0.0).then_inc(masks_set, 1)
                    nc.gpsimd.iota(iota_i[:, :], [[1, P]], base=0, channel_multiplier=0).then_inc(iotas_made, 1)
                    nc.gpsimd.iota(pidx_i[:, :], [[0, 1]], base=0, channel_multiplier=1).then_inc(iotas_made, 1)
                    pool.wait_ge(masks_set, 2)
                    nc.gpsimd.affine_select(out=ident[:, :], in_=ident[:, :], compare_op=ALU.not_equal, fill=1.0,
                                            base=0, pattern=[[-1, P]], channel_multiplier=1).then_inc(masks_set, 1)
                    nc.gpsimd.memset(pad[:, 0:P], 0).then_inc(masks_set, 1)
                    nc.gpsimd.memset(pad[:, P:2 * P], PAD_DST).then_inc(masks_set, 1)
                    pool.wait_ge(alr_zero, 2)
                    with nc.allow_non_contiguous_dma(reason="vectors of one head's features, one to a partition"):
                        for l in range(2):
                            flat = alr[l][:, :, :].rearrange("p k c -> p (k c)")
                            for odd in range(2):
                                rows = slice(odd * HD, odd * HD + HD)
                                for part, vec in enumerate([gal[l], gar[l]]):
                                    first_c = part * H + odd
                                    pool.dma_start(flat[rows, first_c:first_c + 2 * H + 3:2 * H + 2],
                                                   vec[odd:H:2, :].rearrange("k d -> d k")).then_inc(a_loaded, 16)

                @block.scalar
                def _(act):
                    act.wait_ge(dst_cast, 1)
                    act.wait_ge(thr_set, 1)
                    act.sem_inc(counted, 2)

                    def count(t, u):
                        act.wait_ge(counted, t + 1)
                        nc.scalar.activation(side[:, u % 2, :], dst_f[:, :], ACT.Sign, bias=thr[0:ROWS_E, bass.ds(t, 1)],
                                             scale=-1.0, accum_out=cnt[:, bass.ds(t, 1)]).then_inc(counted, 1)

                    with act.Fori(0, NT_A // 8) as j:
                        for u in range(8):
                            count(8 * j + u, u)
                    for t in range(NT_A // 8 * 8, NT_A):
                        count(t, t)

                @block.tensor
                def _(pe):
                    pe.wait_ge(w_loaded, 16 * N_W)
                    pe.wait_ge(emb_made, 1)
                    for half in range(2):
                        for k in range(2):
                            mm = nc.tensor.matmul(bank[1 + half][0:K3, :], emb_r[:, k, :, :].rearrange("p a r -> p (a r)"),
                                                  w1t[:, 2 + k, half * 512:(half + 1) * 512],
                                                  start=(k == 0), stop=(k == 1))
                        mm.then_inc(w3_made, 1)
                    pe.wait_ge(a_loaded, 16 * 8)
                    for l in range(2):
                        for m in range(2):
                            for k in range(2):
                                mm = nc.tensor.matmul(bank[0][:, (2 * l + m) * 8:(2 * l + m) * 8 + 8],
                                                      wn[l][:, k, m * P:(m + 1) * P], alr[l][:, k, :],
                                                      start=(k == 0), stop=(k == 1))
                    mm.then_inc(elw_made, 1)
                    pe.wait_ge(wx_made, 2)
                    for kb in range(HID // P):
                        if kb >= 4:
                            pe.wait_ge(wc_read, kb - 3)
                        for m in range(2):
                            mm = nc.tensor.matmul(bank[3 + kb % 4][:, 0:RX], w2n[:, m, kb * P:(kb + 1) * P],
                                                  wx1[:, m, :], start=(m == 0), stop=(m == 1))
                        mm.then_inc(wc_made, 1)
                    for m in range(2):
                        mm = nc.tensor.matmul(bank[7][:, 0:RX], b2col[:, m:m + 1].to_broadcast([P, P]),
                                              wx1[:, m, :], start=(m == 0), stop=(m == 1))
                    mm.then_inc(wc_made, 1)

                @block.vector
                def _(dve):
                    dve.wait_ge(e_loaded, 32)
                    nc.vector.tensor_copy(dst_f[:, :], dst_i[:, :]).then_inc(dst_cast, 1)
                    dve.wait_ge(iotas_made, 2)
                    nc.vector.tensor_scalar(thr[:, :], iota_i[:, 0:NT], float(P), P - 0.5, ALU.mult, ALU.add).then_inc(thr_set, 1)
                    nc.vector.tensor_copy(iota_f[:, :], iota_i[:, :])
                    nc.vector.tensor_copy(pidx[:, :], pidx_i[:, :])
                    nc.vector.memset(epst[:, :], LN_EPS)
                    centre.inc(nc.vector.memset(emb_r[:, :, :, :], 0.0))
                    centre.inc(nc.vector.tensor_scalar(row_i[:, :], pidx_i[:, :], PR - 1, None, ALU.bitwise_and))
                    centre.wait(dve)
                    centre.inc(nc.vector.tensor_copy(row_f[:, :], row_i[:, :]))
                    dve.wait_ge(dst_cast, 1)
                    nc.vector.memset(cnt[:, NT + 1:NT + 2], 0.0).then_inc(thr_set, 1)
                    nc.vector.scalar_tensor_tensor(fall[:, 0, 0:COLS_E - 1], dst_f[:, 0:COLS_E - 1], 0.0, dst_f[:, 1:COLS_E],
                                                   ALU.add, ALU.is_gt, accum_out=cnt[:, NT:NT + 1]).then_inc(fall_made, 1)
                    dve.wait_ge(thr_set, 2)
                    nc.vector.tensor_tensor(cnt[0:ROWS_E - 1, NT + 1:NT + 2], dst_f[0:ROWS_E - 1, COLS_E - 1:COLS_E],
                                            row_next[0:ROWS_E - 1, :], ALU.is_gt)
                    for t in range(NT_A, NT):
                        n = t - NT_A
                        if n:
                            dve.wait_ge(fall_made, n)
                        nc.vector.tensor_scalar(fall[:, (n + 1) % 2, :], dst_f[:, :], thr[0:ROWS_E, t:t + 1], 0.0, ALU.is_lt,
                                                ALU.add, accum_out=cnt[:, t:t + 1]).then_inc(fall_made, 1)
                    dve.wait_ge(masks_set, 3)
                    rows = ident[0:HC, 0:HC]
                    nc.vector.tensor_reduce(pick_c[:, :], rows.rearrange("p (c h) -> p c h", h=H), AX.X, ALU.add)
                    nc.vector.tensor_reduce(pick_h[:, :], rows.rearrange("p (c h) -> p h c", h=H), AX.X, ALU.add)
                    nc.vector.tensor_copy(ident_b[:, :], ident[:, :])
                    nc.vector.tensor_copy(pick_hT[:, :].rearrange("p (c h) -> p c h", h=H),
                                          ident[0:H, 0:H].unsqueeze(1).to_broadcast([H, CB, H]))
                    dve.wait_ge(w_loaded, 16 * N_W)
                    nc.vector.tensor_copy(emb_r[:, :, :, 0:LABELS], emb_t[:, :, :].unsqueeze(2).to_broadcast([P, 2, PARTS, LABELS])
                                          ).then_inc(emb_made, 1)
                    centre.inc(nc.vector.tensor_reduce(w_sum[:, :], w1t[:, 0:2, :], AX.X, ALU.add))
                    centre.wait(dve)
                    centre.inc(nc.vector.tensor_scalar(w_mean[:, :], w_sum[:, :], 1.0 / HID, None, ALU.mult))
                    centre.wait(dve)
                    for k in range(2):
                        nc.vector.tensor_scalar(w1t[:, k, :], w1t[:, k, :], w_mean[:, k:k + 1], None, ALU.subtract)
                    for half in range(2):
                        dve.wait_ge(w3_made, half + 1)
                        cols = slice(half * 512, (half + 1) * 512)
                        nc.vector.tensor_tensor(w3_f[:, cols], bank[1 + half][0:K3, :], b1_rows[:, cols], ALU.add).then_inc(w3_read, 1)
                    dve.wait_ge(w3_read, 2)
                    centre.inc(nc.vector.tensor_reduce(w3_sum[:, :], w3_f[:, :], AX.X, ALU.add))
                    centre.wait(dve)
                    centre.inc(nc.vector.tensor_scalar(w3_mean[:, :], w3_sum[:, :], 1.0 / HID, None, ALU.mult))
                    centre.wait(dve)
                    centre.inc(nc.vector.tensor_scalar(w3_f[:, :], w3_f[:, :], w3_mean[:, 0:1], None, ALU.subtract))
                    for k in range(PARTS):
                        centre.wait(dve)
                        centre.inc(nc.vector.tensor_copy(w3_p[:, k, :], w3_f[:, :]))
                        centre.wait(dve)
                        rows = slice(k * PR, (k + 1) * PR)
                        nc.vector.tensor_copy(w3[rows, :], w3_p[rows, k, :])
                        if k < PARTS - 1:
                            centre.inc(nc.vector.tensor_tensor(w3_f[:, :], w3_f[:, :], w3_p[:, k, :], ALU.subtract))
                    dve.wait_ge(elw_made, 1)
                    for l in range(2):
                        for m in range(2):
                            heads = wx[l][:, m, 0:ROW].rearrange("p (h w) -> p h w", w=HW)
                            nc.vector.tensor_copy(heads[:, :, 0:HD], wt[l][:, m, :].rearrange("p (h d) -> p h d", d=HD))
                            c = (2 * l + m) * 8
                            nc.vector.tensor_copy(heads[:, :, HD:HW], bank[0][:, c:c + H].rearrange("p (h a) -> p h a", a=1))
                            last = nc.vector.tensor_copy(wx[l][:, m, ROW:RX], bank[0][:, c + H:c + 2 * H])
                            if m == 1:
                                last.then_inc(wx_made, 1)
                    nc.vector.memset(tile_i[:, :, :], 0)
                    dve.wait_ge(lab_loaded, 16)
                    nc.vector.tensor_scalar(hot[:, :], lab[:, :], row_f[0:K3, 0:1], None, ALU.is_equal)
                    for kb in range(HID // P):
                        dve.wait_ge(wc_made, kb + 1)
                        nc.vector.tensor_copy(wc[:, kb, :], bank[3 + kb % 4][:, 0:RX]).then_inc(wc_read, 1)
                    dve.wait_ge(wc_made, HID // P + 1)
                    nc.vector.tensor_copy(bias_c[:, :], bank[7][:, 0:RX])

            with ExitStack() as pw:
                W = 2 * P
                STRIPS = -(-NT // 2)
                KB = HID // P
                xt = sb("xt", [P, 2, 2, W], ctx=pw)
                sq = sb("sq", [P, KB // 2, 2 * W], ctx=pw)
                sq_sum = sb("sq_sum", [P, W], ctx=pw)
                sd = sb("sd", [P, W], ctx=pw)
                rs = sb("rs", [P, W], ctx=pw)
                nrm = sb("nrm", [P, KB, W], ctx=pw)
                xn = sb("xn", [P, 2, KB, W], ctx=pw)
                feat = sb("feat", [P, 2, 2, RX], ctx=pw)
                HI = 64
                rep_lo = sb("rep_lo", [ROWS_E, P], ctx=pw)
                rep_dst = sb("rep_dst", [ROWS_E, ROWS_E], ctx=pw)
                first_e = sb("first_e", [P, NT + 1], ctx=pw)
                unsorted = sb("unsorted", [1, 1], I32, ctx=pw)
                n_e = sb("n_e", [P, NT], ctx=pw)
                n_ci = sb("n_ci", [P, NT], I32, ctx=pw)
                n_c = sb("n_c", [P, NT], ctx=pw)
                chunk0 = sb("chunk0", [P, NT + 1], ctx=pw)
                cid_i = sb("cid_i", [P, CG], I32, ctx=pw)
                cid = sb("cid", [P, CG], ctx=pw)
                upto = sb("upto", [P, 3, NT], ctx=pw)
                tile_c = sb("tile_c", [P, CG], ctx=pw)
                tile_ch = sb("tile_ch", [P, CG], ctx=pw)
                tile_e = sb("tile_e", [P, CG], ctx=pw)
                node0 = sb("node0", [P, CG], ctx=pw)
                base_f = sb("base_f", [P, CG], ctx=pw)
                base_i = sb("base_i", [P, CG], I32, ctx=pw)
                sl_d = sb("sl_d", [P, CG, P], I32, ctx=pw)
                sl_s = sb("sl_s", [P, CG, P], I32, ctx=pw)
                sl_df = sb("sl_df", [P, CG, P], ctx=pw)
                sl_db = sb("sl_db", [P, CG, P], BF16, ctx=pw)
                sl_sf = sb("sl_sf", [P, CG, P], ctx=pw)
                sl_k = sb("sl_k", [P, CG, P], ctx=pw)
                keys = sb("keys", [P, 2 * CG * P + 1], ctx=pw)
                tile_b = sb("tile_b", [P, CG * P], ctx=pw)
                key_t = sb("key_t", [HC, NB, P], ctx=pw)
                diff = sb("diff", [H, NB, 2 * CB], ctx=pw)
                carried = sb("carried", [P, NB], ctx=pw)
                dst_hi_i = sb("dst_hi_i", [ROWS_E, COLS_E], I32, ctx=pw)
                dst_hi, dst_lo = [xn[0:ROWS_E, k, :, :].rearrange("p k n -> p (k n)")[:, 0:COLS_E] for k in range(2)]
                hot_lo = sb("hot_lo", [ROWS_E, P], ctx=pw)
                hot_hi = sb("hot_hi", [ROWS_E, HI], ctx=pw)
                hot_lo_T = sb("hot_lo_T", [P, ROWS_E], ctx=pw)
                before = sb("before", [P, P], ctx=pw)
                after = sb("after", [P, P], ctx=pw)
                place = sb("place", [P, HI], ctx=pw)
                hi_sum = sb("hi_sum", [P, HI + 1], ctx=pw)
                same = sb("same", [ROWS_E, ROWS_E], ctx=pw)
                looked = sb("looked", [ROWS_E, HI], ctx=pw)
                pos_a = sb("pos_a", [ROWS_E, 2], ctx=pw)
                pos_i = sb("pos_i", [ROWS_E, 1], I32, ctx=pw)
                src_u = sb("src_u", [ROWS_E, 1], I32, ctx=pw)
                dst_u = sb("dst_u", [ROWS_E, 1], I32, ctx=pw)
                slots_init = sem("slots_init", pw)
                summed = sem("summed", pw)
                order_known = sem("order_known", pw)
                base_set = sem("base_set", pw)
                sl_loaded = [sem("sl_loaded_d", pw), sem("sl_loaded_s", pw)]
                turned = sem("turned", pw)
                slots_read = sem("slots_read", pw)
                keys_read = sem("keys_read", pw)
                keys_out = sem("keys_out", pw)
                keys_in = sem("keys_in", pw)
                k_ready = sem("k_ready", pw)
                slot_step = Counter(sem("slot_step", pw))
                sort_step = Counter(sem("sort_step", pw))
                hots_counted = sem("hots_counted", pw)
                hist_made = sem("hist_made", pw)
                place_step = sem("place_step", pw)
                place_mm = sem("place_mm", pw)
                hots_placed = sem("hots_placed", pw)
                rows_made = sem("rows_made", pw)
                lo_turned = sem("lo_turned", pw)
                place_looked = sem("place_looked", pw)
                pos_step = sem("pos_step", pw)
                pos_set = sem("pos_set", pw)
                scatter_due = sem("scatter_due", pw)
                src_placed = sem("src_placed", pw)
                dst_placed = sem("dst_placed", pw)
                x_loaded = [sem(f"x_loaded{p}", pw) for p in range(2)]
                h1_made = sem("h1_made", pw)
                sq_made = sem("sq_made", pw)
                sum_made = sem("sum_made", pw)
                var_made = sem("var_made", pw)
                sd_made = sem("sd_made", pw)
                rs_made = sem("rs_made", pw)
                nrm_made = sem("nrm_made", pw)
                xn_made = sem("xn_made", pw)
                feat_mm = sem("feat_mm", pw)
                feat_made = sem("feat_made", pw)
                feat_out = [sem(f"feat_out{p}", pw) for p in range(2)]
                block = pw.enter_context(nc.Block())
                h1 = bank[0:4]
                fp = bank[4:6]
                var = bank[6]
                slots_ps = bank[6][:, W:W + 2 * P]
                rows_ps = bank[7][:, 0:3 * P]
                B = KB // 2
                x_t = xT.rearrange("(k p) n -> p k n", p=P)

                def blocks(ap, w):
                    return ap.rearrange("p (two n) -> p two n", two=2)[:, :, 0:w]

                @block.sync
                def _(sp):
                    def load(s, p, w):
                        sp.dma_start(xt[:, p, :, 0:w], x_t[:, :, bass.ds(s * W, w)]).then_inc(x_loaded[p], 16)

                    def store(s, p, tiles):
                        sp.wait_ge(feat_made, 2 * s + tiles)
                        sp.dma_start(table[0][bass.ds(s * W, tiles * P), :].rearrange("(t p) w -> p t w", p=P),
                                     feat[:, p, 0:tiles, 0:ROW]).then_inc(feat_out[p], 16)

                    load(0, 0, W)
                    load(1, 1, W)
                    for i in range(2):
                        sp.wait_ge(h1_made, B * (i + 1))
                        load(2 + i, i, W)
                    sp.wait_ge(k_ready, CG)
                    sp.dma_start(key_d.rearrange("(g p) e -> p g e", p=P), sl_k[:, :, :]).then_inc(keys_out, 16)
                    sp.dma_start(loc_d.rearrange("(g p) e -> p g e", p=P), sl_db[:, :, :]).then_inc(keys_out, 16)
                    sp.wait_ge(keys_out, 32)
                    sp.wait_ge(slots_init, 2)
                    sp.dma_start(loc_t[0:CB, :, :], loc_d[0:NC, :].rearrange("(b c) e -> c b e", c=CB)).then_inc(keys_in, 16)
                    for h in range(H):
                        sp.dma_start(key_t[h:HC:H, :, :],
                                     key_d[0:NC, :].rearrange("(b c) e -> c b e", c=CB)).then_inc(keys_in, 16)
                    store(0, 0, 2)
                    store(1, 1, 2)
                    with sp.Fori(1, (STRIPS - 3) // 2) as j:
                        for p in range(2):
                            sp.wait_ge(h1_made, B * (2 * j + p + 1))
                            load(2 * j + p + 2, p, W)
                            store(2 * j + p, p, 2)
                    s = STRIPS - 3
                    sp.wait_ge(h1_made, B * (s + 1))
                    load(s + 2, 0, LAST)
                    store(s, 0, 2)
                    store(s + 1, 1, 2)
                    store(s + 2, 0, 1)
                    sp.wait_ge(feat_out[0], 16 * ((STRIPS + 1) // 2))
                    sp.wait_ge(feat_out[1], 16 * (STRIPS // 2))

                def if_unsorted(eng, engine):
                    eng.wait_ge(order_known, 1)
                    falls = nc.values_load_multi_w_load_instructions(
                        unsorted[0:1, 0:1], engines=(engine,), min_val=0, max_val=E,
                        skip_runtime_bounds_check_because="a count of edges")[1][0]
                    return eng.If(falls > 0)

                @block.gpsimd
                def _(pool):
                    nc.gpsimd.iota(cid_i[:, :], [[P, CG]], base=0, channel_multiplier=1).then_inc(slots_init, 1)
                    nc.gpsimd.memset(loc_t[:, :, :], 0.0).then_inc(slots_init, 1)
                    with if_unsorted(pool, ET.Pool):
                        with pool.Fori(0, COLS_E) as c:
                            pool.wait_ge(pos_set, c + 1)
                            pool.sem_inc(scatter_due, 1)
                            pool.indirect_dma_start(src_s[:, :], bass.IndirectOffsetOnAxis(pos_i[:, 0:1], 0), src_u[:, :],
                                                    None).then_inc(src_placed, 16)
                            pool.indirect_dma_start(dst_s[:, :], bass.IndirectOffsetOnAxis(pos_i[:, 0:1], 0), dst_u[:, :],
                                                    None).then_inc(dst_placed, 16)
                        pool.wait_ge(src_placed, 16 * COLS_E)
                        pool.wait_ge(dst_placed, 16 * COLS_E)
                    pool.wait_ge(base_set, 1)
                    for g in range(CG):
                        pool.indirect_dma_start(sl_d[:, g, :], None, dst_s[:, :],
                                                bass.IndirectOffsetOnAxis(base_i[:, g:g + 1], 0)).then_inc(sl_loaded[0], 16)
                    for g in range(CG):
                        pool.indirect_dma_start(sl_s[:, g, :], None, src_s[:, :],
                                                bass.IndirectOffsetOnAxis(base_i[:, g:g + 1], 0)).then_inc(sl_loaded[1], 16)

                @block.tensor
                def _(pe):
                    def count_nodes():
                        with pe.Fori(0, COLS_E) as c:
                            pe.wait_ge(hots_counted, c + 1)
                            nc.tensor.matmul(bank[4][:, 0:HI], hot_lo[:, :], hot_hi[:, :], start=True, stop=True).then_inc(hist_made, 1)

                    def first_places():
                        pe.wait_ge(place_step, COLS_E + 1)
                        nc.tensor.matmul(bank[5][:, 0:HI], after[:, :], place[:, :], start=True, stop=True)
                        nc.tensor.matmul(bank[5][:, HI:2 * HI], ones[:, :], place[:, :], start=True, stop=True).then_inc(place_mm, 1)

                    def place_edges():
                        pe.wait_ge(place_step, COLS_E + 2)
                        with pe.Fori(0, COLS_E) as c:
                            pe.wait_ge(hots_placed, c + 1)
                            nc.tensor.matmul(bank[4][:, 0:HI], hot_lo[:, :], hot_hi[:, :], start=True, stop=True)
                            nc.tensor.matmul(bank[5][:, 0:ROWS_E], rep_lo[:, :], ident[0:ROWS_E, 0:ROWS_E], start=True, stop=True)
                            nc.tensor.matmul(bank[6][0:ROWS_E, 0:ROWS_E], rep_dst[:, :], ident[0:ROWS_E, 0:ROWS_E],
                                             start=True, stop=True).then_inc(rows_made, 1)
                            pe.wait_ge(lo_turned, c + 1)
                            nc.tensor.matmul(bank[7][0:ROWS_E, 0:HI], hot_lo_T[:, :], place[:, :], start=True, stop=True
                                             ).then_inc(place_looked, 1)

                    def turn_slots(g):
                        pe.wait_ge(k_ready, CG)
                        if g:
                            pe.wait_ge(slots_read, g)
                            pe.wait_ge(keys_read, g)
                        nc.tensor.transpose(slots_ps[:, 0:P], sl_sf[:, g, :], ident[:, :])
                        nc.tensor.transpose(slots_ps[:, P:2 * P], sl_df[:, g, :], ident[:, :])
                        nc.tensor.matmul(rows_ps[:, 0:P], sl_k[:, g, 0:1].to_broadcast([P, P]), ident[:, :], start=True, stop=True)
                        nc.tensor.matmul(rows_ps[:, P:2 * P], sl_k[:, g, P - 1:P].to_broadcast([P, P]), ident[:, :],
                                         start=True, stop=True)
                        nc.tensor.matmul(rows_ps[:, 2 * P:3 * P], tile_c[:, g:g + 1].to_broadcast([P, P]), ident[:, :],
                                         start=True, stop=True).then_inc(turned, 1)

                    def first(s, p, w, x_rounds, between=None):
                        pe.wait_ge(x_loaded[p], x_rounds)
                        for b in range(B):
                            if beyond(s, 1):
                                pe.wait_ge(nrm_made, B * (s - 1) + b + 1)
                            for half in range(2):
                                cols = slice((2 * b + half) * P, (2 * b + half + 1) * P)
                                o = h1[b][:, half * W:half * W + w]
                                for k in range(2):
                                    nc.tensor.matmul(o, w1t[:, k, cols], xt[:, p, k, 0:w], start=(k == 0), stop=False)
                                mm = nc.tensor.matmul(o, w3[:, cols], hot[:, bass.ds(s * W, w)], start=False, stop=True)
                            mm.then_inc(h1_made, 1)
                            if between:
                                between(b)

                    def variance(s, w):
                        pe.wait_ge(sum_made, s + 1)
                        nc.tensor.matmul(var[:, 0:w], ones[:, :], sq_sum[:, 0:w], start=True, stop=True).then_inc(var_made, 1)

                    def second(s, p, t):
                        pe.wait_ge(xn_made, s + 1)
                        if beyond(s, 1):
                            pe.wait_ge(feat_made, 2 * (s - 1) + t + 1)
                        for k in range(KB):
                            mm = nc.tensor.matmul(fp[t][:, 0:RX], xn[:, p, k, t * P:(t + 1) * P], wc[:, k, :],
                                                  start=(k == 0), stop=(k == KB - 1))
                        mm.then_inc(feat_mm, 1)

                    def strip(s, p, w, x_rounds, between=None):
                        first(s, p, w, x_rounds, between)
                        if beyond(s, 1):
                            second(s - 1, 1 - p, 0)
                        if between:
                            between(B)
                            pe.wait_ge(slots_read, B + 1)
                        variance(s, w)
                        if beyond(s, 1):
                            second(s - 1, 1 - p, 1)
                        if between:
                            pe.wait_ge(sd_made, s + 1)
                            between(B + 1)
                            between(B + 2)

                    nc.tensor.matmul(bank[7][:, 0:NT + 2], ones[0:ROWS_E, :], cnt[:, :], start=True, stop=True).then_inc(summed, 1)
                    first(0, 0, W, 16)
                    with if_unsorted(pe, ET.PE):
                        count_nodes()
                        first_places()
                        place_edges()
                    variance(0, W)
                    strip(1, 1, W, 16)
                    assert CG == B + 3
                    strip(2, 0, W, 32, turn_slots)
                    first(3, 1, W, 32)
                    second(2, 0, 0)
                    pe.wait_ge(slots_read, CG)
                    variance(3, W)
                    second(2, 0, 1)
                    with pe.Fori(2, (STRIPS - 1) // 2) as j:
                        strip(2 * j, 0, W, 16 * j + 16)
                        strip(2 * j + 1, 1, W, 16 * j + 16)
                    strip(STRIPS - 1, 0, LAST, 16 * (STRIPS // 2) + 16)
                    second(STRIPS - 1, 0, 0)

                @block.scalar
                def _(act):
                    def read_slots(g):
                        act.wait_ge(turned, g + 1)
                        nc.scalar.copy(src_idx[:, g * P:(g + 1) * P], slots_ps[:, 0:P])
                        nc.scalar.copy(dst_loc[:, g * P:(g + 1) * P], slots_ps[:, P:2 * P]).then_inc(slots_read, 1)

                    def strip(s, p, w, between=None):
                        if beyond(s, 1):
                            act.wait_ge(sum_made, s)
                        for b in range(B):
                            act.wait_ge(h1_made, B * s + b + 1)
                            nc.scalar.activation(blocks(sq[:, b, :], w), blocks(h1[b][:, :], w), ACT.Square).then_inc(sq_made, 1)
                            if between:
                                between(b)
                        if between:
                            between(B)
                        act.wait_ge(var_made, s + 1)
                        nc.scalar.activation(sd[:, 0:w], var[:, 0:w], ACT.Sqrt, bias=epst[:, 0:1], scale=1.0 / HID
                                             ).then_inc(sd_made, 1)
                        if between:
                            between(B + 1)
                        if beyond(s, 2):
                            act.wait_ge(feat_mm, 2 * (s - 1))
                        for k in range(KB):
                            if k % 2 == 0:
                                act.wait_ge(nrm_made, B * s + k // 2 + 1)
                            a = nc.scalar.activation(xn[:, p, k, 0:w], nrm[:, k, 0:w], ACT.Relu, bias=b_col[:, k:k + 1],
                                                     scale=g_col[:, k:k + 1])
                        a.then_inc(xn_made, 1)
                        if between:
                            between(B + 2)

                    strip(0, 0, W)
                    strip(1, 1, W)
                    strip(2, 0, W, read_slots)
                    strip(3, 1, W)
                    with act.Fori(2, (STRIPS - 1) // 2) as j:
                        strip(2 * j, 0, W)
                        strip(2 * j + 1, 1, W)
                    strip(STRIPS - 1, 0, LAST)

                @block.vector
                def _(dve):
                    s = slot_step

                    def sort():
                        q = sort_step

                        def hots(c, made):
                            nc.vector.tensor_scalar(hot_lo[:, :], iota_f[0:ROWS_E, :], dst_lo[:, bass.ds(c, 1)], None, ALU.is_equal)
                            nc.vector.tensor_scalar(hot_hi[:, :], iota_f[0:ROWS_E, 0:HI], dst_hi[:, bass.ds(c, 1)], None,
                                                    ALU.is_equal).then_inc(made, 1)

                        q.inc(nc.vector.tensor_scalar(dst_hi_i[:, :], dst_i[:, :], 7, None, ALU.arith_shift_right))
                        q.inc(nc.vector.tensor_scalar(before[:, :], iota_f[:, :], pidx[:, 0:1], None, ALU.is_lt))
                        q.inc(nc.vector.tensor_scalar(after[:, :], iota_f[:, :], pidx[:, 0:1], None, ALU.is_gt))
                        nc.vector.memset(place[:, :], 0.0).then_inc(place_step, 1)
                        q.inc(nc.vector.memset(hi_sum[:, 0:1], 0.0))
                        q.wait(dve)
                        q.inc(nc.vector.tensor_copy(dst_hi[:, :], dst_hi_i[:, :]))
                        q.wait(dve)
                        q.inc(nc.vector.scalar_tensor_tensor(dst_lo[:, :], dst_hi[:, :], -float(P), dst_f[:, :], ALU.mult, ALU.add))
                        q.wait(dve)
                        with dve.Fori(0, COLS_E) as c:
                            hots(c, hots_counted)
                            dve.wait_ge(hist_made, c + 1)
                            dve.wait_ge(place_step, c + 1)
                            nc.vector.tensor_tensor(place[:, :], place[:, :], bank[4][:, 0:HI], ALU.add).then_inc(place_step, 1)
                        dve.wait_ge(place_mm, 1)
                        q.inc(nc.vector.tensor_tensor_scan(hi_sum[:, 1:HI + 1], ones[:, 0:HI], bank[5][:, HI:2 * HI], 0.0,
                                                           ALU.mult, ALU.add))
                        q.wait(dve)
                        nc.vector.tensor_tensor(place[:, :], hi_sum[:, 0:HI], bank[5][:, 0:HI], ALU.add).then_inc(place_step, 1)
                        dve.wait_ge(place_step, COLS_E + 2)
                        with dve.Fori(0, COLS_E) as c:
                            nc.vector.tensor_copy(rep_lo[:, :], dst_lo[:, bass.ds(c, 1)].to_broadcast([ROWS_E, P]))
                            nc.vector.tensor_copy(rep_dst[:, :], dst_f[:, bass.ds(c, 1)].to_broadcast([ROWS_E, ROWS_E]))
                            hots(c, hots_placed)
                            dve.wait_ge(rows_made, c + 1)
                            nc.vector.tensor_scalar(hot_lo_T[:, :], bank[5][:, 0:ROWS_E], pidx[:, 0:1], None,
                                                    ALU.is_equal).then_inc(lo_turned, 1)
                            nc.vector.scalar_tensor_tensor(same[:, :], bank[6][0:ROWS_E, 0:ROWS_E], dst_f[:, bass.ds(c, 1)],
                                                           before[0:ROWS_E, 0:ROWS_E], ALU.is_equal, ALU.mult,
                                                           accum_out=pos_a[:, 0:1]).then_inc(pos_step, 1)
                            dve.wait_ge(place_looked, c + 1)
                            nc.vector.scalar_tensor_tensor(looked[:, :], bank[7][0:ROWS_E, 0:HI], 1.0, hot_hi[:, :], ALU.mult,
                                                           ALU.mult, accum_out=pos_a[:, 1:2]).then_inc(pos_step, 1)
                            nc.vector.tensor_tensor(place[:, :], place[:, :], bank[4][:, 0:HI], ALU.add).then_inc(place_step, 1)
                            dve.wait_ge(pos_step, 2 * c + 2)
                            nc.vector.tensor_tensor(pos_i[:, :], pos_a[:, 0:1], pos_a[:, 1:2], ALU.add)
                            nc.vector.tensor_copy(src_u[:, :], src_i[:, bass.ds(c, 1)])
                            nc.vector.tensor_copy(dst_u[:, :], dst_i[:, bass.ds(c, 1)]).then_inc(pos_set, 1)
                            dve.wait_ge(src_placed, 16 * c + 16)
                            dve.wait_ge(dst_placed, 16 * c + 16)
                            dve.wait_ge(place_step, COLS_E + 3 + c)

                    def chunks_of_tiles():
                        s.inc(nc.vector.memset(first_e[:, 0:1], 0.0))
                        s.inc(nc.vector.memset(chunk0[:, 0:1], 0.0))
                        s.inc(nc.vector.memset(keys[:, 0:1], -BIG))
                        s.inc(nc.vector.memset(flags[:, :, :], 0.0))
                        s.inc(nc.vector.memset(flags_x[:, :, :], 0.0))
                        dve.wait_ge(slots_init, 1)
                        s.inc(nc.vector.tensor_copy(cid[:, :], cid_i[:, :]))
                        dve.wait_ge(summed, 1)
                        s.inc(nc.vector.tensor_scalar(first_e[:, 1:NT_A + 1], bank[7][:, 0:NT_A], float(E), 0.5, ALU.add, ALU.mult))
                        s.inc(nc.vector.tensor_copy(first_e[:, NT_A + 1:NT + 1], bank[7][:, NT_A:NT]))
                        falls = bank[7][0:1, NT:NT + 2]
                        nc.vector.tensor_scalar(unsorted[:, :], falls[:, 0:1], falls[:, 1:2], None, ALU.add).then_inc(order_known, 1)
                        s.wait(dve)
                        s.inc(nc.vector.tensor_tensor(n_e[:, :], first_e[:, 1:NT + 1], first_e[:, 0:NT], ALU.subtract))
                        s.wait(dve)
                        s.inc(nc.vector.tensor_scalar(n_ci[:, :], n_e[:, :], float(P - 1), None, ALU.add))
                        s.wait(dve)
                        s.inc(nc.vector.tensor_scalar(n_ci[:, :], n_ci[:, :], 7, None, ALU.arith_shift_right))
                        s.wait(dve)
                        s.inc(nc.vector.tensor_copy(n_c[:, :], n_ci[:, :]))
                        s.wait(dve)
                        s.inc(nc.vector.tensor_tensor_scan(chunk0[:, 1:NT + 1], ones[:, 0:NT], n_c[:, :], 0.0, ALU.mult, ALU.add))
                        s.wait(dve)
                        s.inc(nc.vector.tensor_copy(n_chunks[:, :], chunk0[0:1, NT:NT + 1]))
                        starts = chunk0[:, 1:NT]
                        for g in range(CG):
                            c = cid[:, g:g + 1]
                            s.inc(nc.vector.tensor_scalar(upto[:, 0, 0:NT - 1], starts, c, 0.0, ALU.is_le, ALU.add,
                                                          accum_out=tile_c[:, g:g + 1]))
                            s.inc(nc.vector.scalar_tensor_tensor(upto[:, 1, 0:NT - 1], starts, c, n_c[:, 0:NT - 1], ALU.is_le,
                                                                 ALU.mult, accum_out=tile_ch[:, g:g + 1]))
                            s.inc(nc.vector.scalar_tensor_tensor(upto[:, 2, 0:NT - 1], starts, c, n_e[:, 0:NT - 1], ALU.is_le,
                                                                 ALU.mult, accum_out=tile_e[:, g:g + 1]))
                            s.wait(dve)
                        s.inc(nc.vector.tensor_scalar(node0[:, :], tile_c[:, :], float(P), None, ALU.mult))
                        s.inc(nc.vector.tensor_tensor(base_f[:, :], cid[:, :], tile_ch[:, :], ALU.subtract))
                        s.wait(dve)
                        s.inc(nc.vector.scalar_tensor_tensor(base_f[:, :], base_f[:, :], float(P), tile_e[:, :], ALU.mult, ALU.add))
                        s.wait(dve)
                        nc.vector.tensor_scalar(base_i[:, :], base_f[:, :], float(E), None, ALU.min).then_inc(base_set, 1)

                    def read_slots():
                        dve.wait_ge(sl_loaded[0], 16 * CG)
                        dve.wait_ge(sl_loaded[1], 16 * CG)
                        for g in range(CG):
                            nc.vector.tensor_copy(sl_sf[:, g, :], sl_s[:, g, :])
                            nc.vector.tensor_scalar(sl_df[:, g, :], sl_d[:, g, :], node0[:, g:g + 1], None, ALU.subtract)
                            nc.vector.tensor_scalar(sl_db[:, g, :], sl_d[:, g, :], node0[:, g:g + 1], None, ALU.subtract)
                            nc.vector.tensor_scalar(sl_k[:, g, :], sl_d[:, g, :], BIG, None, ALU.mult).then_inc(k_ready, 1)

                    def read_rows(g):
                        dve.wait_ge(turned, g + 1)
                        ends = keys[:, 1 + 2 * g * P:1 + 2 * (g + 1) * P].rearrange("p (c two) -> p two c", two=2)
                        s.inc(nc.vector.tensor_copy(ends, rows_ps[:, 0:2 * P].rearrange("p (two c) -> p two c", two=2)))
                        nc.vector.tensor_copy(tile_b[:, g * P:(g + 1) * P], rows_ps[:, 2 * P:3 * P]).then_inc(keys_read, 1)

                    def find_segments():
                        s.wait(dve)
                        dve.wait_ge(keys_read, CG)
                        s.inc(nc.vector.tensor_copy(tile_i[:, :, 0:CB], tile_b[0:1, 0:NC].rearrange("p (b c) -> p b c", c=CB)))
                        s.inc(nc.vector.tensor_copy(tile_i[:, 0:NB - 1, CB:CB + 1],
                                                    tile_b[0:1, CB:NC].rearrange("p (b c) -> p b c", c=CB)[:, :, 0:1]))
                        k0 = keys[0:H, 0:2 * NC].rearrange("p (b c) -> p b c", c=2 * CB)
                        k1 = keys[0:H, 1:2 * NC + 1].rearrange("p (b c) -> p b c", c=2 * CB)
                        s.inc(nc.vector.tensor_tensor(diff[:, :, :], k0, k1, ALU.subtract))
                        k_end = keys[:, 0:2 * NC].rearrange("p (b c) -> p b c", c=2 * CB)[:, :, 0]
                        t_first = tile_b[:, 0:NC].rearrange("p (b c) -> p b c", c=CB)[:, :, 0]
                        s.inc(nc.vector.tensor_scalar(carried[:, :], k_end, 1.0 / BIG, None, ALU.mult))
                        s.wait(dve)
                        s.inc(nc.vector.scalar_tensor_tensor(flags_x[:, :, 1:2 * CB + 1], diff[:, :, :], -1.0, diff[:, :, :],
                                                             ALU.mult, ALU.min))
                        s.inc(nc.vector.scalar_tensor_tensor(carried[:, :], t_first, -float(P), carried[:, :], ALU.mult, ALU.add))
                        s.wait(dve)
                        s.inc(nc.vector.tensor_scalar(carry_row[:, :], carried[:, :], pidx[:, 0:1], None, ALU.is_equal))
                        dve.wait_ge(keys_in, 16 * (H + 1))
                        s.inc(nc.vector.tensor_tensor(flags[:, :, 1:P], key_t[:, :, 0:P - 1], key_t[:, :, 1:P], ALU.subtract))
                        s.wait(dve)

                    def norm(s, w):
                        dve.wait_ge(sq_made, B * (s + 1))
                        if beyond(s, 1):
                            dve.wait_ge(var_made, s)
                        nc.vector.tensor_reduce(sq_sum[:, 0:w], sq[:, :, :].rearrange("p b (two n) -> p n (b two)", two=2)[:, 0:w, :],
                                                AX.X, ALU.add).then_inc(sum_made, 1)
                        dve.wait_ge(sd_made, s + 1)
                        nc.vector.reciprocal(rs[:, 0:w], sd[:, 0:w]).then_inc(rs_made, 1)
                        dve.wait_ge(rs_made, s + 1)
                        if beyond(s, 1):
                            dve.wait_ge(xn_made, s)
                        for b in range(B):
                            nc.vector.tensor_tensor(nrm[:, 2 * b:2 * b + 2, 0:w], blocks(h1[b][:, :], w),
                                                    rs[:, 0:w].unsqueeze(1).to_broadcast([P, 2, w]), ALU.mult).then_inc(nrm_made, 1)

                    def features(s, p, t, out_rounds):
                        dve.wait_ge(feat_mm, 2 * s + t + 1)
                        if out_rounds is not None:
                            dve.wait_ge(feat_out[p], out_rounds)
                        nc.vector.tensor_tensor(er[:, bass.ds(2 * s + t, 1), :].rearrange("p a h -> p (a h)"), fp[t][:, ROW:RX],
                                                bias_c[:, ROW:RX], ALU.add)
                        nc.vector.tensor_tensor(feat[:, p, t, :], fp[t][:, 0:RX], bias_c[:, :], ALU.add).then_inc(feat_made, 1)

                    def strip(s, p, w, out_rounds):
                        norm(s, w)
                        for t in range(2):
                            features(s - 1, 1 - p, t, out_rounds)

                    chunks_of_tiles()
                    with if_unsorted(dve, ET.DVE):
                        sort()
                    norm(0, W)
                    strip(1, 1, W, None)
                    read_slots()
                    for g in range(B + 1):
                        read_rows(g)
                    norm(2, W)
                    for g in range(B + 1, CG):
                        read_rows(g)
                    for t in range(2):
                        features(1, 1, t, None)
                    find_segments()
                    with dve.Fori(1, (STRIPS - 3) // 2) as j:
                        strip(2 * j + 1, 1, W, 16 * j)
                        strip(2 * j + 2, 0, W, 16 * j)
                    rounds = (STRIPS - 1) // 2
                    strip(STRIPS - 2, 1, W, 16 * (rounds - 1))
                    strip(STRIPS - 1, 0, LAST, 16 * (rounds - 1))
                    features(STRIPS - 1, 0, 0, 16 * rounds)

        acc = sb("acc", [P, NT, ROW])
        for layer in range(2):
            attention(nc, layer, table[layer], bank, ident, ones, iota_f, pick_c, pick_h, pick_hT, src_idx, dst_loc,
                      loc_t, ident_b, pidx, flags, flags_x, tile_i,
                      n_chunks, carry_row, er, acc)
            if layer == 0:
                next_features(nc, bank, ident, biasb[0], acc, er, wx2, table[1])
        finish(nc, x, biasb[1], acc, epst, out)


def attention(nc, layer, table, bank, ident, ones, iota_f, pick_c, pick_h, pick_hT, src_idx, dst_loc, loc_t, ident_b,
              pidx, flags, flags_x, tile_i, n_chunks, carry_row, er, acc):
    with ExitStack() as ctx:
        def sb(name, shape, dt=F32):
            return ctx.enter_context(nc.sbuf_tensor(f"{name}_{layer}", shape, dt))

        def sem(name):
            return ctx.enter_context(nc.semaphore(f"{name}_{layer}"))

        G = sb("gathered", [P, RING, CB, ROW])
        O = sb("onehots", [P, RING, CB, P])
        idx = sb("idx", [P, RING, CB], I32)
        fl = sb("flags_b", [HC, RING, P + 1], BF16)
        fx = sb("flags_xb", [H, RING, 2 * CB + 2])
        far = sb("far", [P, 2, 4, P])
        OT = sb("onehots_T", [P, 2, 4, P], BF16)
        er_p = sb("er_parts", [P, NT, H, PARTS], BF16)
        er_rest = sb("er_rest", [P, 2, NT, H])
        fw = sb("fw", [HC, P])
        seg = sb("seg", [HC, P])
        fw2 = sb("fw2", [HC, P])
        seg2 = sb("seg2", [HC, P])
        spread = sb("spread", [HC, CB, 2])
        ends = sb("ends", [H, 2 * CB + 1])
        ends_f = sb("ends_f", [H, 2 * CB + 1])
        ends_m = sb("ends_m", [H, 2 * CB + 1])
        moved = sb("moved", [H, 2, H])
        back = sb("back", [HC, 2, CB])
        ends_c = sb("ends_c", [HC, 2])
        ref = sb("ref", [P, 2, H])
        ref_l = sb("ref_l", [P, 2, H])
        ref_d = sb("ref_d", [P, H])
        alpha = sb("alpha", [P, H])
        er_e = sb("er_e", [P, HC])
        z = sb("z", [P, 2, HC])
        zl = sb("zl", [P, 2, HC])
        zd = sb("zd", [P, HC])

        el_T = bank[0]
        small = bank[1]
        ends_ps = small[0:H, 0:2 * CB]
        back_ps = small[0:HC, 64:64 + 2 * CB]
        moved_ps = small[:, 128:128 + 2 * H]
        m_ps = small[:, 256:256 + HC]
        er_ps = bank[2][:, 0:HC * PARTS]
        rows_ps = [bank[3], bank[4]]
        part = [bank[5], bank[6], bank[7]]

        gathered = [sem(f"gathered{u}") for u in range(RING)]
        idx_set = sem("idx_set")
        granted = sem("granted")
        flags_set = sem("flags_set")
        acc_zero = sem("acc_zero")
        el_turned = sem("el_turned")
        scan_step = sem("scan_step")
        spread_made = sem("spread_made")
        ends_made = sem("ends_made")
        ends_step = sem("ends_step")
        moved_made = sem("moved_made")
        back_made = sem("back_made")
        back_step = sem("back_step")
        seg_made = sem("seg_made")
        m_turned = sem("m_turned")
        ref_step = sem("ref_step")
        ref_made = sem("ref_made")
        alpha_made = sem("alpha_made")
        o_made = sem("o_made")
        rows_made = sem("rows_made")
        far_made = sem("far_made")
        er_split = sem("er_split")
        ot_made = sem("ot_made")
        er_mm = sem("er_mm")
        er_made = sem("er_made")
        z_step = sem("z_step")
        zd_made = sem("zd_made")
        ex_made = sem("ex_made")
        weighted = sem("weighted")
        weighted_a = sem("weighted_a")
        part_made = sem("part_made")
        summed = sem("summed")
        scaled = sem("scaled")
        block = ctx.enter_context(nc.Block())
        CREDIT = RING * CB
        TG = 4
        NTG = -(-CB // TG)
        LOOPS = NB // RING - 1
        BY_ACT = [8, 10, 12, 14, 16, 18]
        BY_DVE = [c for c in range(CB) if c not in BY_ACT]

        def el(u):
            return G[:, u, :, :].rearrange("p c (h w) -> p (c h) w", w=HW)[:, :, HD]

        def tiles(engine, b):
            return nc.values_load_multi_w_load_instructions(
                tile_i[0:1, bass.ds(b, 1), :].rearrange("p a c -> p (a c)"), engines=(engine,), min_val=0, max_val=NT - 1,
                skip_runtime_bounds_check_because="a count of at most NT - 1 tiles that start before the chunk")[1]

        def last_block_used(eng, engine):
            n = nc.values_load_multi_w_load_instructions(
                n_chunks[0:1, 0:1], engines=(engine,), min_val=0, max_val=NC,
                skip_runtime_bounds_check_because="a count of at most CHUNKS chunks")[1][0]
            return eng.If(n > (NB - 1) * CB)

        def steps(eng, engine, step):
            with eng.Fori(0, LOOPS) as i:
                for u in range(RING):
                    step(i * RING + u, u, i, CB, True)
            for u in range(RING - 2):
                step(LOOPS * RING + u, u, LOOPS, CB, True)
            with last_block_used(eng, engine):
                step(NB - 2, RING - 2, LOOPS, CB, True)
                step(NB - 1, RING - 1, LOOPS, CB_LAST, False)
            with eng.Else():
                step(NB - 2, RING - 2, LOOPS, CB, False)

        @block.gpsimd
        def _(pool):
            pool.sem_inc(summed, CREDIT)

            def gather(b, u, n=CB):
                pool.wait_ge(idx_set, b + 1)
                for c in range(n):
                    if c % MG == 0:
                        pool.wait_ge(summed, CB * b + c + MG)
                        pool.sem_inc(granted, 1)
                    pool.indirect_dma_start(G[:, u, c, :], None, table[:, :],
                                            bass.IndirectOffsetOnAxis(idx[:, u, c:c + 1], 0)).then_inc(gathered[u], 16)

            with pool.Fori(0, LOOPS) as i:
                for u in range(RING):
                    gather(i * RING + u, u)
            for u in range(RING - 1):
                gather(LOOPS * RING + u, u)
            with last_block_used(pool, ET.Pool):
                gather(NB - 1, RING - 1, CB_LAST)

        @block.tensor
        def _(pe):
            def segments(b, u, i):
                in_last = isinstance(b, int) and b == NB - 1
                pe.wait_ge(gathered[u], 16 * (CB * i + (CB_LAST if in_last else CB)))
                nc.tensor.transpose(el_T[0:HC, 0:P], el(u), ident[:, :]).then_inc(el_turned, 1)

            def ends_across(b):
                pe.wait_ge(spread_made, b + 1)
                nc.tensor.matmul(ends_ps, pick_h[:, :], spread[:, :, :].rearrange("p c two -> p (c two)"),
                                 start=True, stop=True).then_inc(ends_made, 1)

            def ends_back(b):
                pe.wait_ge(moved_made, b + 1)
                nc.tensor.matmul(back_ps, pick_hT[:, :], ends_m[:, 1:2 * CB + 1], start=True, stop=True)
                nc.tensor.matmul(moved_ps, ones[0:H, :], moved[:, :, :].rearrange("p a h -> p (a h)"),
                                 start=True, stop=True).then_inc(back_made, 1)

            def maxima(b):
                pe.wait_ge(seg_made, b + 1)
                nc.tensor.transpose(m_ps, seg2[:, :], ident[0:HC, 0:HC]).then_inc(m_turned, 1)

            def rows(b, g):
                pe.wait_ge(far_made, NTG * b + max(g - 1, 0))
                for c in range(g * TG, min(g * TG + TG, CB)):
                    mm = nc.tensor.matmul(rows_ps[g % 2][:, (c % TG) * P:(c % TG + 1) * P],
                                          ident_b[:, c:c + 1].to_broadcast([P, P]),
                                          loc_t[:, bass.ds(b, 1), :].rearrange("p a e -> p (a e)"), start=True, stop=True)
                mm.then_inc(rows_made, 1)

            def er_of_slots(b, t, g):
                pe.wait_ge(ot_made, NTG * b + g + 1)
                if g == 0 and beyond(b, 1):
                    pe.wait_ge(er_made, b)
                for c in range(g * TG, min(g * TG + TG, CB)):
                    mm = nc.tensor.matmul(er_ps[:, c * H * PARTS:(c + 1) * H * PARTS], OT[:, g % 2, c % TG, :],
                                          er_p[:, bass.ds(t[c], 1), :, :].rearrange("p a h k -> p (a h k)"), start=True, stop=True)
                mm.then_inc(er_mm, 1)

            def sums(b, u, c0, c1):
                for c in range(c0, c1):
                    if c in BY_ACT:
                        pe.wait_ge(weighted_a, len(BY_ACT) * b + BY_ACT.index(c) + 1)
                    else:
                        pe.wait_ge(weighted, len(BY_DVE) * b + BY_DVE.index(c) + 1)
                    pe.wait_ge(summed, CREDIT + CB * b + c - NPS + 1)
                    nc.tensor.matmul(part[c % NPS][:, 0:ROW], O[:, u, c, :], G[:, u, c, :],
                                     start=True, stop=True).then_inc(part_made, 1)

            def step(b, u, i, n_b, has_next):
                un, i_n = (u + 1) % RING, i + (u + 1) // RING
                if not has_next:
                    sums(b, u, 0, n_b)
                    return
                t = tiles(ET.PE, b + 1)
                for c in range(CB):
                    sums(b, u, c, c + 1)
                    if c == 10:
                        segments(b + 1, un, i_n)
                    if c == 14:
                        ends_across(b + 1)
                    if c == 17:
                        ends_back(b + 1)
                    if c == CB - 1:
                        maxima(b + 1)
                    if c % 2 == 0 and c // 2 < NTG:
                        rows(b + 1, c // 2)
                    if c % 2 == 1 and 0 <= (c - 3) // 2 < NTG:
                        er_of_slots(b + 1, t, (c - 3) // 2)

            def before():
                t = tiles(ET.PE, 0)
                pe.wait_ge(er_split, 2 * PARTS - 1)
                for g in range(NTG + 1):
                    if g < NTG:
                        rows(0, g)
                    if g >= 1:
                        er_of_slots(0, t, g - 1)
                segments(0, 0, 0)
                ends_across(0)
                ends_back(0)
                maxima(0)

            before()
            steps(pe, ET.PE, step)

        @block.scalar
        def _(act):
            def indices(b, u, i):
                act.wait_ge(gathered[u], 16 * CB * i)
                nc.scalar.copy(fl[:, u, :], flags[:, bass.ds(b, 1), :].rearrange("p a e -> p (a e)"))
                nc.scalar.copy(fx[:, u, :], flags_x[:, bass.ds(b, 1), :].rearrange("p a c -> p (a c)")).then_inc(flags_set, 1)
                nc.scalar.copy(idx[:, u, :], src_idx[:, bass.ds(b * CB, CB)]).then_inc(idx_set, 1)

            def transposed_one_hots(b, weight_next):
                for g in range(NTG):
                    weight_next(g)
                    n = min(TG, CB - g * TG)
                    act.wait_ge(rows_made, NTG * b + g + 1)
                    nc.scalar.activation(far[:, g % 2, 0:n, :], rows_ps[g % 2][:, 0:n * P].rearrange("p (c e) -> p c e", e=P),
                                         ACT.Abs, bias=pidx[:, 0:1], scale=-1.0).then_inc(far_made, 1)
                    act.wait_ge(far_made, NTG * b + g + 1)
                    act.wait_ge(er_mm, NTG * b + max(g - 1, 0))
                    nc.scalar.activation(OT[:, g % 2, 0:n, :], far[:, g % 2, 0:n, :], ACT.Relu, bias=1.0, scale=-1.0
                                         ).then_inc(ot_made, 1)

            def weight(b, u, k):
                if k < len(BY_ACT):
                    c = BY_ACT[k]
                    for h in range(H):
                        row = G[:, u, c, h * HW:(h + 1) * HW]
                        a = nc.scalar.activation(row[:, 0:HD], row[:, 0:HD], ACT.Identity, scale=row[:, HD:HW])
                    a.then_inc(weighted_a, 1)

            def exps(b, u):
                act.wait_ge(ref_made, b + 1)
                nc.scalar.activation(alpha[:, :], ref_d[:, :], ACT.Exp, scale=carry_row[:, bass.ds(b, 1)]).then_inc(alpha_made, 1)
                act.wait_ge(zd_made, b + 1)
                nc.scalar.activation(el(u), zd[:, :], ACT.Exp).then_inc(ex_made, 1)

            def step(b, u, i, n_b, has_next):
                un, i_n = (u + 1) % RING, i + (u + 1) // RING
                act.wait_ge(ex_made, b + 1)
                if has_next:
                    transposed_one_hots(b + 1, lambda k: weight(b, u, k))
                    exps(b + 1, un)
                else:
                    for k in range(len(BY_ACT)):
                        weight(b, u, k)

            for u in range(RING):
                indices(u, u, 0)
            transposed_one_hots(0, lambda k: None)
            exps(0, 0)
            def step_and_indices(b, u, i, n_b, has_next):
                if not isinstance(i, int):
                    indices(b + RING, u, i + 1)
                step(b, u, i, n_b, has_next)

            steps(act, ET.Activation, step_and_indices)

        @block.vector
        def _(dve):
            def one_hots(b, u, g):
                n = CB // 3
                nc.vector.tensor_tensor(O[:, u, g * n:(g + 1) * n, :], iota_f[:, :].unsqueeze(1).to_broadcast([P, n, P]),
                                        dst_loc[:, bass.ds(b * CB + g * n, n)].unsqueeze(2).to_broadcast([P, n, P]),
                                        ALU.is_equal).then_inc(o_made, 1)

            def chunk_forward(b, u):
                dve.wait_ge(flags_set, b + 1)
                dve.wait_ge(el_turned, b + 1)
                nc.vector.tensor_tensor_scan(fw[:, :], fl[:, u, 0:P], el_T[0:HC, 0:P], -BIG, ALU.add, ALU.max).then_inc(scan_step, 1)

            def chunk_backward(b, u):
                dve.wait_ge(scan_step, 2 * b + 1)
                nc.vector.tensor_tensor_scan(seg[:, :][:, ::-1], fl[:, u, 1:P + 1][:, ::-1], fw[:, :][:, ::-1], -BIG,
                                             ALU.add, ALU.max).then_inc(scan_step, 1)

            def spread_ends(b):
                dve.wait_ge(scan_step, 2 * b + 2)
                nc.vector.tensor_tensor(spread[:, :, :], pick_c[:, :].unsqueeze(2).to_broadcast([HC, CB, 2]),
                                        seg[:, 0:P:P - 1].unsqueeze(1).to_broadcast([HC, CB, 2]), ALU.mult).then_inc(spread_made, 1)

            def ends_in(b):
                nc.vector.tensor_copy(ends[:, 0:1], ends_m[:, 2 * CB:2 * CB + 1])
                dve.wait_ge(ends_made, b + 1)
                nc.vector.tensor_copy(ends[:, 1:2 * CB + 1], ends_ps).then_inc(ends_step, 1)

            def ends_forward(b, u):
                dve.wait_ge(ends_step, 3 * b + 1)
                nc.vector.tensor_tensor_scan(ends_f[:, :], fx[:, u, 0:2 * CB + 1], ends[:, :], -BIG, ALU.add, ALU.max).then_inc(ends_step, 1)

            def ends_backward(b, u):
                dve.wait_ge(ends_step, 3 * b + 2)
                nc.vector.tensor_tensor_scan(ends_m[:, :][:, ::-1], fx[:, u, 1:2 * CB + 2][:, ::-1], ends_f[:, :][:, ::-1], -BIG,
                                             ALU.add, ALU.max).then_inc(ends_step, 1)

            def moved_maxima(b):
                dve.wait_ge(ends_step, 3 * b + 3)
                nc.vector.tensor_scalar(moved[:, 0, :], ident[0:H, 0:H], ends[:, 0:1], None, ALU.mult)
                nc.vector.tensor_scalar(moved[:, 1, :], ident[0:H, 0:H], ends_m[:, 0:1], None, ALU.mult).then_inc(moved_made, 1)

            def own_ends(b, t0):
                dve.wait_ge(back_made, b + 1)
                nc.vector.tensor_tensor(back[:, :, :], back_ps.rearrange("p (c two) -> p two c", two=2),
                                        pick_c[:, :].unsqueeze(1).to_broadcast([HC, 2, CB]), ALU.mult).then_inc(back_step, 1)
                nc.vector.tensor_tensor(ref[:, :, :], moved_ps.rearrange("p (a h) -> p a h", a=2),
                                        er[:, bass.ds(t0, 1), :].to_broadcast([P, 2, H]), ALU.add).then_inc(ref_step, 1)

            def own_ends_sum(b):
                dve.wait_ge(back_step, 3 * b + 1)
                nc.vector.tensor_reduce(ends_c[:, :], back[:, :, :], AX.X, ALU.add).then_inc(back_step, 1)
                dve.wait_ge(ref_step, 2 * b + 1)
                nc.vector.scalar_tensor_tensor(ref_l[:, :, :], ref[:, :, :], NEG, ref[:, :, :], ALU.mult, ALU.max).then_inc(ref_step, 1)

            def join_forward(b, u):
                dve.wait_ge(back_step, 3 * b + 2)
                nc.vector.tensor_tensor_scan(fw2[:, :], fl[:, u, 0:P], seg[:, :], ends_c[:, 0:1], ALU.add, ALU.max).then_inc(back_step, 1)
                dve.wait_ge(ref_step, 2 * b + 2)
                nc.vector.tensor_tensor(ref_d[:, :], ref_l[:, 0, :], ref_l[:, 1, :], ALU.subtract).then_inc(ref_made, 1)

            def join_backward(b, u):
                dve.wait_ge(back_step, 3 * b + 3)
                nc.vector.tensor_tensor_scan(seg2[:, :][:, ::-1], fl[:, u, 1:P + 1][:, ::-1], fw2[:, :][:, ::-1], ends_c[:, 1:2],
                                             ALU.add, ALU.max).then_inc(seg_made, 1)

            def er_sum(b):
                dve.wait_ge(er_mm, NTG * (b + 1))
                nc.vector.tensor_reduce(er_e[:, :], er_ps.rearrange("p (q k) -> p q k", k=PARTS), AX.X, ALU.add).then_inc(er_made, 1)

            def scores(b, u):
                dve.wait_ge(er_made, b + 1)
                nc.vector.tensor_tensor(z[:, 0, :], el(u), er_e[:, :], ALU.add).then_inc(z_step, 1)
                dve.wait_ge(m_turned, b + 1)
                nc.vector.tensor_tensor(z[:, 1, :], m_ps, er_e[:, :], ALU.add).then_inc(z_step, 1)

            def leaky(b):
                dve.wait_ge(z_step, 3 * b + 2)
                nc.vector.scalar_tensor_tensor(zl[:, :, :], z[:, :, :], NEG, z[:, :, :], ALU.mult, ALU.max).then_inc(z_step, 1)

            def below_maximum(b):
                dve.wait_ge(z_step, 3 * b + 3)
                nc.vector.tensor_tensor(zd[:, :], zl[:, 0, :], zl[:, 1, :], ALU.subtract).then_inc(zd_made, 1)

            def rescale(b, t0):
                dve.wait_ge(alpha_made, b + 1)
                dve.wait_ge(summed, CREDIT + CB * b)
                a = acc[:, bass.ds(t0, 1), :].rearrange("p a (h w) -> p (a h) w", w=HW)
                nc.vector.tensor_tensor(a, a, alpha[:, :].unsqueeze(2).to_broadcast([P, H, HW]), ALU.mult).then_inc(scaled, 1)

            def weight(b, u, c0, c1):
                for c in BY_DVE[c0:c1]:
                    rows = G[:, u, c, :].rearrange("p (h w) -> p h w", w=HW)
                    nc.vector.tensor_tensor(rows[:, :, 0:HD], rows[:, :, 0:HD], rows[:, :, HD:HW].to_broadcast([P, H, HD]),
                                            ALU.mult).then_inc(weighted, 1)

            def add(b, t, c):
                dve.wait_ge(part_made, CB * b + c + 1)
                if c:
                    dve.wait_ge(summed, CREDIT + CB * b + c)
                else:
                    dve.wait_ge(scaled, b + 1)
                a = acc[:, bass.ds(t[c], 1), :].rearrange("p a w -> p (a w)")
                nc.vector.tensor_tensor(a, a, part[c % NPS][:, 0:ROW], ALU.add).then_inc(summed, 1)

            def step(b, u, i, n_b, has_next):
                un = (u + 1) % RING
                t = tiles(ET.DVE, b)
                dve.wait_ge(ex_made, b + 1)
                weight(b, u, 0, 4)
                rescale(b, t[0])
                n = un
                ahead = {
                    1: [lambda: one_hots(b + 1, n, 0)], 3: [lambda: one_hots(b + 1, n, 1)],
                    5: [lambda: one_hots(b + 1, n, 2)],
                    11: [lambda: chunk_forward(b + 1, n)], 12: [lambda: chunk_backward(b + 1, n)],
                    13: [lambda: spread_ends(b + 1)],
                    14: [lambda: ends_in(b + 1), lambda: ends_forward(b + 1, n)],
                    15: [lambda: ends_backward(b + 1, n), lambda: moved_maxima(b + 1)],
                    16: [lambda: own_ends(b + 1, t[CB]), lambda: own_ends_sum(b + 1)],
                    17: [lambda: join_forward(b + 1, n)], 18: [lambda: join_backward(b + 1, n), lambda: er_sum(b + 1)],
                    19: [lambda: scores(b + 1, n)], 20: [lambda: leaky(b + 1), lambda: below_maximum(b + 1)]}
                for c in range(n_b):
                    if has_next:
                        for stage in ahead.get(c, []):
                            stage()
                    add(b, t, c)
                    weight(b, u, c + 4, c + 5)

            def split_er():
                n = 0
                rest = er[:, :, :]
                for k in range(PARTS):
                    nc.vector.tensor_copy(er_p[:, :, :, k], rest).then_inc(er_split, 1)
                    n += 1
                    dve.wait_ge(er_split, n)
                    if k < PARTS - 1:
                        nc.vector.tensor_tensor(er_rest[:, k, :, :], rest, er_p[:, :, :, k], ALU.subtract).then_inc(er_split, 1)
                        n += 1
                        dve.wait_ge(er_split, n)
                        rest = er_rest[:, k, :, :]

            def before():
                split_er()
                nc.vector.memset(acc[:, :, :], 0.0).then_inc(acc_zero, 1)
                nc.vector.memset(ends_m[:, :], -BIG).then_inc(acc_zero, 1)
                for g in range(3):
                    one_hots(0, 0, g)
                dve.wait_ge(acc_zero, 2)
                t0 = nc.values_load_multi_w_load_instructions(
                    tile_i[0:1, 0, 0:1], engines=(ET.DVE,), min_val=0, max_val=NT - 1,
                    skip_runtime_bounds_check_because="as in tiles")[1]
                chunk_forward(0, 0)
                chunk_backward(0, 0)
                spread_ends(0)
                ends_in(0)
                ends_forward(0, 0)
                ends_backward(0, 0)
                moved_maxima(0)
                own_ends(0, t0[0])
                own_ends_sum(0)
                join_forward(0, 0)
                join_backward(0, 0)
                er_sum(0)
                scores(0, 0)
                leaky(0)
                below_maximum(0)
                dve.wait_ge(summed, CREDIT)

            before()
            steps(dve, ET.DVE, step)


def node_reciprocals(acc, rden, step, dve):
    den = acc[:, :, :].rearrange("p t (h w) -> p (t h) w", w=HW)[:, :, HD]
    flat = rden[:, :, :].rearrange("p t h -> p (t h)")
    dve.tensor_scalar(flat, den, DEN_MIN, None, ALU.max).then_inc(step, 1)
    dve.wait_ge(step, 1)
    dve.reciprocal(flat, flat).then_inc(step, 1)
    dve.wait_ge(step, 2)


def next_features(nc, bank, ident, bias, acc, er, wx2, table):
    RN = 4
    ROUNDS = NT // RN
    with ExitStack() as ctx:
        def sb(name, shape, dt=F32):
            return ctx.enter_context(nc.sbuf_tensor(name, shape, dt))

        def sem(name):
            return ctx.enter_context(nc.semaphore(name))

        rden = sb("nf_rden", [P, NT, H])
        hid = sb("nf_hid", [P, RN, D])
        hid_T = sb("nf_hid_T", [P, RN, 2, P])
        feat = sb("nf_feat", [P, RN, RX])
        d_step = sem("nf_d_step")
        h_scaled = sem("nf_h_scaled")
        h_made = sem("nf_h_made")
        turned = sem("nf_turned")
        hT_made = sem("nf_hT_made")
        mm_made = sem("nf_mm_made")
        f_made = sem("nf_f_made")
        f_out = [sem(f"nf_f_out{u}") for u in range(RN)]
        block = ctx.enter_context(nc.Block())

        def rounds(eng, ahead, behind):
            ahead(0, 0, 0)
            for u in range(RN):
                ahead(u + 1, (u + 1) % RN, (u + 1) // RN)
                behind(u, u, 0)
            with eng.Fori(1, ROUNDS) as j:
                for u in range(RN):
                    ahead(RN * j + u + 1, (u + 1) % RN, j + (u + 1) // RN)
                    behind(RN * j + u, u, j)
            behind(NT - 1, 0, ROUNDS)

        assert NT == RN * ROUNDS + 1

        @block.vector
        def _(dve):
            node_reciprocals(acc, rden, d_step, nc.vector)

            def scale(i, u, j):
                if beyond(j, 1):
                    dve.wait_ge(turned, i - RN + 1)
                a = acc[:, bass.ds(i, 1), :].rearrange("p a (h w) -> p (a h) w", w=HW)
                nc.vector.tensor_tensor(hid[:, u, :].rearrange("p (h d) -> p h d", d=HD), a[:, :, 0:HD],
                                        rden[:, bass.ds(i, 1), :].rearrange("p a h -> p (a h)").unsqueeze(2)
                                        .to_broadcast([P, H, HD]), ALU.mult).then_inc(h_scaled, 1)

            def add_bias(i, u, j):
                dve.wait_ge(h_scaled, i + 1)
                nc.vector.tensor_tensor(hid[:, u, :], hid[:, u, :], bias[:, :], ALU.add).then_inc(h_made, 1)

            rounds(dve, scale, add_bias)

        @block.tensor
        def _(pe):
            def turn(i, u, j):
                pe.wait_ge(h_made, i + 1)
                if beyond(i, 2):
                    pe.wait_ge(hT_made, i - 1)
                for k in range(2):
                    tr = nc.tensor.transpose(bank[u % 2][:, k * P:(k + 1) * P], hid[:, u, k * P:(k + 1) * P], ident[:, :])
                tr.then_inc(turned, 1)

            def product(i, u, j):
                pe.wait_ge(hT_made, i + 1)
                if beyond(i, 2):
                    pe.wait_ge(f_made, i - 1)
                for k in range(2):
                    mm = nc.tensor.matmul(bank[2 + u % 2][:, 0:RX], hid_T[:, u, k, :], wx2[:, k, :], start=(k == 0), stop=(k == 1))
                mm.then_inc(mm_made, 1)

            rounds(pe, turn, product)

        @block.scalar
        def _(act):
            def rectify(i, u, j):
                act.wait_ge(turned, i + 1)
                if beyond(j, 1):
                    act.wait_ge(mm_made, i - RN + 1)
                nc.scalar.activation(hid_T[:, u, :, :], bank[u % 2][:, 0:2 * P].rearrange("p (k n) -> p k n", k=2),
                                     ACT.Relu).then_inc(hT_made, 1)

            def copy_out(i, u, j):
                act.wait_ge(mm_made, i + 1)
                if beyond(j, 1):
                    act.wait_ge(f_out[u], 16 * j)
                nc.scalar.copy(er[:, bass.ds(i, 1), :].rearrange("p a h -> p (a h)"), bank[2 + u % 2][:, ROW:RX])
                nc.scalar.copy(feat[:, u, :], bank[2 + u % 2][:, 0:RX]).then_inc(f_made, 1)

            rounds(act, rectify, copy_out)

        @block.sync
        def _(sp):
            def store(i, u):
                sp.wait_ge(f_made, i + 1)
                sp.dma_start(table[bass.ds(i * P, P), :], feat[:, u, 0:ROW]).then_inc(f_out[u], 16)

            with sp.Fori(0, ROUNDS) as j:
                for u in range(RN):
                    store(RN * j + u, u)
            store(NT - 1, 0)
            for u in range(RN):
                sp.wait_ge(f_out[u], 16 * (ROUNDS + (u == 0)))


def finish(nc, x, bias, acc, epst, out):
    GT = 7
    GROUPS = NT // GT
    ROUNDS = GROUPS // 2
    assert NT == GT * GROUPS and GROUPS == 2 * ROUNDS + 1
    with ExitStack() as ctx:
        def sb(name, shape, dt=F32):
            return ctx.enter_context(nc.sbuf_tensor(name, shape, dt))

        def sem(name):
            return ctx.enter_context(nc.semaphore(name))

        xs = sb("fi_x", [P, 2, GT, D])
        rden = sb("fi_rden", [P, NT, H])
        y = sb("fi_y", [P, 2, GT, D])
        res = sb("fi_res", [P, 2, GT, D])
        stats = sb("fi_stats", [P, 2, GT, 6])
        mv = sb("fi_mv", [P, 2, GT, 2])
        sd = sb("fi_sd", [P, 2, GT])
        rs = sb("fi_rs", [P, 2, 2, GT])
        x_in = [sem(f"fi_x_in{p}") for p in range(2)]
        d_step = sem("fi_d_step")
        y_step = sem("fi_y_step")
        x_used = sem("fi_x_used")
        stats_made = sem("fi_stats_made")
        stats_seen = sem("fi_stats_seen")
        mv_made = sem("fi_mv_made")
        sd_made = sem("fi_sd_made")
        rs_step = sem("fi_rs_step")
        rs_made = sem("fi_rs_made")
        r_made = sem("fi_r_made")
        r_out = [sem(f"fi_r_out{p}") for p in range(2)]
        block = ctx.enter_context(nc.Block())
        GP = GT * P

        @block.sync
        def _(sp):
            def load(g, p):
                sp.dma_start(xs[:, p, :, :], x[bass.ds(g * GP, GP), :].rearrange("(t p) d -> p t d", p=P)).then_inc(x_in[p], 16)

            def store(g, p):
                for t in range(GT):
                    sp.wait_ge(r_made, g * GT + t + 1)
                    sp.dma_start(out[bass.ds(g * GP + t * P, P), :], res[:, p, t, :]).then_inc(r_out[p], 16)

            load(0, 0)
            load(1, 1)
            with sp.Fori(0, ROUNDS - 1) as j:
                for p in range(2):
                    sp.wait_ge(x_used, 2 * j + p + 1)
                    load(2 * j + p + 2, p)
                    store(2 * j + p, p)
            sp.wait_ge(x_used, GROUPS - 2)
            sp.dma_start(xs[:, 0, 0:GT - 1, :], x[(GROUPS - 1) * GP:(NT - 1) * P, :].rearrange("(t p) d -> p t d", p=P)
                         ).then_inc(x_in[0], 16)
            sp.dma_start(xs[0:LAST, 0, GT - 1, :], x[(NT - 1) * P:N, :]).then_inc(x_in[0], 16)
            store(GROUPS - 3, 0)
            store(GROUPS - 2, 1)
            for t in range(GT):
                sp.wait_ge(r_made, NT - GT + t + 1)
                n = P if t < GT - 1 else LAST
                r = (NT - GT + t) * P
                sp.dma_start(out[r:r + n, :], res[0:n, 0, t, :]).then_inc(r_out[0], 16)
            sp.wait_ge(r_out[0], 16 * GT * (ROUNDS + 1))
            sp.wait_ge(r_out[1], 16 * GT * ROUNDS)

        @block.vector
        def _(dve):
            node_reciprocals(acc, rden, d_step, nc.vector)

            def scale(g, p, again):
                if again:
                    dve.wait_ge(r_made, GT * (g - 1))
                a = acc[:, bass.ds(g * GT, GT), :].rearrange("p t (h w) -> p (t h) w", w=HW)
                r = rden[:, bass.ds(g * GT, GT), :].rearrange("p t h -> p (t h)")
                nc.vector.tensor_tensor(y[:, p, :, :].rearrange("p t (h d) -> p (t h) d", d=HD), a[:, :, 0:HD],
                                        r.unsqueeze(2).to_broadcast([P, GT * H, HD]), ALU.mult).then_inc(y_step, 1)

            def inverse_deviation(g, p):
                dve.wait_ge(sd_made, g + 1)
                nc.vector.reciprocal(rs[:, p, 0, :], sd[:, p, :]).then_inc(rs_step, 1)

            def mean_shift(g, p):
                dve.wait_ge(rs_step, g + 1)
                nc.vector.scalar_tensor_tensor(rs[:, p, 1, :], mv[:, p, :, 0], -1.0, rs[:, p, 0, :], ALU.mult,
                                               ALU.mult).then_inc(rs_made, 1)

            def residual(g, p, x_rounds, before):
                dve.wait_ge(y_step, 2 * g + 1)
                nc.vector.tensor_tensor(y[:, p, :, :], y[:, p, :, :], bias[:, :].unsqueeze(1).to_broadcast([P, GT, D]),
                                        ALU.add).then_inc(y_step, 1)
                if before:
                    mean_shift(g - 1, 1 - p)
                dve.wait_ge(y_step, 2 * g + 2)
                dve.wait_ge(x_in[p], x_rounds)
                nc.vector.scalar_tensor_tensor(y[:, p, :, :], y[:, p, :, :], 0.0, xs[:, p, :, :], ALU.max,
                                               ALU.add).then_inc(x_used, 1)
                dve.wait_ge(x_used, g + 1)
                for t in range(GT):
                    nc.vector.bn_stats(stats[:, p, t, :], y[:, p, t, :]).then_inc(stats_made, 1)
                for t in range(GT):
                    dve.wait_ge(stats_made, GT * g + t + 1)
                    dve.sem_inc(stats_seen, 1)
                    nc.vector.bn_aggr(mv[:, p, t, :], stats[:, p, t, :]).then_inc(mv_made, 1)

            def group(g, p, j, x_rounds, before, again):
                scale(g, p, again)
                if before:
                    inverse_deviation(g - 1, 1 - p)
                residual(g, p, x_rounds, before)

            group(0, 0, 0, 16, False, False)
            group(1, 1, 0, 16, True, False)
            with dve.Fori(1, ROUNDS) as j:
                group(2 * j, 0, j, 16 * j + 16, True, True)
                group(2 * j + 1, 1, j, 16 * j + 16, True, True)
            group(GROUPS - 1, 0, ROUNDS, 16 * ROUNDS + 32, True, True)
            inverse_deviation(GROUPS - 1, 0)
            mean_shift(GROUPS - 1, 0)

        @block.scalar
        def _(act):
            def deviation(g, p):
                act.wait_ge(mv_made, GT * (g + 1))
                nc.scalar.activation(sd[:, p, :], mv[:, p, :, 1], ACT.Sqrt, bias=epst[:, 0:1]).then_inc(sd_made, 1)

            def norm(g, p, j_out):
                act.wait_ge(rs_made, g + 1)
                if j_out is not None:
                    act.wait_ge(r_out[p], j_out)
                for t in range(GT):
                    nc.scalar.activation(res[:, p, t, :], y[:, p, t, :], ACT.Identity, bias=rs[:, p, 1, t:t + 1],
                                         scale=rs[:, p, 0, t:t + 1]).then_inc(r_made, 1)

            deviation(0, 0)
            norm(0, 0, None)
            deviation(1, 1)
            norm(1, 1, None)
            with act.Fori(1, ROUNDS) as j:
                for p in range(2):
                    deviation(2 * j + p, p)
                    norm(2 * j + p, p, 16 * GT * j)
            deviation(GROUPS - 1, 0)
            norm(GROUPS - 1, 0, 16 * GT * ROUNDS)


def kernel(x, src, dst, node_type_24, L0_gnn_emb, L0_gnn_le_W1, L0_gnn_le_b1, L0_gnn_ln_g, L0_gnn_ln_b, L0_gnn_le_W2,
           L0_gnn_le_b2, L0_gnn_W1, L0_gnn_al1, L0_gnn_ar1, L0_gnn_b1, L0_gnn_W2, L0_gnn_al2, L0_gnn_ar2, L0_gnn_b2):
    import numpy as np
    import concourse.bacc as bacc
    from concourse.bass_utils import run_bass_kernel_spmd

    nc = bacc.Bacc("TRN2", target_bir_lowering=False, num_devices=1)
    arrays = {}

    def given(name, a):
        arrays[name] = np.ascontiguousarray(a)
        return nc.dram_tensor(name, arrays[name].shape, mybir.dt.from_np(arrays[name].dtype), kind="ExternalInput").ap()

    t = np.transpose
    out = nc.dram_tensor("out", (N, D), F32, kind="ExternalOutput").ap()
    gnn_kernel(
        nc, given("x", x), given("xT", t(np.asarray(x))), given("src", src), given("dst", dst), given("labels", node_type_24),
        given("embT", t(np.asarray(L0_gnn_emb))), given("leW1T", t(np.asarray(L0_gnn_le_W1))), given("le_b1", L0_gnn_le_b1),
        given("ln_g", L0_gnn_ln_g), given("ln_b", L0_gnn_ln_b), given("leW2", L0_gnn_le_W2), given("le_b2", L0_gnn_le_b2),
        [given("W1", L0_gnn_W1), given("W2", L0_gnn_W2)],
        [given("W1T", t(np.asarray(L0_gnn_W1))), given("W2T", t(np.asarray(L0_gnn_W2)))],
        [given("al1", L0_gnn_al1), given("al2", L0_gnn_al2)], [given("ar1", L0_gnn_ar1), given("ar2", L0_gnn_ar2)],
        [given("b1", L0_gnn_b1), given("b2", L0_gnn_b2)], out)
    r = run_bass_kernel_spmd(nc, [arrays], core_ids=[0])
    return r.results[0]["out"]
```
